# Optimizing a Trainium2 kernel written in Bass

```python
import numpy as np
import jax
import jax.numpy as jnp

def _softmax(x, axis=-1):
    return jax.nn.softmax(x, axis=axis)

def _gelu(x):
    return jax.nn.gelu(x, approximate=True)

def _silu(x):
    return jax.nn.silu(x)

def _sigmoid(x):
    return jax.nn.sigmoid(x)

def _layernorm(x, axis=-1, eps=1e-05):
    m = jnp.mean(x, axis=axis, keepdims=True)
    v = jnp.var(x, axis=axis, keepdims=True)
    return (x - m) / jnp.sqrt(v + eps)

def _scatter_add(tgt, idx, src, axis=0):
    return tgt.at[idx].add(src)

def _segment_sum(src, seg, n):
    return jax.ops.segment_sum(src, seg, n)
kernel_name = 'mk_recurrent_d4_jaxref_r8_d2b47d'

def setup_inputs(seed: int=0):
    np.random.seed(seed)
    _w = jnp.asarray

    def _L0_attn_setup():
        import jax, jax.numpy as jnp
        import numpy as np
        B, S, D_IN = (4, 256, 128)
        D_Q = D_K = D_V = 128
        key = jax.random.key(seed)
        ks = jax.random.split(key, 6)
        s = lambda d: 1.0 / np.sqrt(d)
        return {'x': jax.random.normal(ks[0], (B, S, D_IN), dtype=jnp.float32), 'Wk': jax.random.normal(ks[1], (D_K, D_IN), dtype=jnp.float32) * s(D_IN), 'Wq': jax.random.normal(ks[2], (D_Q, D_IN), dtype=jnp.float32) * s(D_IN), 'Wv': jax.random.normal(ks[3], (D_V, D_IN), dtype=jnp.float32) * s(D_IN), 'Wa': jax.random.normal(ks[4], (D_Q, D_K), dtype=jnp.float32) * s(D_K), 'Wb': jax.random.normal(ks[5], (D_V, D_V), dtype=jnp.float32) * s(D_V)}
    _L0_attn_in = _L0_attn_setup()

    def _L0_ffn_setup():
        import jax, jax.numpy as jnp
        import numpy as np
        TOP_K = 2
        key = jax.random.key(seed)
        k1, k2, k3 = jax.random.split(key, 3)
        B, S, H, E = (4, 256, 128, 8)
        hidden_states = jax.random.normal(k1, (B, S, H), dtype=jnp.float32)
        Wg = jax.random.normal(k2, (H, E), dtype=jnp.float32) * H ** (-0.5)
        We = jax.random.normal(k3, (E, H, H), dtype=jnp.float32) * H ** (-0.5)
        be = jnp.zeros((E, H), dtype=jnp.float32)
        return {'hidden_states': hidden_states, 'Wg': Wg, 'We': We, 'be': be}
    _L0_ffn_in = _L0_ffn_setup()

    def _L1_attn_setup():
        import jax, jax.numpy as jnp
        import numpy as np
        DIM = 128
        NHEADS = 16
        DIM_HEAD = 64
        DIMD = NHEADS * DIM_HEAD
        key = jax.random.key(seed)
        kx, kq, kk, kv, ko, kb = jax.random.split(key, 6)
        s = DIM ** (-0.5)
        return {'x': jax.random.normal(kx, (4, 256, DIM), dtype=jnp.float32), 'Wq': jax.random.normal(kq, (DIM, DIMD), dtype=jnp.float32) * s, 'Wk': jax.random.normal(kk, (DIM, DIMD), dtype=jnp.float32) * s, 'Wv': jax.random.normal(kv, (DIM, DIMD), dtype=jnp.float32) * s, 'Wo': jax.random.normal(ko, (DIMD, DIM), dtype=jnp.float32) * DIMD ** (-0.5), 'bo': jax.random.normal(kb, (DIM,), dtype=jnp.float32) * 0.01}
    _L1_attn_in = _L1_attn_setup()

    def _L1_ffn_setup():
        import jax, jax.numpy as jnp
        import numpy as np
        B, L, D = (2, 256, 128)
        E = 15
        H = D * 1
        K = 3
        T = 1.0
        key = jax.random.key(seed)
        ks = jax.random.split(key, 12)
        s = 0.02
        return {'x': jax.random.normal(ks[0], (B, L, D), dtype=jnp.float32), 'router_W': jax.random.normal(ks[1], (D, E), dtype=jnp.float32) * s, 'router_b': jnp.zeros((E,), dtype=jnp.float32), 'sW1': jax.random.normal(ks[2], (D, H), dtype=jnp.float32) * s, 'sb1': jnp.zeros((H,), dtype=jnp.float32), 'sW2': jax.random.normal(ks[3], (H, D), dtype=jnp.float32) * s, 'sb2': jnp.zeros((D,), dtype=jnp.float32), 'eW1': jax.random.normal(ks[4], (E, D, H), dtype=jnp.float32) * s, 'eb1': jnp.zeros((E, H), dtype=jnp.float32), 'eW2': jax.random.normal(ks[5], (E, H, D), dtype=jnp.float32) * s, 'eb2': jnp.zeros((E, D), dtype=jnp.float32)}
    _L1_ffn_in = _L1_ffn_setup()

    def _L2_attn_setup():
        import jax, jax.numpy as jnp
        import numpy as np
        EMB = 128
        HEADS = 16
        HEADSIZE = EMB // HEADS
        EPS = 1e-05

        def _layernorm(x, g, b):
            m = jnp.mean(x, axis=-1, keepdims=True)
            v = jnp.mean((x - m) ** 2, axis=-1, keepdims=True)
            return (x - m) * jax.lax.rsqrt(v + EPS) * g + b
        key = jax.random.key(seed)
        ks = jax.random.split(key, 6)
        B, T = (4, 256)
        s = 1.0 / np.sqrt(EMB)
        return {'x': jax.random.normal(ks[0], (B, T, EMB), dtype=jnp.float32), 'Wk': jax.random.normal(ks[1], (EMB, EMB), dtype=jnp.float32) * s, 'Wq': jax.random.normal(ks[2], (EMB, EMB), dtype=jnp.float32) * s, 'Wv': jax.random.normal(ks[3], (EMB, EMB), dtype=jnp.float32) * s, 'Wo': jax.random.normal(ks[4], (EMB, EMB), dtype=jnp.float32) * s, 'bo': jnp.zeros((EMB,), dtype=jnp.float32), 'kln_g': jnp.ones((HEADSIZE,), dtype=jnp.float32), 'kln_b': jnp.zeros((HEADSIZE,), dtype=jnp.float32), 'qln_g': jnp.ones((HEADSIZE,), dtype=jnp.float32), 'qln_b': jnp.zeros((HEADSIZE,), dtype=jnp.float32)}
    _L2_attn_in = _L2_attn_setup()

    def _L2_ffn_setup():
        import jax, jax.numpy as jnp
        import numpy as np
        N_HEADS = 16
        NUM_EXPERTS = 4
        TOP_K = 2
        D_MODEL = 128
        GATE_HID = 128
        key = jax.random.key(seed)
        ks = jax.random.split(key, 12)
        B, T, C, E = (2, 128, D_MODEL, NUM_EXPERTS)
        s = 1.0 / np.sqrt(C)
        return {'hidden_states': jax.random.normal(ks[0], (B, T, C), jnp.float32), 'Wq': jax.random.normal(ks[1], (E, C, C), jnp.float32) * s, 'bq': jnp.zeros((E, C), jnp.float32), 'Wk': jax.random.normal(ks[2], (E, C, C), jnp.float32) * s, 'bk': jnp.zeros((E, C), jnp.float32), 'Wv': jax.random.normal(ks[3], (E, C, C), jnp.float32) * s, 'bv': jnp.zeros((E, C), jnp.float32), 'Wg1': jax.random.normal(ks[4], (C, GATE_HID), jnp.float32) * s, 'bg1': jnp.zeros((GATE_HID,), jnp.float32), 'Wg2': jax.random.normal(ks[5], (GATE_HID, E), jnp.float32) / np.sqrt(GATE_HID), 'bg2': jnp.zeros((E,), jnp.float32), 'Wo': jax.random.normal(ks[6], (C, C), jnp.float32) * s, 'bo': jnp.zeros((C,), jnp.float32)}
    _L2_ffn_in = _L2_ffn_setup()

    def _L3_attn_setup():
        import jax, jax.numpy as jnp
        import numpy as np
        import math
        D_MODEL = 128
        N_HEADS = 16
        D_K = D_MODEL // N_HEADS
        MAX_REL = 32
        key = jax.random.key(seed)
        ks = jax.random.split(key, 8)
        B, S = (8, 128)
        x = jax.random.normal(ks[0], (B, S, D_MODEL), dtype=jnp.float32)
        scale = 1.0 / math.sqrt(D_MODEL)
        Wq = jax.random.normal(ks[1], (D_MODEL, D_MODEL), dtype=jnp.float32) * scale
        Wk = jax.random.normal(ks[2], (D_MODEL, D_MODEL), dtype=jnp.float32) * scale
        Wv = jax.random.normal(ks[3], (D_MODEL, D_MODEL), dtype=jnp.float32) * scale
        Wo = jax.random.normal(ks[4], (D_MODEL, D_MODEL), dtype=jnp.float32) * scale
        b_o = jnp.zeros((D_MODEL,), dtype=jnp.float32)
        rel_k_emb = jax.random.normal(ks[5], (2 * MAX_REL + 1, D_K), dtype=jnp.float32) * 0.02
        rel_v_emb = jax.random.normal(ks[6], (2 * MAX_REL + 1, D_K), dtype=jnp.float32) * 0.02
        return {'x': x, 'Wq': Wq, 'Wk': Wk, 'Wv': Wv, 'Wo': Wo, 'b_o': b_o, 'rel_k_emb': rel_k_emb, 'rel_v_emb': rel_v_emb}
    _L3_attn_in = _L3_attn_setup()

    def _L3_ffn_setup():
        import jax, jax.numpy as jnp
        import numpy as np
        B, T, C, H, E = (1, 32, 128, 256, 8)
        STD = 0.02
        key = jax.random.key(seed)
        ks = jax.random.split(key, 8)
        f32 = jnp.float32
        return {'x': jax.random.normal(ks[0], (B, T, C), f32), 'up': jax.random.normal(ks[1], (E, H, C), f32) * STD, 'gate': jax.random.normal(ks[2], (E, H, C), f32) * STD, 'down': jax.random.normal(ks[3], (E, C, H), f32) * STD, 'router': jax.random.normal(ks[4], (E, C), f32) * STD, 'w_up_s': jax.random.normal(ks[5], (H, C), f32) * STD, 'w_gate_s': jax.random.normal(ks[6], (H, C), f32) * STD, 'w_down_s': jax.random.normal(ks[7], (C, H), f32) * STD}
    _L3_ffn_in = _L3_ffn_setup()
    _d = {'L0_attn_x': _L0_attn_in['x'], 'L0_attn_Wk': _L0_attn_in['Wk'], 'L0_attn_Wq': _L0_attn_in['Wq'], 'L0_attn_Wv': _L0_attn_in['Wv'], 'L0_attn_Wa': _L0_attn_in['Wa'], 'L0_attn_Wb': _L0_attn_in['Wb'], 'L0_ffn_Wg': _L0_ffn_in['Wg'], 'L0_ffn_We': _L0_ffn_in['We'], 'L0_ffn_be': _L0_ffn_in['be'], 'L1_attn_Wq': _L1_attn_in['Wq'], 'L1_attn_Wk': _L1_attn_in['Wk'], 'L1_attn_Wv': _L1_attn_in['Wv'], 'L1_attn_Wo': _L1_attn_in['Wo'], 'L1_attn_bo': _L1_attn_in['bo'], 'L1_ffn_router_W': _L1_ffn_in['router_W'], 'L1_ffn_router_b': _L1_ffn_in['router_b'], 'L1_ffn_sW1': _L1_ffn_in['sW1'], 'L1_ffn_sb1': _L1_ffn_in['sb1'], 'L1_ffn_sW2': _L1_ffn_in['sW2'], 'L1_ffn_sb2': _L1_ffn_in['sb2'], 'L1_ffn_eW1': _L1_ffn_in['eW1'], 'L1_ffn_eb1': _L1_ffn_in['eb1'], 'L1_ffn_eW2': _L1_ffn_in['eW2'], 'L1_ffn_eb2': _L1_ffn_in['eb2'], 'L2_attn_Wk': _L2_attn_in['Wk'], 'L2_attn_Wq': _L2_attn_in['Wq'], 'L2_attn_Wv': _L2_attn_in['Wv'], 'L2_attn_Wo': _L2_attn_in['Wo'], 'L2_attn_bo': _L2_attn_in['bo'], 'L2_attn_kln_g': _L2_attn_in['kln_g'], 'L2_attn_kln_b': _L2_attn_in['kln_b'], 'L2_attn_qln_g': _L2_attn_in['qln_g'], 'L2_attn_qln_b': _L2_attn_in['qln_b'], 'L2_ffn_Wq': _L2_ffn_in['Wq'], 'L2_ffn_bq': _L2_ffn_in['bq'], 'L2_ffn_Wk': _L2_ffn_in['Wk'], 'L2_ffn_bk': _L2_ffn_in['bk'], 'L2_ffn_Wv': _L2_ffn_in['Wv'], 'L2_ffn_bv': _L2_ffn_in['bv'], 'L2_ffn_Wg1': _L2_ffn_in['Wg1'], 'L2_ffn_bg1': _L2_ffn_in['bg1'], 'L2_ffn_Wg2': _L2_ffn_in['Wg2'], 'L2_ffn_bg2': _L2_ffn_in['bg2'], 'L2_ffn_Wo': _L2_ffn_in['Wo'], 'L2_ffn_bo': _L2_ffn_in['bo'], 'L3_attn_Wq': _L3_attn_in['Wq'], 'L3_attn_Wk': _L3_attn_in['Wk'], 'L3_attn_Wv': _L3_attn_in['Wv'], 'L3_attn_Wo': _L3_attn_in['Wo'], 'L3_attn_b_o': _L3_attn_in['b_o'], 'L3_attn_rel_k_emb': _L3_attn_in['rel_k_emb'], 'L3_attn_rel_v_emb': _L3_attn_in['rel_v_emb'], 'L3_ffn_up': _L3_ffn_in['up'], 'L3_ffn_gate': _L3_ffn_in['gate'], 'L3_ffn_down': _L3_ffn_in['down'], 'L3_ffn_router': _L3_ffn_in['router'], 'L3_ffn_w_up_s': _L3_ffn_in['w_up_s'], 'L3_ffn_w_gate_s': _L3_ffn_in['w_gate_s'], 'L3_ffn_w_down_s': _L3_ffn_in['w_down_s']}
    _x0 = _d['L0_attn_x']
    _d['L0_attn_x'] = jax.random.normal(jax.random.fold_in(jax.random.key(seed), 1), (4, 512, 128), dtype=_x0.dtype)
    del _x0
    return _d

def reference(L0_attn_x, L0_attn_Wk, L0_attn_Wq, L0_attn_Wv, L0_attn_Wa, L0_attn_Wb, L0_ffn_Wg, L0_ffn_We, L0_ffn_be, L1_attn_Wq, L1_attn_Wk, L1_attn_Wv, L1_attn_Wo, L1_attn_bo, L1_ffn_router_W, L1_ffn_router_b, L1_ffn_sW1, L1_ffn_sb1, L1_ffn_sW2, L1_ffn_sb2, L1_ffn_eW1, L1_ffn_eb1, L1_ffn_eW2, L1_ffn_eb2, L2_attn_Wk, L2_attn_Wq, L2_attn_Wv, L2_attn_Wo, L2_attn_bo, L2_attn_kln_g, L2_attn_kln_b, L2_attn_qln_g, L2_attn_qln_b, L2_ffn_Wq, L2_ffn_bq, L2_ffn_Wk, L2_ffn_bk, L2_ffn_Wv, L2_ffn_bv, L2_ffn_Wg1, L2_ffn_bg1, L2_ffn_Wg2, L2_ffn_bg2, L2_ffn_Wo, L2_ffn_bo, L3_attn_Wq, L3_attn_Wk, L3_attn_Wv, L3_attn_Wo, L3_attn_b_o, L3_attn_rel_k_emb, L3_attn_rel_v_emb, L3_ffn_up, L3_ffn_gate, L3_ffn_down, L3_ffn_router, L3_ffn_w_up_s, L3_ffn_w_gate_s, L3_ffn_w_down_s):

    def _L0_attn_ref(x, Wk, Wq, Wv, Wa, Wb):
        import jax, jax.numpy as jnp
        import numpy as np
        B, S, D_IN = (4, 256, 128)
        D_Q = D_K = D_V = 128
        k = jnp.einsum('bsd,kd->bsk', x, Wk)
        q = jnp.einsum('bsd,qd->bsq', x, Wq)
        v = jnp.einsum('bsd,vd->bsv', x, Wv)
        ak = jnp.einsum('bsk,qk->bsq', k, Wa)
        e = jnp.einsum('biq,bjq->bij', q, ak)
        alpha = jax.nn.softmax(e, axis=-1)
        u = jnp.einsum('bsv,wv->bsw', v, Wb)
        out = jnp.einsum('bij,bjv->biv', alpha, u)
        return out

    def _L0_ffn_ref(hidden_states, Wg, We, be):
        import jax, jax.numpy as jnp
        import numpy as np
        TOP_K = 2
        B, S, H = hidden_states.shape
        T = B * S
        x = hidden_states.reshape(T, H)
        probs = jax.nn.softmax(x @ Wg, axis=-1)
        top_vals, top_idx = jax.lax.top_k(probs, TOP_K)
        gates = top_vals / jnp.sum(top_vals, axis=-1, keepdims=True)
        expert_out = jnp.einsum('th,ehd->etd', x, We) + be[:, None, :]
        tok = jnp.arange(T)[:, None]
        sel = expert_out[top_idx, tok, :]
        out = jnp.sum(gates[..., None] * sel, axis=1)
        return out.reshape(B, S, H)

    def _L1_attn_ref(x, Wq, Wk, Wv, Wo, bo):
        import jax, jax.numpy as jnp
        import numpy as np
        DIM = 128
        NHEADS = 16
        DIM_HEAD = 64
        DIMD = NHEADS * DIM_HEAD
        bs, n, d = x.shape
        scale = DIM_HEAD ** (-0.5)

        def split_heads(t):
            return t.reshape(bs, n, NHEADS, DIM_HEAD).transpose(0, 2, 1, 3)
        q = split_heads(x @ Wq) * scale
        k = split_heads(x @ Wk)
        v = split_heads(x @ Wv)
        scores = jnp.einsum('bhqd,bhkd->bhqk', q, k)
        weights = jax.nn.softmax(scores, axis=-1)
        context = jnp.einsum('bhqk,bhkd->bhqd', weights, v)
        context = context.transpose(0, 2, 1, 3).reshape(bs, n, DIMD)
        return context @ Wo + bo

    def _L1_ffn_ref(x, router_W, router_b, sW1, sb1, sW2, sb2, eW1, eb1, eW2, eb2):
        import jax, jax.numpy as jnp
        import numpy as np
        B, L, D = (2, 256, 128)
        E = 15
        H = D * 1
        K = 3
        T = 1.0
        b, l, d = x.shape
        n = b * l
        xt = x.reshape(n, d)
        shared = jax.nn.relu(xt @ sW1 + sb1) @ sW2 + sb2
        logits = xt @ router_W + router_b
        probs = jax.nn.softmax(logits / T, axis=-1)
        top_p, top_i = jax.lax.top_k(probs, K)
        cw = jnp.zeros((n, E), dtype=probs.dtype)
        cw = cw.at[jnp.arange(n)[:, None], top_i].set(top_p)
        h = jax.nn.relu(jnp.einsum('nd,edh->neh', xt, eW1) + eb1)
        ye = jnp.einsum('neh,ehd->ned', h, eW2) + eb2
        routed = jnp.einsum('ned,ne->nd', ye, cw)
        return (shared + routed).reshape(b, l, d)

    def _L2_attn_ref(x, Wk, Wq, Wv, Wo, bo, kln_g, kln_b, qln_g, qln_b):
        import jax, jax.numpy as jnp
        import numpy as np
        EMB = 128
        HEADS = 16
        HEADSIZE = EMB // HEADS
        EPS = 1e-05

        def _layernorm(x, g, b):
            m = jnp.mean(x, axis=-1, keepdims=True)
            v = jnp.mean((x - m) ** 2, axis=-1, keepdims=True)
            return (x - m) * jax.lax.rsqrt(v + EPS) * g + b
        B, T, E = x.shape
        k = jnp.einsum('bte,fe->btf', x, Wk).reshape(B, T, HEADS, HEADSIZE)
        q = jnp.einsum('bte,fe->btf', x, Wq).reshape(B, T, HEADS, HEADSIZE)
        v = jnp.einsum('bte,fe->btf', x, Wv).reshape(B, T, HEADS, HEADSIZE)
        k = _layernorm(k, kln_g, kln_b)
        q = _layernorm(q, qln_g, qln_b)
        scale = E ** (-0.25)
        q = q * scale
        k = k * scale
        dot = jnp.einsum('bihd,bjhd->bhij', q, k)
        causal = jnp.triu(jnp.ones((T, T), dtype=bool), k=1)
        dot = jnp.where(causal, -jnp.inf, dot)
        att = jax.nn.softmax(dot, axis=-1)
        out = jnp.einsum('bhij,bjhd->bihd', att, v).reshape(B, T, E)
        return jnp.einsum('bte,fe->btf', out, Wo) + bo

    def _L2_ffn_ref(hidden_states, Wq, bq, Wk, bk, Wv, bv, Wg1, bg1, Wg2, bg2, Wo, bo):
        import jax, jax.numpy as jnp
        import numpy as np
        N_HEADS = 16
        NUM_EXPERTS = 4
        TOP_K = 2
        D_MODEL = 128
        GATE_HID = 128
        B, T, C = hidden_states.shape
        H = N_HEADS
        D = C // H
        pooled = hidden_states.mean(axis=1)
        logits = jax.nn.relu(pooled @ Wg1 + bg1) @ Wg2 + bg2
        vals, idx = jax.lax.top_k(logits, TOP_K)
        sm = jax.nn.softmax(vals, axis=-1)
        weights = jnp.zeros_like(logits).at[jnp.arange(B)[:, None], idx].set(sm)

        def moe_proj(W, b):
            Wc = jnp.einsum('be,ecd->bcd', weights, W)
            bc = weights @ b
            return jnp.einsum('btc,bcd->btd', hidden_states, Wc) + bc[:, None, :]
        q = moe_proj(Wq, bq).reshape(B, T, H, D)
        k = moe_proj(Wk, bk).reshape(B, T, H, D)
        v = moe_proj(Wv, bv).reshape(B, T, H, D)
        scores = jnp.einsum('bthd,bshd->bhts', q, k) / np.sqrt(D).astype(np.float32)
        attn = jax.nn.softmax(scores, axis=-1)
        out = jnp.einsum('bhts,bshd->bthd', attn, v).reshape(B, T, C)
        return out @ Wo + bo

    def _L3_attn_ref(x, Wq, Wk, Wv, Wo, b_o, rel_k_emb, rel_v_emb):
        import jax, jax.numpy as jnp
        import numpy as np
        import math
        D_MODEL = 128
        N_HEADS = 16
        D_K = D_MODEL // N_HEADS
        MAX_REL = 32
        B, S, D = x.shape
        H, dk = (N_HEADS, D_K)
        inv_sqrt_dk = 1.0 / math.sqrt(dk)
        Q = (x @ Wq.T).reshape(B, S, H, dk)
        K = (x @ Wk.T).reshape(B, S, H, dk)
        V = (x @ Wv.T).reshape(B, S, H, dk)
        pos = jnp.arange(S)
        rel_idx = jnp.clip(pos[None, :] - pos[:, None], -MAX_REL, MAX_REL) + MAX_REL
        rel_k = rel_k_emb[rel_idx]
        rel_v = rel_v_emb[rel_idx]
        scores = jnp.einsum('bihd,bjhd->bhij', Q, K) * inv_sqrt_dk
        scores = scores + jnp.einsum('bihd,ijd->bhij', Q, rel_k) * inv_sqrt_dk
        attn = jax.nn.softmax(scores, axis=-1)
        ctx = jnp.einsum('bhij,bjhd->bihd', attn, V)
        ctx = ctx + jnp.einsum('bhij,ijd->bihd', attn, rel_v)
        ctx = ctx.reshape(B, S, D)
        out = ctx @ Wo.T + b_o
        return out

    def _L3_ffn_ref(x, up, gate, down, router, w_up_s, w_gate_s, w_down_s):
        import jax, jax.numpy as jnp
        import numpy as np
        B, T, C, H, E = (1, 32, 128, 256, 8)
        STD = 0.02
        b, t, c = x.shape
        x_ = x.reshape(b * t, c)
        logits = x_ @ router.T
        idx = jnp.argmax(logits, axis=-1)
        onehot = jax.nn.one_hot(idx, router.shape[0], dtype=x.dtype)
        u = jnp.einsum('bc,ehc->ebh', x_, up)
        g = jnp.einsum('bc,ehc->ebh', x_, gate)
        h = jax.nn.silu(g) * u
        ye = jnp.einsum('ebh,ech->ebc', h, down)
        y = jnp.einsum('ebc,be->bc', ye, onehot)
        ys = jax.nn.silu(x_ @ w_gate_s.T) * (x_ @ w_up_s.T) @ w_down_s.T
        return (y + ys).reshape(b, t, c)
    x = L0_attn_x
    xn = _layernorm(x, axis=-1)
    s = _L0_attn_ref(xn, L0_attn_Wk, L0_attn_Wq, L0_attn_Wv, L0_attn_Wa, L0_attn_Wb)
    g = _silu(_L0_ffn_ref(xn, L0_ffn_Wg, L0_ffn_We, L0_ffn_be))
    x = x + s * g
    xn = _layernorm(x, axis=-1)
    s = _L1_attn_ref(xn, L1_attn_Wq, L1_attn_Wk, L1_attn_Wv, L1_attn_Wo, L1_attn_bo)
    g = _silu(_L1_ffn_ref(xn, L1_ffn_router_W, L1_ffn_router_b, L1_ffn_sW1, L1_ffn_sb1, L1_ffn_sW2, L1_ffn_sb2, L1_ffn_eW1, L1_ffn_eb1, L1_ffn_eW2, L1_ffn_eb2))
    x = x + s * g
    xn = _layernorm(x, axis=-1)
    s = _L2_attn_ref(xn, L2_attn_Wk, L2_attn_Wq, L2_attn_Wv, L2_attn_Wo, L2_attn_bo, L2_attn_kln_g, L2_attn_kln_b, L2_attn_qln_g, L2_attn_qln_b)
    g = _silu(_L2_ffn_ref(xn, L2_ffn_Wq, L2_ffn_bq, L2_ffn_Wk, L2_ffn_bk, L2_ffn_Wv, L2_ffn_bv, L2_ffn_Wg1, L2_ffn_bg1, L2_ffn_Wg2, L2_ffn_bg2, L2_ffn_Wo, L2_ffn_bo))
    x = x + s * g
    xn = _layernorm(x, axis=-1)
    s = _L3_attn_ref(xn, L3_attn_Wq, L3_attn_Wk, L3_attn_Wv, L3_attn_Wo, L3_attn_b_o, L3_attn_rel_k_emb, L3_attn_rel_v_emb)
    g = _silu(_L3_ffn_ref(xn, L3_ffn_up, L3_ffn_gate, L3_ffn_down, L3_ffn_router, L3_ffn_w_up_s, L3_ffn_w_gate_s, L3_ffn_w_down_s))
    x = x + s * g
    return x

_drawn_inputs = setup_inputs


def setup_inputs(seed=0):
    import zlib

    import numpy as np

    out = dict(_drawn_inputs(seed))
    spreads = {'L0_ffn_be': (0.0, 0.1),
     'L1_ffn_router_b': (0.0, 0.8),
     'L1_ffn_sb1': (0.0, 0.8),
     'L1_ffn_sb2': (0.0, 0.8),
     'L1_ffn_eb1': (0.0, 0.8),
     'L1_ffn_eb2': (0.0, 0.8),
     'L2_attn_bo': (0.0, 0.8),
     'L2_attn_kln_g': (1.0, 0.6),
     'L2_attn_kln_b': (0.0, 2.0),
     'L2_attn_qln_g': (1.0, 0.6),
     'L2_attn_qln_b': (0.0, 0.8),
     'L2_ffn_bq': (0.0, 0.8),
     'L2_ffn_bk': (0.0, 2.0),
     'L2_ffn_bv': (0.0, 0.8),
     'L2_ffn_bg1': (0.0, 0.8),
     'L2_ffn_bg2': (0.0, 0.8),
     'L2_ffn_bo': (0.0, 0.8),
     'L3_attn_b_o': (0.0, 2.0)}
    factors = {'L1_attn_Wq': 8.0,
     'L1_attn_Wk': 8.0,
     'L1_attn_Wv': 8.0,
     'L1_attn_Wo': 8.0,
     'L1_attn_bo': 8.0,
     'L1_ffn_router_W': 8.0,
     'L1_ffn_sW1': 8.0,
     'L1_ffn_sW2': 8.0,
     'L1_ffn_eW1': 8.0,
     'L1_ffn_eW2': 8.0,
     'L2_attn_Wk': 8.0,
     'L2_attn_Wq': 8.0,
     'L2_attn_Wv': 8.0,
     'L2_attn_Wo': 8.0,
     'L2_ffn_Wq': 8.0,
     'L2_ffn_Wk': 8.0,
     'L2_ffn_Wv': 8.0,
     'L2_ffn_Wg1': 8.0,
     'L2_ffn_Wg2': 8.0,
     'L2_ffn_Wo': 8.0,
     'L3_attn_Wq': 8.0,
     'L3_attn_Wk': 8.0,
     'L3_attn_Wv': 8.0,
     'L3_attn_Wo': 8.0,
     'L3_attn_rel_k_emb': 8.0,
     'L3_attn_rel_v_emb': 31.622,
     'L3_ffn_up': 8.0,
     'L3_ffn_gate': 8.0,
     'L3_ffn_down': 8.0,
     'L3_ffn_router': 8.0,
     'L3_ffn_w_up_s': 8.0,
     'L3_ffn_w_gate_s': 8.0,
     'L3_ffn_w_down_s': 8.0}
    for name, (base, spread) in spreads.items():
        noise = np.random.default_rng([zlib.crc32(name.encode()), seed]).standard_normal(out[name].shape)
        drawn = base * np.exp(spread * noise) if base else spread * noise
        out[name] = jnp.asarray(drawn.astype(out[name].dtype))
    for name, factor in factors.items():
        out[name] = (out[name] * factor).astype(out[name].dtype)
    return out
```

```python
import concourse.bass as bass
from concourse import mybir
from contextlib import ExitStack
import numpy as np

B, S, D = 4, 512, 128
NTT = S // 128
EPS = 1e-5
L1_HEADS, L1_DH = 16, 64
HEADS, DH = 16, 8
L1_EXPERTS = 16
L0_EXPERTS = 8
L3_EXPERTS, L3_HID = 9, 256
MAX_REL = 32
BAND = 127
WIN = 96
A_ROW = 224
GROW = 32
NPARTS = 3
STACK = NPARTS * NPARTS * DH
NEG = -1e30


class Steps:

    def __init__(self, eng, sem):
        self.eng, self.sem, self.n = eng, sem, 0

    def add(self, ins):
        ins.then_inc(self.sem, 1)
        self.n += 1

    def settle(self):
        self.eng.wait_ge(self.sem, self.n)


class Jobs:

    def __init__(self, banks, filled, emptied, jobs):
        self.banks, self.filled, self.emptied = banks, filled, emptied
        self.names = [n for n, _ in jobs]
        self.engines = [e for _, e in jobs]

    def bank(self, name):
        return self.banks[self.names.index(name) % len(self.banks)]

    def n_filled(self, name):
        return self.names.index(name) + 1

    def n_emptied(self, j):
        return self.emptied[self.engines[j]], self.engines[:j + 1].count(self.engines[j])

    def wait_free(self, pe, name):
        j = self.names.index(name) - len(self.banks)
        if j >= 0:
            pe.wait_ge(*self.n_emptied(j))

    def wait_filled(self, eng, name):
        eng.wait_ge(self.filled, self.n_filled(name))

    def wait_emptied(self, eng, name):
        eng.wait_ge(*self.n_emptied(self.names.index(name)))

    def wait_all_free(self, pe):
        for e in sorted(set(self.engines)):
            pe.wait_ge(self.emptied[e], self.engines.count(e))


def build(nc, T, out):
    f32, bf16 = mybir.dt.float32, mybir.dt.bfloat16
    ALU, ACT, AX = mybir.AluOpType, mybir.ActivationFunctionType, mybir.AxisListType

    ctx = ExitStack()
    with ctx:
        def sb(name, shape, dt=f32):
            return ctx.enter_context(nc.sbuf_tensor(name, shape, dt))

        wa = sb("wa", [128, 5632])
        wb = sb("wb", [128, 10624])
        x_all = sb("x_all", [128, B, NTT, D])
        ident = sb("ident", [128, 128])
        ident_b = sb("ident_b", [128, 128], bf16)
        ones_row = sb("ones_row", [1, 128])
        causal_f = sb("causal_f", [128, 128])
        causal_b = sb("causal_b", [128, 128], bf16)
        tri = sb("tri", [128, 15, 15])
        arena = sb("arena", [128, 32768], bf16)
        arena_f = arena[:, :].bitcast(f32)
        pt = sb("pt", [128, 4, NTT, S])
        pt_f = pt[:, :, :, :].rearrange("p a b c -> p (a b c)")
        prob = sb("prob", [128, 3, S])
        prob_f = prob[:, :, :].rearrange("p a b -> p (a b)")
        xn = sb("xn", [128, NTT, D])
        xnT = sb("xnT", [128, S])
        acc = sb("acc", [128, NTT, D])
        acc_f = acc[:, :, :].rearrange("p t d -> p (t d)")
        tmp = sb("tmp", [128, 2, NTT, D])
        ctx_raw = sb("ctx_raw", [128, S])
        ctx_n = sb("ctx_n", [128, 2, S])
        v_pad = sb("v_pad", [128, NTT, HEADS, GROW])
        negmax = sb("negmax", [128, 64])
        rowsum = sb("rowsum", [128, 64])
        ln_st = sb("ln_st", [128, NTT, 6])
        ln_mv = sb("ln_mv", [128, NTT, 2])
        ln_rs = sb("ln_rs", [128, NTT])
        minus_half = sb("minus_half", [128, 1])
        lg = sb("lg", [128, NTT, 16])
        ex = sb("ex", [128, NTT, 16])
        gate = sb("gate", [128, NTT, 16])
        rank = sb("rank", [128, NTT, 16])
        red = sb("red", [128, NTT])
        small = sb("small", [128, 64])

        def ps(name):
            return ctx.enter_context(nc.psum_tensor(name, [128, 512], f32))

        bank_s = [ps(f"bank_s{i}") for i in range(3)]
        bank_t = [ps(f"bank_t{i}") for i in range(2)]
        bank_v = ps("bank_v")
        bank_m = [ps(f"bank_m{i}") for i in range(2)]
        bank_o = bank_m[1]
        score_banks = bank_s + bank_m[0:1]

        kept = {}
        for n in ("loaded", "w0", "w1", "w2", "w3", "consts", "stored", "go0", "go1", "go2", "go3",
                  "causal_set", "q1_zeroed", "stack_zeroed", "keys_zeroed", "v_set", "zeroed", "half_set", "v3_set"):
            kept[n] = ctx.enter_context(nc.semaphore(n))
        s_esent = [ctx.enter_context(nc.semaphore(f"s_esent{i}")) for i in range(2)]
        s_askew = [ctx.enter_context(nc.semaphore(f"s_askew{i}")) for i in range(2)]
        SENT, SKEWED = 16 * 4 * NTT // 2, 16 * HEADS // 2
        cleared = {}

        def sem(name):
            cleared[name] = ctx.enter_context(nc.semaphore(name))
            return cleared[name]

        fin, s_resumed = sem("fin"), sem("s_resumed")
        s_dve, s_act, s_pool = sem("s_dve"), sem("s_act"), sem("s_pool")
        s_var, s_rstd, s_xn = sem("s_var"), sem("s_rstd"), sem("s_xn")
        a_fill, a_act, a_dve = sem("a_fill"), sem("a_act"), sem("a_dve")
        f_fill, f_act, f_dve = sem("f_fill"), sem("f_act"), sem("f_dve")
        r_fill, r_dve = sem("r_fill"), sem("r_dve")
        r2_fill, r2_dve = sem("r2_fill"), sem("r2_dve")
        s_gate, s_lgsub, s_exp, s_acc, s_silu, s_e1 = (sem(n) for n in
                                                      ("s_gate", "s_lgsub", "s_exp", "s_acc", "s_silu", "s_e1"))
        att = {}
        for i in range(2):
            att[i] = {n: sem(f"{n}_{i}") for n in ("scored", "maxed", "exped", "turned", "ev_dve", "ev_act",
                                                   "pv", "craw", "inverted", "projected")}
        s_final = sem("s_final")
        s_round, s_rest, s_sent, s_pooled, s_mixed, s_normed, s_hvar, s_hrstd, s_again, s_taken = (sem(n) for n in (
            "s_round", "s_rest", "s_sent", "s_pooled", "s_mixed", "s_normed", "s_hvar", "s_hrstd", "s_again", "s_taken"))
        (s_qkept, s_offsets, s_tanh, s_aturned, s_amasked, s_band, s_bmasked, s_numer, s_normal, r_act) = (
            sem(n) for n in ("s_qkept", "s_offsets", "s_tanh", "s_aturned", "s_amasked", "s_band", "s_bmasked",
                             "s_numer", "s_normal", "r_act"))
        s_near = [sem(f"s_near{i}") for i in range(2)]
        s_written = [sem(f"s_written{i}") for i in range(3)]
        s_stacked = [sem(f"s_stacked{i}") for i in range(2)]
        nums = [s.num for s in cleared.values()]
        assert nums == list(range(nums[0], nums[0] + len(nums)))
        clear_range = range(nums[0], nums[-1] + 1)

        block = ctx.enter_context(nc.Block())

        def iterations(eng, go):
            return eng.Fori(0, B)

        def meet(eng, go, b):
            eng.drain().then_inc(fin, 1)
            eng.wait_ge(go, b + 1)

        def meet_sync(sp, go, b):
            meet(sp, go, b)
            sp.sem_inc(s_resumed, 1)
            sp.wait_ge(s_resumed, 1)

        def meet_and_clear(pool, go, b, others=4):
            pool.drain()
            pool.wait_ge(fin, others)
            pool.sem_clear(clear_range)
            pool.drain().then_inc(go, 1)
            pool.wait_ge(go, b + 1)

        def x_of(b):
            return x_all[:, bass.ds(b, 1), :, :].rearrange("p b t d -> p (b t) d")

        def flat(t3):
            return t3.rearrange("p t d -> p (t d)")

        def bank3(bank):
            return bank[:, :].rearrange("p (t d) -> p t d", t=NTT)

        def layer_norm(dve, b, d):
            x = x_of(b)
            for t in range(NTT):
                d.add(dve.bn_stats(ln_st[:, t, :], x[:, t, :]))
            d.settle()
            for t in range(NTT):
                dve.bn_aggr(ln_mv[:, t, :], ln_st[:, t, :]).then_inc(s_var, 1)
            dve.wait_ge(s_var, NTT)
            dve.wait_ge(s_rstd, 1)
            for t in range(NTT):
                dve.tensor_scalar(xn[:, t, :], x[:, t, :], ln_mv[:, t, 0:1], ln_rs[:, t:t + 1],
                                  ALU.subtract, ALU.mult).then_inc(s_xn, 1)

        def inverse_deviation(pool):
            pool.wait_ge(s_var, NTT)
            pool.tensor_scalar(ln_rs[:, :], ln_mv[:, :, 1], EPS, None, ALU.add).then_inc(s_pool, 1)
            pool.wait_ge(s_pool, 1)
            pool.tensor_tensor(ln_rs[:, :], ln_rs[:, :], minus_half[:, 0:1].to_broadcast([128, NTT]), ALU.pow
                               ).then_inc(s_rstd, 1)

        def turn_xn(pe, A):
            for t in range(NTT):
                pe.wait_ge(s_xn, t + 1)
                last = pe.transpose(A.bank("X")[:, t * 128:(t + 1) * 128], xn[:, t, :], ident[:, :])
            last.then_inc(A.filled, 1)

        def evac(eng, A, name, dst, src=None, scale=None):
            A.wait_filled(eng, name)
            src = A.bank(name)[:, :] if src is None else src
            if eng is nc.scalar or A.engines[A.names.index(name)] == "act":
                ins = nc.scalar.activation(dst, src, ACT.Copy, scale=1.0 if scale is None else scale)
            elif scale is None:
                ins = nc.vector.tensor_copy(dst, src)
            else:
                ins = nc.vector.tensor_scalar(dst, src, scale, None, ALU.mult)
            ins.then_inc(A.emptied[A.engines[A.names.index(name)]], 1)

        def project(pe, A, name, w, rhs, n=S):
            A.wait_free(pe, name)
            pe.matmul(A.bank(name)[:, 0:n], w, rhs, start=True, stop=True).then_inc(A.filled, 1)

        def token_products(pe, A, name, rhs, width, lhs=None, bias=None):
            A.wait_free(pe, name)
            lhs = xnT if lhs is None else lhs
            for t in range(NTT):
                o = A.bank(name)[:, t * width:(t + 1) * width]
                last = pe.matmul(o, lhs[:, t * 128:(t + 1) * 128], rhs, start=True, stop=bias is None)
                if bias is not None:
                    last = pe.matmul(o, ones_row[0:1, :], bias, start=False, stop=True)
            last.then_inc(A.filled, 1)

        def top_k(dve, d, logits, T_, E, k, mask, cmp_a, cmp_b):
            mine = logits.unsqueeze(3).to_broadcast([128, T_, E, E])
            other = logits.unsqueeze(2).to_broadcast([128, T_, E, E])
            ca = cmp_a.rearrange("p (t e f) -> p t e f", t=T_, e=E)
            cb = cmp_b.rearrange("p (t e f) -> p t e f", t=T_, e=E)
            d.add(dve.tensor_tensor(ca, other, mine, ALU.is_gt))
            d.add(dve.tensor_tensor(cb, other, mine, ALU.is_ge))
            d.settle()
            for t in range(T_):
                d.add(dve.tensor_tensor(cb[:, t], cb[:, t], tri[:, 0:E, 0:E], ALU.mult))
            d.settle()
            d.add(dve.tensor_tensor(ca, ca, cb, ALU.max))
            d.settle()
            d.add(dve.tensor_reduce(rank[:, 0:T_, 0:E], ca, AX.X, ALU.add))
            d.settle()
            d.add(dve.tensor_scalar(mask, rank[:, 0:T_, 0:E], float(k) - 0.5, None, ALU.is_lt))

        def shifted(dve, d, logits, T_, E):
            d.add(dve.tensor_reduce(red[:, 0:T_], logits, AX.X, ALU.max))
            d.settle()
            dve.tensor_tensor(ex[:, 0:T_, 0:E], logits, red[:, 0:T_].unsqueeze(2).to_broadcast([128, T_, E]),
                              ALU.subtract).then_inc(s_lgsub, 1)

        def exp_logits(act, T_, E):
            act.wait_ge(s_lgsub, 1)
            act.activation(ex[:, 0:T_, 0:E], ex[:, 0:T_, 0:E], ACT.Exp).then_inc(s_exp, 1)

        def gates(dve, d, T_, E, of_all):
            d.settle()
            dve.wait_ge(s_exp, 1)
            d.add(dve.tensor_tensor(gate[:, 0:T_, 0:E], ex[:, 0:T_, 0:E], gate[:, 0:T_, 0:E], ALU.mult))
            d.settle()
            d.add(dve.tensor_reduce(red[:, 0:T_], (ex if of_all else gate)[:, 0:T_, 0:E], AX.X, ALU.add))
            d.settle()
            d.add(dve.reciprocal(red[:, 0:T_], red[:, 0:T_]))
            d.settle()
            dve.tensor_tensor(gate[:, 0:T_, 0:E], gate[:, 0:T_, 0:E],
                              red[:, 0:T_].unsqueeze(2).to_broadcast([128, T_, E]), ALU.mult).then_inc(s_gate, 1)

        def gated(dve, F, e, first=0):
            F.wait_filled(dve, f"Y{e}")
            if e - 1 - first > 0:
                dve.wait_ge(s_acc, e - 1 - first)
            dst = acc[:, :, :] if e < first else tmp[:, e % 2]
            dve.tensor_tensor(dst, bank3(F.bank(f"Y{e}")), gate[:, :, e:e + 1].to_broadcast([128, NTT, D]),
                              ALU.mult).then_inc(F.emptied["dve"], 1)

        def add_up(pool, F, es, base):
            for i, e in enumerate(es):
                F.wait_emptied(pool, f"Y{e}")
                if i:
                    pool.wait_ge(s_acc, i)
                elif base is not None:
                    F.wait_emptied(pool, base)
                pool.tensor_tensor(acc[:, :, :], acc[:, :, :], tmp[:, e % 2], ALU.add).then_inc(s_acc, 1)

        def silu_tanh(act, n):
            act.wait_ge(s_acc, n)
            act.activation(flat(tmp[:, 0]), acc_f, ACT.Tanh, scale=0.5).then_inc(s_e1, 1)

        def silu(dve, d):
            dve.wait_ge(s_e1, 1)
            dve.scalar_tensor_tensor(acc_f, flat(tmp[:, 0]), 1.0, acc_f, ALU.add, ALU.mult).then_inc(s_silu, 1)
            dve.wait_ge(s_silu, 1)

        def residual(dve, d, b, src):
            d.add(dve.scalar_tensor_tensor(tmp[:, 1], src, 0.5, acc[:, :, :], ALU.mult, ALU.mult))
            d.settle()
            x = x_of(b)
            dve.tensor_tensor(x, x, tmp[:, 1], ALU.add).then_inc(s_final, 1)

        class Attention:

            LAG = 3

            def __init__(self, which, per_group, R, scores, pv, wo, blocks=lambda k: NTT, heads=HEADS,
                         unit=None, n_scores=4, by_rows=False):
                self.s = att[which]
                self.banks = score_banks[0:n_scores]
                self.unit = unit or per_group * NTT
                self.by_rows = by_rows
                self.heads, self.per_group, self.R = heads, per_group, R
                self.scores, self.pv_products, self.wo, self.blocks = scores, pv, wo, blocks
                self.nt = heads * NTT
                self.groups = heads // per_group
                self.per = per_group * NTT
                self.units = self.per // self.unit
                self.steps = self.nt + 12

            def wait_copied(self, eng, k):
                eng.wait_ge(self.s["ev_dve" if k % 2 == 0 else "ev_act"], k // 2 + 1)

            def at(self, tau, after):
                g, r = divmod(tau - after - self.LAG - (self.per - 1), self.per)
                return g if r == 0 and 0 <= g < self.groups else None

            def unit_at(self, tau, after):
                u, r = divmod(tau - after - self.LAG - (self.unit - 1), self.unit)
                return u if r == 0 and 0 <= u < self.nt // self.unit else None

            def number(self, g, m, i):
                return g * self.per + (i * self.per_group + m if self.by_rows else m * NTT + i)

            def copy_tile(self, eng, k):
                h, i = divmod(k, NTT)
                n = self.blocks(k)
                eng.wait_ge(self.s["turned"], k + 1)
                if h >= 4:
                    eng.wait_ge(self.s["pv"], (k - 4 * NTT) // self.unit + 1)
                dst = pt[:, h % 4, 0:n, i * 128:(i + 1) * 128]
                src = bank_t[k % 2][:, 0:n * 128].rearrange("p (j i) -> p j i", j=n)
                if k % 2 == 0:
                    nc.vector.tensor_copy(dst, src).then_inc(self.s["ev_dve"], 1)
                else:
                    nc.scalar.activation(dst, src, ACT.Copy).then_inc(self.s["ev_act"], 1)

            def spread_sums(self, pe, g, bank):
                rows = 128 // self.per_group
                for i in range(NTT):
                    for m in range(self.per_group):
                        k = self.number(g, m, i)
                        last = pe.matmul(bank[rows * m:rows * m + rows, i * 128:(i + 1) * 128],
                                         rowsum[:, k:k + 1].to_broadcast([128, rows]), ident[:, :],
                                         start=True, stop=True, skip_group_check=True)
                return last

            def pe(self, pe):
                s = self.s
                for tau in range(self.steps):
                    if tau < self.nt:
                        n = len(self.banks)
                        if tau >= n:
                            pe.wait_ge(s["exped"], tau - n + 1)
                        self.scores(pe, tau, self.banks[tau % len(self.banks)]).then_inc(s["scored"], 1)
                    k = tau - self.LAG
                    if 0 <= k < self.nt:
                        pe.wait_ge(s["exped"], k + 1)
                        if k >= 2:
                            self.wait_copied(pe, k - 2)
                        for j in range(self.blocks(k)):
                            last = pe.transpose(bank_t[k % 2][:, j * 128:(j + 1) * 128],
                                                prob[:, k % 3, j * 128:(j + 1) * 128], ident[:, :])
                        last.then_inc(s["turned"], 1)
                    u = self.unit_at(tau, 2)
                    if u is not None:
                        self.wait_copied(pe, self.unit * (u + 1) - 1)
                        self.wait_copied(pe, self.unit * (u + 1) - 2)
                        g = u // self.units
                        if g >= len(self.R.banks):
                            self.R.wait_emptied(pe, f"R{g - len(self.R.banks)}")
                        self.pv_products(pe, u).then_inc(s["pv"], 1)
                    g = self.at(tau, 5)
                    if g is not None:
                        pe.wait_ge(s["inverted"], g + 1)
                        pe.wait_ge(s["craw"], g + 1)
                        self.spread_sums(pe, g, self.R.bank(f"R{g}")).then_inc(self.R.filled, 1)
                    g = self.at(tau, 8)
                    if g is not None:
                        self.R.wait_emptied(pe, f"R{g}")
                        for t in range(NTT):
                            last = pe.matmul(bank_o[:, t * 128:(t + 1) * 128], ctx_n[:, g % 2, t * 128:(t + 1) * 128],
                                             self.wo[:, g, :], start=(g == 0 and t == 0), stop=(g == self.groups - 1),
                                             skip_group_check=True)
                        last.then_inc(s["projected"], 1)

            def act(self, act):
                s = self.s
                for tau in range(self.steps):
                    k = tau - self.LAG
                    if 0 <= k < self.nt and k % 2 == 1:
                        self.copy_tile(act, k)
                    if tau < self.nt:
                        act.wait_ge(s["maxed"], tau + 1)
                        if tau >= 3:
                            act.wait_ge(s["turned"], tau - 2)
                        n = self.blocks(tau) * 128
                        act.activation(prob[:, tau % 3, 0:n], self.banks[tau % len(self.banks)][:, 0:n], ACT.Exp,
                                       bias=negmax[:, tau:tau + 1], accum_out=rowsum[:, tau:tau + 1]
                                       ).then_inc(s["exped"], 1)
                    g = self.at(tau, 3)
                    if g is not None:
                        act.wait_ge(s["pv"], (g + 1) * self.units)
                        if g >= 1:
                            self.R.wait_emptied(act, f"R{g - 1}")
                        act.activation(ctx_raw[:, :], self.R.bank(f"R{g}")[:, :], ACT.Copy).then_inc(s["craw"], 1)

            def dve(self, dve):
                s = self.s
                for tau in range(self.steps):
                    if tau < self.nt:
                        dve.wait_ge(s["scored"], tau + 1)
                        n = self.blocks(tau) * 128
                        dve.tensor_reduce(negmax[:, tau:tau + 1], self.banks[tau % len(self.banks)][:, 0:n], AX.X, ALU.max,
                                          negate=True).then_inc(s["maxed"], 1)
                    k = tau - self.LAG
                    if 0 <= k < self.nt and k % 2 == 0:
                        self.copy_tile(dve, k)
                    g = self.at(tau, 3)
                    if g is not None:
                        cols = rowsum[:, g * self.per:(g + 1) * self.per]
                        dve.wait_ge(s["exped"], (g + 1) * self.per)
                        dve.reciprocal(cols, cols).then_inc(s["inverted"], 1)
                    g = self.at(tau, 6)
                    if g is not None:
                        dve.wait_ge(s["craw"], g + 1)
                        self.R.wait_filled(dve, f"R{g}")
                        if g >= 2:
                            dve.wait_ge(s["projected"], g - 1)
                        dve.tensor_tensor(ctx_n[:, g % 2, :], ctx_raw[:, :], self.R.bank(f"R{g}")[:, :],
                                          ALU.mult).then_inc(self.R.emptied["dve"], 1)

        def carve(base, spec):
            at, views = 0, {}
            for name, shape in spec:
                n = int(np.prod(shape[1:]))
                v = base[0:shape[0], at:at + n]
                if len(shape) == 3:
                    v = v.rearrange("p (a b) -> p a b", a=shape[1])
                elif len(shape) == 4:
                    v = v.rearrange("p (a b c) -> p a b c", a=shape[1], b=shape[2])
                views[name] = v
                at += n
            assert at <= base.shape[1], (at, base.shape)
            return views

        spec0 = [(n, T[n].shape) for n in ("w0_lin", "w0_g", "w0_e", "w0_be")]
        spec2 = [(n, T[n].shape) for n in ("w2_qk", "w2_v", "w2_ln", "w2_o", "w2_fe", "w2_fb", "w2_fbv", "w2_g1",
                                           "w2_b1", "w2_g2", "w2_b2", "w2_fo")]
        spec1 = [(n, T[n].shape) for n in ("w1_qkv", "w1_o", "w1_bo", "w1_r", "w1_rb", "w1_e1", "w1_eb1", "w1_e2",
                                           "w1_eb2")]
        w_a = carve(wa, spec0 + spec2)
        w_b = carve(wb, spec1)
        w = {**w_a, **w_b}
        W3B = ("w3_lin", "w3_o", "w3_up", "w3_gate", "w3_down", "w3_rt", "w3_relk", "w3_rv0", "w3_rv1", "w3_rvb",
               "w3_m0", "w3_m1", "w3_ma", "w3_sel")
        late_views = carve(wb, [(n, T[n].shape) for n in W3B])

        def loads_sync(sp):
            sp.dma_start(x_all[:, :, :, :].rearrange("p b t d -> p (b t) d"),
                         T["x"].rearrange("b (t p) d -> p (b t) d", p=128)).then_inc(kept["loaded"], 16)
            for n in ("ident", "causal", "tri", "ones_row"):
                dst = {"ident": ident, "causal": causal_f, "tri": tri, "ones_row": ones_row}[n]
                sp.dma_start(dst[tuple(slice(None) for _ in dst.shape)], T[n]).then_inc(kept["consts"], 16)
            for key, spec in (("w0", spec0), ("w1", spec1), ("w2", spec2)):
                for n, _ in spec:
                    sp.dma_start(w[n], T[n]).then_inc(kept[key], 16)

        def wait_weights(eng, key, n):
            eng.wait_ge(kept[key], 16 * n)

        L0A = lambda: Jobs(bank_m, a_fill, {"act": a_act, "dve": a_dve},
                           [("X", "act"), ("LG", "dve"), ("Q", "act"), ("K", "act"), ("V", "dve"), ("AK", "act"),
                            ("U", "dve"), ("GT", "dve")])
        L0F = lambda: Jobs(bank_s + bank_t, f_fill, {"act": f_act, "dve": f_dve},
                           [("B", "dve")] + [(f"Y{e}", "dve") for e in range(L0_EXPERTS)])
        q0, k0, ak0, v0 = (arena_f[:, i * S:(i + 1) * S] for i in range(4))
        u0 = arena_f[:, 4 * S:5 * S].rearrange("p (j d) -> p j d", j=NTT)
        gT = ctx_raw

        def l0_scores(pe, k, bank):
            return pe.matmul(bank[:, :], q0[:, k * 128:(k + 1) * 128], ak0, start=True, stop=True)

        def l0_attention():
            return Attention(0, 1, None, l0_scores, None, None, heads=1)

        def layer0_tensor(pe):
            wait_weights(pe, "consts", 4)
            wait_weights(pe, "w0", len(spec0))
            with iterations(pe, 0) as b:
                A, F, M = L0A(), L0F(), l0_attention()
                turn_xn(pe, A)
                A.wait_emptied(pe, "X")
                token_products(pe, A, "LG", w["w0_g"], L0_EXPERTS)
                project(pe, A, "Q", w["w0_lin"][:, 0, :], xnT[:, :])
                project(pe, A, "K", w["w0_lin"][:, 1, :], xnT[:, :])
                project(pe, A, "V", w["w0_lin"][:, 2, :], xnT[:, :])
                A.wait_emptied(pe, "K")
                project(pe, A, "AK", w["w0_lin"][:, 3, :], k0)
                A.wait_emptied(pe, "V")
                token_products(pe, A, "U", w["w0_lin"][:, 4, :], D, lhs=v0)
                pe.wait_ge(s_gate, 1)
                A.wait_free(pe, "GT")
                for t in range(NTT):
                    last = pe.transpose(A.bank("GT")[0:L0_EXPERTS, t * 128:(t + 1) * 128],
                                        gate[:, t, 0:L0_EXPERTS], ident[:, :])
                last.then_inc(A.filled, 1)
                A.wait_emptied(pe, "GT")
                token_products(pe, F, "B", w["w0_be"], D, lhs=gT[0:L0_EXPERTS])
                for e in range(L0_EXPERTS):
                    token_products(pe, F, f"Y{e}", w["w0_e"][:, e, :], D)
                F.wait_all_free(pe)
                A.wait_emptied(pe, "AK")
                s = M.s
                for tau in range(NTT + 2):
                    if tau < NTT:
                        if tau >= 3:
                            pe.wait_ge(s["exped"], tau - 2)
                        l0_scores(pe, tau, bank_s[tau % 3]).then_inc(s["scored"], 1)
                    k = tau - 2
                    if k >= 0:
                        pe.wait_ge(s["exped"], k + 1)
                        if k >= 2:
                            M.wait_copied(pe, k - 2)
                        for j in range(NTT):
                            last = pe.transpose(bank_t[k % 2][:, j * 128:(j + 1) * 128],
                                                prob[:, k % 3, j * 128:(j + 1) * 128], ident[:, :])
                        last.then_inc(s["turned"], 1)
                A.wait_emptied(pe, "U")
                for i in range(NTT):
                    M.wait_copied(pe, i)
                    for j in range(NTT):
                        last = pe.matmul(bank_v[:, i * 128:(i + 1) * 128], pt[:, 0, j, i * 128:(i + 1) * 128],
                                         u0[:, j, :], start=(j == 0), stop=(j == NTT - 1))
                last.then_inc(s["pv"], 1)
                meet(pe, kept["go0"], b)

        def layer0_scalar(act):
            wait_weights(act, "consts", 4)
            with iterations(act, 0) as b:
                A, F, M = L0A(), L0F(), l0_attention()
                evac(act, A, "X", xnT[:, :])
                evac(act, A, "Q", q0)
                exp_logits(act, NTT, L0_EXPERTS)
                evac(act, A, "K", k0)
                evac(act, A, "AK", ak0)
                s = M.s
                for tau in range(NTT + 2):
                    if tau < NTT:
                        act.wait_ge(s["maxed"], tau + 1)
                        if tau >= 3:
                            act.wait_ge(s["turned"], tau - 2)
                        act.activation(prob[:, tau % 3, :], bank_s[tau % 3][:, :], ACT.Exp,
                                       bias=negmax[:, tau:tau + 1], accum_out=rowsum[:, tau:tau + 1]
                                       ).then_inc(s["exped"], 1)
                    if tau >= 2 and tau % 2 == 1:
                        M.copy_tile(act, tau - 2)
                silu_tanh(act, L0_EXPERTS)
                meet(act, kept["go0"], b)

        def layer0_vector(dve):
            wait_weights(dve, "loaded", 1)
            wait_weights(dve, "consts", 4)
            dve.tensor_copy(ident_b[:, :], ident[:, :])
            dve.tensor_copy(causal_b[:, :], causal_f[:, :]).then_inc(kept["causal_set"], 1)
            with iterations(dve, 0) as b:
                A, F, M = L0A(), L0F(), l0_attention()
                d = Steps(dve, s_dve)
                layer_norm(dve, b, d)
                E = L0_EXPERTS
                evac(dve, A, "LG", lg[:, :, 0:E], A.bank("LG")[:, 0:NTT * E].rearrange("p (t e) -> p t e", t=NTT))
                A.wait_emptied(dve, "LG")
                shifted(dve, d, lg[:, :, 0:E], NTT, E)
                n = NTT * E * E
                top_k(dve, d, lg[:, :, 0:E], NTT, E, 2, gate[:, :, 0:E], prob_f[:, 0:n], prob_f[:, n:2 * n])
                evac(dve, A, "V", v0)
                gates(dve, d, NTT, E, of_all=False)
                evac(dve, A, "U", u0, bank3(A.bank("U")))
                evac(dve, A, "GT", gT[0:E, :], A.bank("GT")[0:E, :])
                evac(dve, F, "B", acc[:, :, :], bank3(F.bank("B")))
                for e in range(E):
                    gated(dve, F, e)
                s = M.s
                for tau in range(NTT + 2):
                    if tau < NTT:
                        dve.wait_ge(s["scored"], tau + 1)
                        dve.tensor_reduce(negmax[:, tau:tau + 1], bank_s[tau % 3][:, :], AX.X, ALU.max,
                                          negate=True).then_inc(s["maxed"], 1)
                    if tau >= 2 and tau % 2 == 0:
                        M.copy_tile(dve, tau - 2)
                silu(dve, d)
                dve.wait_ge(s["pv"], 1)
                dve.wait_ge(s["exped"], NTT)
                d.add(dve.reciprocal(rowsum[:, 0:NTT], rowsum[:, 0:NTT]))
                d.settle()
                d.add(dve.tensor_tensor(tmp[:, 0], bank3(bank_v),
                                        rowsum[:, 0:NTT].unsqueeze(2).to_broadcast([128, NTT, D]), ALU.mult))
                d.settle()
                residual(dve, d, b, tmp[:, 0])
                meet(dve, kept["go0"], b)

        def layer0_gpsimd(pool):
            pool.memset(minus_half[:, :], -0.5).then_inc(kept["half_set"], 1)
            pool.wait_ge(kept["half_set"], 1)
            with iterations(pool, 0) as b:
                F = L0F()
                inverse_deviation(pool)
                add_up(pool, F, range(L0_EXPERTS), "B")
                meet_and_clear(pool, kept["go0"], b, others=3)

        QK1 = [f"{m}{c}" for c in range(8) for m in "QK"]
        all_banks = bank_m + bank_s + bank_t + [bank_v]
        L1A = lambda: Jobs(all_banks, a_fill, {"act": a_act, "dve": a_dve},
                           [("X", "act"), ("LG", "dve")]
                           + [(n, "act" if n[0] == "Q" else "dve") for n in QK1]
                           + [(f"V{t}{i}", "dve" if i else "act") for t in range(NTT) for i in range(2)]
                           + [("H0", "act"), ("GT", "dve"), ("B", "dve")]
                           + [j for e in range(L1_EXPERTS)
                              for j in ([(f"H{e + 1}", "act")] if e + 1 < L1_EXPERTS else []) + [(f"Y{e}", "dve")]])
        L1R = lambda: Jobs([bank_v], r_fill, {"dve": r_dve}, [(f"R{g}", "dve") for g in range(8)])
        q1 = arena_f[:, 0:16 * S].rearrange("p (h s) -> p h s", h=L1_HEADS)
        k1 = arena_f[:, 16 * S:24 * S].rearrange("p (c s) -> p c s", c=8)
        v1 = arena_f[:, 24 * S:32 * S].rearrange("p (t n) -> p t n", t=NTT)
        hid = pt[:, 0]

        def l1_scores(pe, k, bank):
            h, i = divmod(k, NTT)
            return pe.matmul(bank[:, :], q1[:, h, i * 128:(i + 1) * 128], k1[:, h // 2, :], start=True, stop=True)

        def l1_pv(pe, g):
            for j in range(NTT):
                for m in range(2):
                    h = 2 * g + m
                    last = pe.matmul(bank_v[64 * m:64 * m + 64, :], v1[:, j, h * 64:(h + 1) * 64], pt[:, h % 4, j, :],
                                     start=(j == 0), stop=(j == NTT - 1), skip_group_check=True)
            return last

        def l1_attention():
            return Attention(0, 2, L1R(), l1_scores, l1_pv, w["w1_o"])

        def layer1_tensor(pe):
            wait_weights(pe, "w1", len(spec1))
            with iterations(pe, 1) as b:
                A, M = L1A(), l1_attention()
                turn_xn(pe, A)
                A.wait_emptied(pe, "X")
                token_products(pe, A, "LG", w["w1_r"], 15, bias=w["w1_rb"])
                for n in QK1:
                    c = int(n[1:])
                    project(pe, A, n, w["w1_qkv"][:, "QK".index(n[0]), c * 128:(c + 1) * 128], xnT[:, :])
                for t in range(NTT):
                    for i in range(2):
                        A.wait_free(pe, f"V{t}{i}")
                        pe.matmul(A.bank(f"V{t}{i}")[:, :], xnT[:, t * 128:(t + 1) * 128],
                                  w["w1_qkv"][:, 2, i * 512:(i + 1) * 512], start=True, stop=True
                                  ).then_inc(A.filled, 1)
                project(pe, A, "H0", w["w1_e1"][:, 0, :], xnT[:, :])
                pe.wait_ge(s_gate, 1)
                A.wait_free(pe, "GT")
                for t in range(NTT):
                    last = pe.transpose(A.bank("GT")[0:16, t * 128:(t + 1) * 128], gate[:, t, :], ident[:, :])
                last.then_inc(A.filled, 1)
                A.wait_emptied(pe, "GT")
                token_products(pe, A, "B", w["w1_eb2"], D, lhs=gT[0:16])
                for e in range(L1_EXPERTS):
                    if e + 1 < L1_EXPERTS:
                        project(pe, A, f"H{e + 1}", w["w1_e1"][:, e + 1, :], xnT[:, :])
                    A.wait_emptied(pe, f"H{e}")
                    token_products(pe, A, f"Y{e}", w["w1_e2"][:, e, :], D, lhs=hid[:, e % 4, :])
                A.wait_all_free(pe)
                M.pe(pe)
                for t in range(NTT):
                    last = pe.matmul(bank_o[:, t * 128:(t + 1) * 128], ones_row[0:1, :], w["w1_bo"],
                                     start=False, stop=True, skip_group_check=True)
                last.then_inc(M.s["projected"], 1)
                meet(pe, kept["go1"], b)

        def layer1_scalar(act):
            wait_weights(act, "w1", len(spec1))
            with iterations(act, 1) as b:
                A, M = L1A(), l1_attention()
                evac(act, A, "X", xnT[:, :])
                act.wait_ge(kept["q1_zeroed"], 1)
                for n in QK1:
                    if n[0] == "Q":
                        A.wait_filled(act, n)
                        for m in range(2):
                            rows = slice(64 * m, 64 * m + 64)
                            last = act.activation(q1[rows, 2 * int(n[1:]) + m, :], A.bank(n)[rows, :], ACT.Copy,
                                                  scale=L1_DH ** -0.5)
                        last.then_inc(a_act, 1)
                    if n == "Q1":
                        exp_logits(act, NTT, 15)
                for t in range(NTT):
                    evac(act, A, f"V{t}0", v1[:, t, 0:512])
                for e in range(L1_EXPERTS):
                    if e >= 4:
                        A.wait_filled(act, f"Y{e - 4}")
                    A.wait_filled(act, f"H{e}")
                    act.activation(hid[:, e % 4, :], A.bank(f"H{e}")[:, :], ACT.Relu, bias=w["w1_eb1"][:, e:e + 1]
                                   ).then_inc(A.emptied["act"], 1)
                silu_tanh(act, L1_EXPERTS)
                M.act(act)
                meet(act, kept["go1"], b)

        def layer1_vector(dve):
            with iterations(dve, 1) as b:
                A, M = L1A(), l1_attention()
                d = Steps(dve, s_dve)
                layer_norm(dve, b, d)
                E = 15
                evac(dve, A, "LG", lg[:, :, 0:E], A.bank("LG")[:, 0:NTT * E].rearrange("p (t e) -> p t e", t=NTT))
                A.wait_emptied(dve, "LG")
                shifted(dve, d, lg[:, :, 0:E], NTT, E)
                n = NTT * E * E
                vp = v_pad[:, :, :, :].rearrange("p a b c -> p (a b c)")
                top_k(dve, d, lg[:, :, 0:E], NTT, E, 3, gate[:, :, 0:E], vp[:, 0:n], vp[:, n:2 * n])
                d.add(dve.memset(gate[:, :, 15:16], 1.0))
                for c in range(8):
                    evac(dve, A, f"K{c}", k1[:, c, :])
                for t in range(NTT):
                    evac(dve, A, f"V{t}1", v1[:, t, 512:1024])
                gates(dve, d, NTT, E, of_all=True)
                evac(dve, A, "GT", gT[0:16, :], A.bank("GT")[0:16, :])
                evac(dve, A, "B", acc[:, :, :], bank3(A.bank("B")))
                for e in range(L1_EXPERTS):
                    gated(dve, A, e)
                silu(dve, d)
                M.dve(dve)
                dve.wait_ge(M.s["projected"], M.groups + 1)
                residual(dve, d, b, bank3(bank_o))
                meet(dve, kept["go1"], b)

        def layer1_gpsimd(pool):
            pool.memset(arena_f[:, 0:16 * S], 0.0).then_inc(kept["q1_zeroed"], 1)
            with iterations(pool, 1) as b:
                inverse_deviation(pool)
                add_up(pool, L1A(), range(L1_EXPERTS), "B")
                meet_and_clear(pool, kept["go1"], b, others=3)

        scratch = nc.dram_tensor("qk_parts", (4, NPARTS, 2, 128, S), bf16).ap()

        def stack(slot):
            return arena[:, slot * HEADS * S:(slot + 1) * HEADS * S].rearrange("p (h s) -> p h s", h=HEADS)

        def send_parts(sp, version, parts, ready, n, stored):
            sp.wait_ge(ready, n)
            sp.dma_start(scratch[version].rearrange("a q p s -> p (a q) s"), parts).then_inc(stored, 16)

        def fetch_stack(sp, version, which, slot, is_query, done):
            for s_ in range(NPARTS * NPARTS):
                part = s_ // NPARTS if is_query else s_ % NPARTS
                sp.dma_start(stack(slot)[s_ * DH:(s_ + 1) * DH],
                             scratch[version, part, which].rearrange("(h d) s -> d h s", d=DH)).then_inc(done, 16)

        N_FETCH = 16 * NPARTS * NPARTS

        class Split:

            def __init__(self, number, whole, parts):
                self.n, self.whole, self.parts = number, whole, parts

            def act(self, act):
                for i in range(2):
                    if i:
                        act.wait_ge(s_rest, 2 * self.n + 1)
                    act.activation(self.parts[:, i], self.whole, ACT.Copy).then_inc(s_round, 1)

            def dve(self, dve):
                for i in range(2):
                    dve.wait_ge(s_round, 2 * self.n + i + 1)
                    if i:
                        dve.wait_ge(s_rest, 2 * self.n + 1)
                    dst = self.parts[:, 2] if i else self.whole
                    dve.tensor_tensor(dst, self.whole, self.parts[:, i], ALU.subtract).then_inc(s_rest, 1)

        def part_view(words):
            return words.bitcast(bf16).rearrange("p (a n) -> p a n", a=NPARTS)

        L2A = lambda: Jobs(bank_m, a_fill, {"act": a_act, "dve": a_dve},
                           [("X", "act"), ("P1", "dve"), ("QK0", "dve"), ("QK1", "act"), ("P2", "dve"), ("VA", "act"),
                            ("WT", "dve"), ("FQ", "dve"), ("FK", "dve"), ("FV", "act"), ("QT", "act"), ("KT", "act")])
        v_banks = [bank_v, bank_m[0]]
        L2R = lambda i: Jobs(v_banks, (r_fill, r2_fill)[i], {"dve": (r_dve, r2_dve)[i]},
                             [(f"R{g}", "dve") for g in range(4)])
        heads_qk = pt_f[:, 0:1024]
        heads_sq = pt_f[:, 1024:2048]
        whole2 = [pt_f[:, 2048:3072], pt_f[:, 3072:4096]]
        parts2 = [part_view(pt_f[:, 4096:5632]), part_view(pt_f[:, 5632:7168])]
        mixed_w = pt_f[:, 7168:7552]
        h_sum, h_var = pt_f[:, 7552:7680], pt_f[:, 7680:7808]
        pooled, hidden1, mixed_b, prod_b = small[:, 0:1], small[:, 1:2], small[:, 2:4], small[:, 4:12]
        ln_scaled = small[:, 16:48].rearrange("p (a d) -> p a d", a=4)
        va = xn

        def stacked_scores(first_slot, causal):
            def scores(pe, k, bank):
                g, r = divmod(k, 4 * NTT)
                i, m = divmod(r, 4)
                h = 4 * g + m
                n = (i + 1) * 128 if causal else S
                last = pe.matmul(bank[:, 0:n], stack(first_slot)[:, h, i * 128:(i + 1) * 128],
                                 stack(first_slot + 1)[:, h, 0:n], start=True, stop=not causal)
                if causal:
                    last = pe.matmul(bank[:, i * 128:n], ident_b[:, :], causal_b[:, :], start=False, stop=True)
                return last
            return scores

        def group_pv(causal):
            def pv(pe, u):
                g, i = divmod(u, NTT)
                n = i + 1 if causal else NTT
                for j in range(n):
                    for m in range(4):
                        last = pe.matmul(v_banks[g % 2][GROW * m:GROW * (m + 1), i * 128:(i + 1) * 128],
                                         v_pad[:, j, 4 * g + m, :], pt[:, u % 4, j, m * 128:(m + 1) * 128],
                                         start=(j == 0), stop=(j == n - 1), skip_group_check=True)
                return last
            return pv

        def l2_attention(i):
            return Attention(i, 4, L2R(i), stacked_scores(2 * i, i == 1), group_pv(i == 1),
                             w["w2_fo"] if i == 0 else w["w2_o"],
                             blocks=(lambda k: k % (4 * NTT) // 4 + 1) if i == 1 else (lambda k: NTT),
                             unit=4, n_scores=3, by_rows=True)

        def layer2_tensor(pe):
            wait_weights(pe, "w2", len(spec2))
            pe.wait_ge(kept["v_set"], 2)
            pe.wait_ge(kept["causal_set"], 1)
            with iterations(pe, 2) as b:
                A = L2A()
                turn_xn(pe, A)
                pe.wait_ge(s_pooled, 1)
                project(pe, A, "P1", w["w2_g1"], pooled, n=1)
                for i in range(2):
                    A.wait_free(pe, f"QK{i}")
                    for t in range(2):
                        last = pe.matmul(A.bank(f"QK{i}")[:, t * 256:(t + 1) * 256],
                                         xnT[:, (2 * i + t) * 128:(2 * i + t + 1) * 128], w["w2_qk"],
                                         start=True, stop=True)
                    last.then_inc(A.filled, 1)
                A.wait_emptied(pe, "P1")
                project(pe, A, "P2", hidden1.to_broadcast([128, 128]), w["w2_g2"], n=4)
                token_products(pe, A, "VA", w["w2_v"], D)
                pe.wait_ge(s_gate, 1)
                A.wait_free(pe, "WT")
                pe.transpose(A.bank("WT")[0:4, 0:128], gate[:, 0, 0:4], ident[:, :]).then_inc(A.filled, 1)
                pe.wait_ge(s_mixed, 1)
                project(pe, A, "FQ", mixed_w[:, 0:128], xnT[:, :])
                project(pe, A, "FK", mixed_w[:, 128:256], xnT[:, :])
                A.wait_free(pe, "FV")
                A.wait_emptied(pe, "WT")
                for t in range(NTT):
                    o = A.bank("FV")[:, t * 128:(t + 1) * 128]
                    pe.matmul(o, xnT[:, t * 128:(t + 1) * 128], mixed_w[:, 256:384], start=True, stop=False)
                    last = pe.matmul(o, gT[0:4, 0:128], w["w2_fbv"], start=False, stop=True)
                last.then_inc(A.filled, 1)
                pe.wait_ge(s_normed, 1)
                for i, n in enumerate(("QT", "KT")):
                    A.wait_free(pe, n)
                    for t in range(NTT):
                        last = pe.transpose(A.bank(n)[:, t * 128:(t + 1) * 128],
                                            heads_qk[:, (2 * t + i) * 128:(2 * t + i + 1) * 128], ident[:, :])
                    last.then_inc(A.filled, 1)
                A.wait_all_free(pe)
                for i in range(2):
                    pe.wait_ge(s_stacked[i], 2 * N_FETCH)
                    if i:
                        pe.wait_ge(s_again, 1)
                        pe.wait_ge(s_taken, 1)
                    l2_attention(i).pe(pe)
                meet(pe, kept["go2"], b)

        def layer2_scalar(act):
            wait_weights(act, "w2", len(spec2))
            with iterations(act, 2) as b:
                A = L2A()
                evac(act, A, "X", xnT[:, :])
                evac(act, A, "QK1", heads_qk[:, 512:1024])
                exp_logits(act, 1, 4)
                evac(act, A, "VA", flat(va[:, :, :]))
                A.wait_emptied(act, "FQ")
                A.wait_emptied(act, "FK")
                Split(0, whole2[0], parts2[0]).act(act)
                act.wait_ge(s_hvar, 1)
                act.activation(h_var, h_var, ACT.Sqrt).then_inc(s_hrstd, 1)
                act.wait_ge(kept["v_set"], 2)
                act_copy = A.bank("FV")[:, :].rearrange("p (t h d) -> p t h d", t=NTT, h=HEADS)
                A.wait_filled(act, "FV")
                act.activation(v_pad[:, :, :, 0:DH], act_copy, ACT.Copy).then_inc(A.emptied["act"], 1)
                evac(act, A, "QT", whole2[1][:, 0:S])
                evac(act, A, "KT", whole2[1][:, S:2 * S])
                A.wait_emptied(act, "KT")
                Split(1, whole2[1], parts2[1]).act(act)
                for i in range(2):
                    if i == 0:
                        act.wait_ge(s_sent, 32)
                    l2_attention(i).act(act)
                    if i == 0:
                        act.wait_ge(s_taken, 1)
                        act.activation(flat(tmp[:, 0]), acc_f, ACT.Tanh, scale=0.5).then_inc(s_e1, 1)
                meet(act, kept["go2"], b)

        def layer2_vector(dve):
            wait_weights(dve, "w2", len(spec2))
            scale2 = float(D) ** -0.25
            dve.memset(arena_f[64:128, 16 * S:32 * S], 0.0).then_inc(kept["keys_zeroed"], 1)
            dve.tensor_scalar(ln_scaled, w["w2_ln"], scale2, None, ALU.mult).then_inc(kept["causal_set"], 1)
            dve.wait_ge(kept["causal_set"], 2)
            with iterations(dve, 2) as b:
                A = L2A()
                d = Steps(dve, s_dve)
                layer_norm(dve, b, d)
                A.wait_emptied(dve, "X")
                d.add(dve.tensor_reduce(pooled, xnT[:, :], AX.X, ALU.add))
                d.settle()
                dve.tensor_scalar(pooled, pooled, 1.0 / S, None, ALU.mult).then_inc(s_pooled, 1)
                A.wait_filled(dve, "P1")
                dve.tensor_scalar(hidden1, A.bank("P1")[:, 0:1], w["w2_b1"], 0.0, ALU.add, ALU.max
                                  ).then_inc(A.emptied["dve"], 1)
                evac(dve, A, "QK0", heads_qk[:, 0:512])
                A.wait_filled(dve, "P2")
                dve.tensor_tensor(lg[:, 0, 0:4], A.bank("P2")[:, 0:4], w["w2_b2"], ALU.add
                                  ).then_inc(A.emptied["dve"], 1)
                A.wait_emptied(dve, "P2")
                shifted(dve, d, lg[:, 0:1, 0:4], 1, 4)
                top_k(dve, d, lg[:, 0:1, 0:4], 1, 4, 2, gate[:, 0:1, 0:4], prob_f[:, 0:16], prob_f[:, 16:32])
                gates(dve, d, 1, 4, of_all=False)
                dve.wait_ge(s_gate, 1)
                for e in range(4):
                    if e == 0:
                        d.add(dve.tensor_scalar(mixed_w, w["w2_fe"][:, 0, :], gate[:, 0, 0:1], None, ALU.mult))
                    else:
                        d.settle()
                        d.add(dve.scalar_tensor_tensor(mixed_w, w["w2_fe"][:, e, :], gate[:, 0, e:e + 1], mixed_w,
                                                       ALU.mult, ALU.add))
                d.settle()
                pb = prod_b.rearrange("p (a e) -> p a e", a=2)
                dve.tensor_tensor(pb, w["w2_fb"], gate[:, 0:1, 0:4].to_broadcast([128, 2, 4]), ALU.mult
                                  ).then_inc(s_mixed, 1)
                dve.wait_ge(s_mixed, 1)
                d.add(dve.tensor_reduce(mixed_b, pb, AX.X, ALU.add))
                d.settle()
                evac(dve, A, "WT", gT[0:4, 0:128], A.bank("WT")[0:4, 0:128])
                A.wait_filled(dve, "FQ")
                dve.tensor_scalar(whole2[0][:, 0:S], A.bank("FQ")[:, :], mixed_b[:, 0:1], DH ** -0.5, ALU.add, ALU.mult
                                  ).then_inc(A.emptied["dve"], 1)
                A.wait_filled(dve, "FK")
                dve.tensor_scalar(whole2[0][:, S:2 * S], A.bank("FK")[:, :], mixed_b[:, 1:2], None, ALU.add
                                  ).then_inc(A.emptied["dve"], 1)
                A.wait_emptied(dve, "FK")
                Split(0, whole2[0], parts2[0]).dve(dve)
                A.wait_emptied(dve, "QK0")
                A.wait_emptied(dve, "QK1")
                v = heads_qk.rearrange("p (n d) -> p n d", d=DH)
                sq = heads_sq.rearrange("p (n d) -> p n d", d=DH)
                n = NTT * 2 * HEADS
                wide = [128, n, DH]
                d.add(dve.tensor_reduce(h_sum, v, AX.X, ALU.add))
                d.settle()
                d.add(dve.tensor_scalar(h_sum, h_sum, 1.0 / DH, None, ALU.mult))
                d.settle()
                d.add(dve.tensor_tensor(v, v, h_sum.unsqueeze(2).to_broadcast(wide), ALU.subtract))
                d.settle()
                d.add(dve.tensor_tensor(sq, v, v, ALU.mult))
                d.settle()
                d.add(dve.tensor_reduce(h_var, sq, AX.X, ALU.add))
                d.settle()
                dve.tensor_scalar(h_var, h_var, 1.0 / DH, EPS, ALU.mult, ALU.add).then_inc(s_hvar, 1)
                dve.wait_ge(s_hrstd, 1)
                d.add(dve.reciprocal(h_var, h_var))
                d.settle()
                d.add(dve.tensor_tensor(v, v, h_var.unsqueeze(2).to_broadcast(wide), ALU.mult))
                d.settle()
                v5 = heads_qk.rearrange("p (t a h d) -> p t a h d", t=NTT, a=2, h=HEADS)
                for what, op in ((0, ALU.mult), (2, ALU.add)):
                    for a in range(2):
                        par = ln_scaled[:, what + a, :].unsqueeze(1).unsqueeze(1).to_broadcast([128, NTT, HEADS, DH])
                        ins = dve.tensor_tensor(v5[:, :, a], v5[:, :, a], par, op)
                        if what == 2 and a == 1:
                            ins.then_inc(s_normed, 1)
                        else:
                            d.add(ins)
                    if what == 0:
                        d.settle()
                Split(1, whole2[1], parts2[1]).dve(dve)
                dve.wait_ge(s_sent, 32)
                l2_attention(0).dve(dve)
                dve.wait_ge(att[0]["projected"], 4)
                dve.tensor_copy(acc[:, :, :], bank3(bank_o)).then_inc(s_taken, 1)
                silu(dve, d)
                l2_attention(1).dve(dve)
                dve.wait_ge(att[1]["projected"], 4)
                residual(dve, d, b, bank3(bank_o))
                meet(dve, kept["go2"], b)

        def layer2_gpsimd(pool):
            pool.memset(arena_f[64:128, 0:16 * S], 0.0).then_inc(kept["stack_zeroed"], 1)
            pool.wait_ge(kept["stack_zeroed"], 1)
            pool.memset(v_pad[:, :, :, :].rearrange("p a b c -> p (a b c)"), 0.0).then_inc(kept["v_set"], 1)
            pool.wait_ge(kept["v_set"], 1)
            pool.memset(v_pad[:, :, :, DH:DH + 1].rearrange("p a b c -> p (a b) c"), 1.0).then_inc(kept["v_set"], 1)
            with iterations(pool, 2) as b:
                inverse_deviation(pool)
                pool.wait_ge(att[0]["pv"], 4 * NTT)
                L2A().wait_emptied(pool, "VA")
                pool.tensor_copy(v_pad[:, :, :, 0:DH], va[:, :, :].rearrange("p t (h d) -> p t h d", h=HEADS)
                                 ).then_inc(s_again, 1)
                meet_and_clear(pool, kept["go2"], b)

        def load_weights(sp, spec, views, sem_):
            for n, _ in spec:
                sp.dma_start(views[n], T[n]).then_inc(sem_, 16)

        def layer2_sync(sp):
            sp.wait_ge(kept["go1"], B)
            load_weights(sp, [(n, None) for n in W3B], {n: late_views[n] for n in W3B}, kept["w3"])
            sp.wait_ge(kept["stack_zeroed"], 1)
            sp.wait_ge(kept["keys_zeroed"], 1)
            with iterations(sp, 2) as b:
                for i in range(2):
                    send_parts(sp, i, parts2[i].rearrange("p a (q s) -> p (a q) s", q=2), s_rest, 2 * i + 2, s_sent)
                    sp.wait_ge(s_sent, 16 * (i + 1))
                    fetch_stack(sp, i, 0, 2 * i, True, s_stacked[i])
                    fetch_stack(sp, i, 1, 2 * i + 1, False, s_stacked[i])
                meet_sync(sp, kept["go2"], b)

        E_ROW = HEADS * BAND
        A_SLOT = 32 + 128 * A_ROW
        offset_scores = nc.dram_tensor("offset_scores", (S, HEADS, BAND), f32)
        skewed = nc.dram_tensor("skewed_probs", (2, NTT, A_SLOT), f32)
        spec3b = [(n, T[n].shape) for n in W3B]
        spec3a = [("w3_rk", T["w3_rk"].shape)]
        w3b = carve(wb, spec3b + [("masked0", (128, S)), ("masked1", (128, S))])
        w3a = carve(wa, spec3a + [("banded", (128, 2, NTT, 128)), ("bandedT", (BAND, 4, S))])
        N_W3 = len(spec3a) + len(spec3b)

        L3E = 4 * NTT
        L3A = lambda: Jobs(bank_m, a_fill, {"act": a_act, "dve": a_dve},
                           [("X", "act"), ("LG", "dve"), ("Q", "act"), ("K", "dve"), ("V", "act")]
                           + [(f"E{j}", "act" if j % 2 else "dve") for j in range(L3E)])
        L3F = lambda: Jobs(bank_s + bank_t, f_fill, {"act": f_act, "dve": f_dve},
                           [(f"{m}{e}{i}", "dve") for e in range(1) for i in range(2) for m in "GU"]
                           + [(n, "dve") for e in range(1, L3_EXPERTS)
                              for n in [f"{m}{e}{i}" for i in range(2) for m in "GU"] + [f"Y{e - 1}"]]
                           + [(f"Y{L3_EXPERTS - 1}", "dve")])
        L3R = lambda: Jobs([bank_v], r_fill, {"act": r_act}, [(f"R{g}", "act") for g in range(4)])
        hid3 = pt_f[:, 0:2048].rearrange("p (a i s) -> p a i s", a=2, i=2)
        tanh3 = pt_f[:, 2048:3072].rearrange("p (a s) -> p a s", a=2)
        gate3 = pt_f[:, 3072:4096].rearrange("p (a s) -> p a s", a=2)
        whole3 = [pt_f[:, 4096:5120], pt_f[:, 5120:6144]]
        parts3 = [part_view(pt_f[:, 6144:7680]), part_view(prob_f)]
        q_kept = pt_f[:, 7680:8192]
        near = tmp[:, :, :, :].rearrange("p a t d -> p (a t d)")[:, 0:2 * NTT * WIN].rearrange(
            "p (a t w) -> p a t w", a=2, t=NTT)
        sums_sb = flat(xn[:, :, :])
        bank_a = bank_s[2]
        offset_banks = bank_s[0:2] + bank_m[0:1]

        def window(i, c):
            w0 = i * 128 + 32 * c - 32
            return max(0, w0), min(S, w0 + WIN), max(0, w0) - w0

        class OffsetAttention(Attention):

            def __init__(self, b):
                self.b = b
                super().__init__(0, 4, L3R(), None, None, w3b["w3_o"])
                self.steps = self.nt + 18

            def pe(self, pe):
                s = self.s
                for tau in range(self.steps):
                    if tau < self.nt:
                        h, i = divmod(tau, NTT)
                        if tau >= 3:
                            pe.wait_ge(s["exped"], tau - 2)
                        if i == 0:
                            pe.wait_ge(s_near[h % 2], 64 * (h // 2 + 1))
                        bank = offset_banks[tau % 3]
                        for c in range(4):
                            lo, hi, at = window(i, c)
                            rows, at_q = slice(32 * c, 32 * c + 32), i * 128 + 32 * c
                            for slot, a, z in ((2, 0, lo), (3, hi, S), (1, lo, hi)):
                                if z > a:
                                    pe.matmul(bank[rows, a:z], stack(0)[:, h, at_q:at_q + 32],
                                              stack(slot)[:, h, a:z], start=True, stop=(slot != 1),
                                              skip_group_check=True)
                            last = pe.matmul(bank[rows, lo:hi], ident[:, rows], near[:, h % 2, i, at:at + hi - lo],
                                             start=False, stop=True, skip_group_check=True)
                        last.then_inc(s["scored"], 1)
                    k = tau - self.LAG
                    if 0 <= k < self.nt:
                        pe.wait_ge(s["exped"], k + 1)
                        if k >= 2:
                            self.wait_copied(pe, k - 2)
                        for j in range(NTT):
                            last = pe.transpose(bank_t[k % 2][:, j * 128:(j + 1) * 128],
                                                prob[:, k % 3, j * 128:(j + 1) * 128], ident[:, :])
                        last.then_inc(s["turned"], 1)
                    g = self.at(tau, 1)
                    if g is not None:
                        self.wait_copied(pe, self.per * (g + 1) - 1)
                        self.wait_copied(pe, self.per * (g + 1) - 2)
                        if g >= 1:
                            pe.wait_ge(s_normal, g)
                        for j in range(NTT):
                            for m in range(4):
                                last = pe.matmul(bank_v[GROW * m:GROW * (m + 1), :], v_pad[:, j, 4 * g + m, :],
                                                 pt[:, m, j, :], start=(j == 0), stop=False, skip_group_check=True)
                        last.then_inc(s["pv"], 1)
                    h, r = divmod(tau - 11, NTT)
                    if r == 0 and 0 <= h < HEADS:
                        pe.wait_ge(s_askew[h % 2], self.b * SKEWED + 16 * (h // 2 + 1))
                        if h >= 1:
                            pe.wait_ge(s_amasked, h)
                        for i in range(NTT):
                            last = pe.transpose(bank_a[0:BAND, i * 128:(i + 1) * 128],
                                                w3a["banded"][:, h % 2, i, 0:BAND], ident[:, :])
                        last.then_inc(s_aturned, 1)
                    g = self.at(tau, 7)
                    if g is not None:
                        pe.wait_ge(s_amasked, 4 * (g + 1))
                        for m in range(4):
                            last = pe.matmul(bank_v[GROW * m:GROW * (m + 1), :], w3b["w3_rvb"],
                                             w3a["bandedT"][:, m, :], start=False, stop=True, skip_group_check=True)
                        last.then_inc(s_band, 1)
                    g = self.at(tau, 9)
                    if g is not None:
                        pe.wait_ge(s["inverted"], g + 1)
                        pe.wait_ge(s["craw"], g + 1)
                        self.spread_sums(pe, g, self.R.bank(f"R{g}")).then_inc(self.R.filled, 1)
                    g = self.at(tau, 12)
                    if g is not None:
                        self.R.wait_emptied(pe, f"R{g}")
                        pe.matmul(bank_v[:, :], w3b["w3_sel"], ctx_raw[:, :], start=True, stop=False)
                        for n in range(2):
                            pe.wait_ge(s_bmasked, 2 * g + n + 1)
                            last = pe.matmul(bank_v[:, :], w3b[f"w3_rv{n}"], w3b[f"masked{n}"],
                                             start=False, stop=(n == 1))
                        last.then_inc(s_numer, 1)
                    g = self.at(tau, 14)
                    if g is not None:
                        pe.wait_ge(s_normal, g + 1)
                        for t in range(NTT):
                            last = pe.matmul(bank_o[:, t * 128:(t + 1) * 128], ctx_n[:, g % 2, t * 128:(t + 1) * 128],
                                             self.wo[:, g, :], start=(g == 0 and t == 0), stop=(g == self.groups - 1),
                                             skip_group_check=True)
                        last.then_inc(s["projected"], 1)

            def act(self, act):
                s = self.s
                for tau in range(self.steps):
                    k = tau - self.LAG
                    if 0 <= k < self.nt and k % 2 == 1:
                        self.copy_tile(act, k)
                    if tau < self.nt:
                        act.wait_ge(s["maxed"], tau + 1)
                        if tau >= 3:
                            act.wait_ge(s["turned"], tau - 2)
                            act.wait_ge(s_written[tau % 3], 16 * (tau // 3))
                        act.activation(prob[:, tau % 3, :], offset_banks[tau % 3][:, :], ACT.Exp,
                                       bias=negmax[:, tau:tau + 1], accum_out=rowsum[:, tau:tau + 1]
                                       ).then_inc(s["exped"], 1)
                    g = self.at(tau, 8)
                    if g is not None:
                        act.wait_ge(s_band, g + 1)
                        if g >= 1:
                            act.wait_ge(s_numer, g)
                        act.activation(ctx_raw[:, :], bank_v[:, :], ACT.Copy).then_inc(s["craw"], 1)
                    g = self.at(tau, 10)
                    if g is not None:
                        if g >= 1:
                            act.wait_ge(s_normal, g)
                        self.R.wait_filled(act, f"R{g}")
                        act.activation(sums_sb, self.R.bank(f"R{g}")[:, :], ACT.Copy).then_inc(r_act, 1)

            def dve(self, dve):
                s = self.s
                for tau in range(self.steps):
                    if tau < self.nt:
                        dve.wait_ge(s["scored"], tau + 1)
                        dve.tensor_reduce(negmax[:, tau:tau + 1], offset_banks[tau % 3][:, :], AX.X, ALU.max,
                                          negate=True).then_inc(s["maxed"], 1)
                    k = tau - self.LAG
                    if 0 <= k < self.nt and k % 2 == 0:
                        self.copy_tile(dve, k)
                    g = self.at(tau, 1)
                    if g is not None:
                        cols = rowsum[:, g * self.per:(g + 1) * self.per]
                        dve.wait_ge(s["exped"], (g + 1) * self.per)
                        dve.reciprocal(cols, cols).then_inc(s["inverted"], 1)
                    h, r = divmod(tau - 12, NTT)
                    if r == 0 and 0 <= h < HEADS:
                        dve.wait_ge(s_aturned, h + 1)
                        if h >= 4:
                            dve.wait_ge(s_band, h // 4)
                        dve.tensor_tensor(w3a["bandedT"][:, h % 4, :].rearrange("p (i n) -> p i n", i=NTT),
                                          bank_a[0:BAND, :].rearrange("p (i n) -> p i n", i=NTT),
                                          w3b["w3_ma"].unsqueeze(1).to_broadcast([BAND, NTT, 128]), ALU.mult
                                          ).then_inc(s_amasked, 1)
                    g = self.at(tau, 13)
                    if g is not None:
                        dve.wait_ge(s_numer, g + 1)
                        self.R.wait_emptied(dve, f"R{g}")
                        if g >= 2:
                            dve.wait_ge(s["projected"], g - 1)
                        dve.tensor_tensor(ctx_n[:, g % 2, :], bank_v[:, :], sums_sb, ALU.mult).then_inc(s_normal, 1)

            def pool(self, pool):
                s = self.s
                for tau in range(self.steps):
                    h, r = divmod(tau - 4, NTT)
                    if r == 0 and 0 <= h < HEADS:
                        for k in range(4 * h, 4 * h + 4):
                            pool.wait_ge(s_written[k % 3], 16 * (k // 3 + 1))
                        if h >= 2:
                            pool.wait_ge(s_aturned, h - 1)
                        src = bass.AP(skewed, (h % 2) * NTT * A_SLOT + 1,
                                      [[A_ROW + 1, 128], [A_SLOT, NTT], [1, BAND]])
                        pool.dma_start(w3a["banded"][:, h % 2, :, 0:BAND], src).then_inc(s_askew[h % 2], 16)
                    g = self.at(tau, 9)
                    if g is not None:
                        pool.wait_ge(s["craw"], g + 1)
                        if g >= 1:
                            pool.wait_ge(s_numer, g)
                        for n in range(2):
                            pool.tensor_tensor(w3b[f"masked{n}"], ctx_raw[:, :], w3b[f"w3_m{n}"], ALU.mult
                                               ).then_inc(s_bmasked, 1)

            def sync(self, sp):
                s = self.s

                def load_near(h):
                    for c in range(4):
                        src = bass.AP(offset_scores, 32 * c * E_ROW + h * BAND + 31,
                                      [[E_ROW - 1, 32], [128 * E_ROW, NTT], [1, WIN]])
                        sp.dma_start(near[32 * c:32 * c + 32, h % 2], src).then_inc(s_near[h % 2], 16)

                load_near(0)
                load_near(1)
                for k in range(self.nt):
                    h, i = divmod(k, NTT)
                    if h >= 2 and i == 0:
                        sp.wait_ge(s_aturned, h - 1)
                    sp.wait_ge(s["exped"], k + 1)
                    lo, hi = max(0, i * 128 - 32), min(S, i * 128 + 160)
                    dst = bass.AP(skewed, ((h % 2) * NTT + i) * A_SLOT + 32 + lo - (i * 128 - 32),
                                  [[A_ROW, 128], [1, hi - lo]])
                    sp.dma_start(dst, prob[:, k % 3, lo:hi]).then_inc(s_written[k % 3], 16)
                    if i == NTT - 1 and h + 2 < HEADS:
                        sp.wait_ge(s["scored"], k + 1)
                        load_near(h + 2)

        def layer3_tensor(pe):
            wait_weights(pe, "w3", N_W3)
            pe.wait_ge(kept["v3_set"], 17)
            with iterations(pe, 3) as b:
                A, F = L3A(), L3F()
                turn_xn(pe, A)
                A.wait_emptied(pe, "X")
                token_products(pe, A, "LG", w3b["w3_rt"], 8)
                project(pe, A, "Q", w3b["w3_lin"][:, 0, :], xnT[:, :])
                project(pe, A, "K", w3b["w3_lin"][:, 1, :], xnT[:, :])
                token_products(pe, A, "V", w3b["w3_lin"][:, 2, :], D)
                pe.wait_ge(s_qkept, 1)
                for j in range(L3E):
                    t, q = divmod(j, 4)
                    project(pe, A, f"E{j}", q_kept[:, t * 128:(t + 1) * 128],
                            w3a["w3_rk"][:, q * 4 * BAND:(q + 1) * 4 * BAND], n=4 * BAND)

                def down(e):
                    F.wait_free(pe, f"Y{e}")
                    F.wait_emptied(pe, f"U{e}1")
                    for t in range(NTT):
                        for i in range(2):
                            last = pe.matmul(F.bank(f"Y{e}")[:, t * 128:(t + 1) * 128],
                                             hid3[:, e % 2, i, t * 128:(t + 1) * 128], w3b["w3_down"][:, e, i * D:(i + 1) * D],
                                             start=(i == 0), stop=(i == 1))
                    last.then_inc(F.filled, 1)

                for e in range(L3_EXPERTS):
                    for i in range(2):
                        project(pe, F, f"G{e}{i}", w3b["w3_gate"][:, e, i * 128:(i + 1) * 128], xnT[:, :])
                        project(pe, F, f"U{e}{i}", w3b["w3_up"][:, e, i * 128:(i + 1) * 128], xnT[:, :])
                    if e:
                        down(e - 1)
                down(L3_EXPERTS - 1)
                F.wait_all_free(pe)
                A.wait_all_free(pe)
                for i in range(2):
                    pe.wait_ge(s_stacked[i], 2 * N_FETCH)
                OffsetAttention(b).pe(pe)
                meet(pe, kept["go3"], b)

        def layer3_scalar(act):
            wait_weights(act, "w3", N_W3)
            act.wait_ge(kept["v3_set"], 17)
            with iterations(act, 3) as b:
                A, F = L3A(), L3F()
                evac(act, A, "X", xnT[:, :])
                A.wait_filled(act, "Q")
                act.activation(q_kept, A.bank("Q")[:, :], ACT.Copy, scale=DH ** -0.5).then_inc(s_qkept, 1)
                evac(act, A, "Q", whole3[0][:, 0:S], scale=DH ** -0.5)
                A.wait_filled(act, "V")
                act.activation(v_pad[:, :, :, 0:DH], A.bank("V")[:, :].rearrange("p (t h d) -> p t h d", t=NTT, h=HEADS),
                               ACT.Copy).then_inc(a_act, 1)
                A.wait_emptied(act, "Q")
                A.wait_emptied(act, "K")
                Split(0, whole3[0], parts3[0]).act(act)
                act.wait_ge(s_rest, 2)
                Split(1, whole3[1], parts3[1]).act(act)
                for j in range(1, L3E, 2):
                    if j >= 2:
                        act.wait_ge(s_esent[j % 2], b * SENT + 16 * (j // 2))
                    evac(act, A, f"E{j}", ctx_n[:, j % 2, 0:4 * BAND], A.bank(f"E{j}")[:, 0:4 * BAND])
                for n in range(2 * L3_EXPERTS):
                    name = f"G{n // 2}{n % 2}"
                    F.wait_filled(act, name)
                    if n >= 2:
                        F.wait_emptied(act, f"G{(n - 2) // 2}{n % 2}")
                    act.activation(tanh3[:, n % 2], F.bank(name)[:, :], ACT.Tanh, scale=0.5).then_inc(s_tanh, 1)
                silu_tanh(act, L3_EXPERTS - 1)
                act.wait_ge(s_sent, 32)
                OffsetAttention(b).act(act)
                meet(act, kept["go3"], b)

        def layer3_vector(dve):
            wait_weights(dve, "w3", N_W3)
            with iterations(dve, 3) as b:
                A, F, M = L3A(), L3F(), OffsetAttention(b)
                d = Steps(dve, s_dve)
                layer_norm(dve, b, d)
                evac(dve, A, "LG", lg[:, :, 0:8], A.bank("LG")[:, 0:NTT * 8].rearrange("p (t e) -> p t e", t=NTT))
                A.wait_emptied(dve, "LG")
                d.add(dve.memset(gate[:, :, 8:9], 1.0))
                top_k(dve, d, lg[:, :, 0:8], NTT, 8, 1, gate[:, :, 0:8], prob_f[:, 0:256], prob_f[:, 256:512])
                A.wait_filled(dve, "K")
                dve.tensor_copy(whole3[0][:, S:2 * S], A.bank("K")[:, :])
                dve.tensor_scalar(whole3[1][:, 0:S], A.bank("K")[:, :], w3b["w3_relk"][:, 0:1], None, ALU.add)
                dve.tensor_scalar(whole3[1][:, S:2 * S], A.bank("K")[:, :], w3b["w3_relk"][:, 1:2], None, ALU.add
                                  ).then_inc(a_dve, 1)
                A.wait_emptied(dve, "K")
                A.wait_emptied(dve, "Q")
                Split(0, whole3[0], parts3[0]).dve(dve)
                Split(1, whole3[1], parts3[1]).dve(dve)
                for j in range(0, L3E, 2):
                    if j >= 2:
                        dve.wait_ge(s_esent[j % 2], b * SENT + 16 * (j // 2))
                    evac(dve, A, f"E{j}", ctx_n[:, j % 2, 0:4 * BAND], A.bank(f"E{j}")[:, 0:4 * BAND])
                for e in range(L3_EXPERTS):
                    for i in range(2):
                        n = 2 * e + i
                        dve.wait_ge(s_tanh, n + 1)
                        if n >= 2:
                            F.wait_emptied(dve, f"U{(n - 2) // 2}{n % 2}")
                        dve.scalar_tensor_tensor(gate3[:, n % 2], tanh3[:, n % 2], 1.0, F.bank(f"G{e}{i}")[:, :],
                                                 ALU.add, ALU.mult).then_inc(f_dve, 1)
                        F.wait_filled(dve, f"U{e}{i}")
                        F.wait_emptied(dve, f"G{e}{i}")
                        if e >= 2:
                            F.wait_filled(dve, f"Y{e - 2}")
                        dve.scalar_tensor_tensor(hid3[:, e % 2, i], gate3[:, n % 2], 0.5, F.bank(f"U{e}{i}")[:, :],
                                                 ALU.mult, ALU.mult).then_inc(f_dve, 1)
                    if e:
                        gated(dve, F, e - 1, first=1)
                gated(dve, F, L3_EXPERTS - 1, first=1)
                silu(dve, d)
                dve.wait_ge(s_sent, 32)
                M.dve(dve)
                dve.wait_ge(M.s["projected"], 4)
                residual(dve, d, b, bank3(bank_o))
                meet(dve, kept["go3"], b)

        def layer3_gpsimd(pool):
            flat_v = v_pad[:, :, :, :].rearrange("p a b c -> p (a b c)")
            pool.memset(flat_v, 0.0).then_inc(kept["v3_set"], 1)
            pool.wait_ge(kept["v3_set"], 1)
            zeros = 2 * NTT * A_SLOT // 128
            pool.dma_start(bass.AP(skewed, 0, [[zeros, 128], [1, zeros]]), flat_v[:, 0:zeros]
                           ).then_inc(kept["zeroed"], 16)
            pool.wait_ge(kept["zeroed"], 16)
            for j in range(NTT):
                for a in range(4):
                    u = DH + 4 * j + a
                    pool.memset(v_pad[32 * a:32 * a + 32, j, :, u:u + 1], 1.0).then_inc(kept["v3_set"], 1)
            pool.wait_ge(kept["v3_set"], 17)
            with iterations(pool, 3) as b:
                A, F = L3A(), L3F()
                inverse_deviation(pool)
                for j in range(L3E):
                    t, q = divmod(j, 4)
                    A.wait_emptied(pool, f"E{j}")
                    dst = bass.AP(offset_scores, t * 128 * E_ROW + q * 4 * BAND, [[E_ROW, 128], [1, 4 * BAND]])
                    pool.dma_start(dst, ctx_n[:, j % 2, 0:4 * BAND]).then_inc(s_esent[j % 2], 16)
                add_up(pool, F, range(1, L3_EXPERTS), "Y0")
                for i in range(2):
                    pool.wait_ge(s_esent[i], b * SENT + SENT)
                pool.sem_inc(s_offsets, 1)
                OffsetAttention(b).pool(pool)
                meet_and_clear(pool, kept["go3"], b)

        def layer3_sync(sp):
            load_weights(sp, spec3a, w3a, kept["w3"])
            sp.wait_ge(kept["zeroed"], 16)
            with iterations(sp, 3) as b:
                for i in range(2):
                    send_parts(sp, 2 + i, parts3[i].rearrange("p a (q s) -> p (a q) s", q=2), s_rest, 2 * i + 2, s_sent)
                    sp.wait_ge(s_sent, 16 * (i + 1))
                    fetch_stack(sp, 2 + i, 0, 2 * i, i == 0, s_stacked[i])
                    fetch_stack(sp, 2 + i, 1, 2 * i + 1, False, s_stacked[i])
                sp.wait_ge(s_offsets, 1)
                sp.wait_ge(s_silu, 1)
                OffsetAttention(b).sync(sp)
                meet_sync(sp, kept["go3"], b)

        def output_sync(sp):
            sp.dma_start(out.rearrange("b (t p) d -> p (b t) d", p=128),
                         x_all[:, :, :, :].rearrange("p b t d -> p (b t) d")).then_inc(kept["stored"], 16)
            sp.wait_ge(kept["stored"], 16)

        @block.sync
        def _(sp):
            loads_sync(sp)
            layer2_sync(sp)
            layer3_sync(sp)
            output_sync(sp)

        @block.tensor
        def _(pe):
            layer0_tensor(pe)
            layer1_tensor(pe)
            layer2_tensor(pe)
            layer3_tensor(pe)

        @block.vector
        def _(dve):
            layer0_vector(dve)
            layer1_vector(dve)
            layer2_vector(dve)
            layer3_vector(dve)

        @block.scalar
        def _(act):
            layer0_scalar(act)
            layer1_scalar(act)
            layer2_scalar(act)
            layer3_scalar(act)

        @block.gpsimd
        def _(pool):
            layer0_gpsimd(pool)
            layer1_gpsimd(pool)
            layer2_gpsimd(pool)
            layer3_gpsimd(pool)


def laid_out(i):
    a = {k: np.asarray(v) for k, v in i.items()}
    f = np.float32
    c = np.ascontiguousarray
    T = {"x": a["L0_attn_x"]}
    T["ident"] = np.eye(128, dtype=f)
    T["ones_row"] = np.ones((1, 128), f)
    T["causal"] = np.triu(np.full((128, 128), NEG, f), 1)
    T["tri"] = c(np.broadcast_to(np.tril(np.ones((15, 15), f), -1), (128, 15, 15)))
    T["w0_lin"] = c(np.stack([a["L0_attn_" + n].T for n in ("Wq", "Wk", "Wv", "Wa", "Wb")], 1))
    T["w0_g"] = a["L0_ffn_Wg"]
    T["w0_e"] = c(a["L0_ffn_We"].transpose(1, 0, 2))
    T["w0_be"] = a["L0_ffn_be"]
    T["w1_qkv"] = c(np.stack([a["L1_attn_" + n] for n in ("Wq", "Wk", "Wv")], 1))
    T["w1_o"] = c(a["L1_attn_Wo"].reshape(8, 128, 128).transpose(1, 0, 2))
    T["w1_bo"] = a["L1_attn_bo"][None]
    T["w1_r"] = a["L1_ffn_router_W"]
    T["w1_rb"] = a["L1_ffn_router_b"][None]
    T["w1_e1"] = c(np.concatenate([a["L1_ffn_eW1"], a["L1_ffn_sW1"][None]]).transpose(1, 0, 2))
    T["w1_eb1"] = c(np.concatenate([a["L1_ffn_eb1"], a["L1_ffn_sb1"][None]]).T)
    T["w1_e2"] = c(np.concatenate([a["L1_ffn_eW2"], a["L1_ffn_sW2"][None]]).transpose(1, 0, 2))
    T["w1_eb2"] = c(np.concatenate([a["L1_ffn_eb2"], a["L1_ffn_sb2"][None]]))

    def padded_out(wo, bo):
        p = np.zeros((4, GROW, 4, 128), f)
        p[:, 0:DH] = wo.reshape(4, 4, DH, 128).transpose(1, 2, 0, 3)
        p[0, DH, 0] = bo
        return p.reshape(128, 4, 128)

    T["w2_qk"] = c(np.concatenate([a["L2_attn_Wq"].T, a["L2_attn_Wk"].T], 1))
    T["w2_v"] = c(a["L2_attn_Wv"].T)
    T["w2_ln"] = c(np.broadcast_to(np.stack([a["L2_attn_" + n] for n in ("qln_g", "kln_g", "qln_b", "kln_b")]),
                                   (128, 4, DH)))
    T["w2_o"] = padded_out(a["L2_attn_Wo"].T, a["L2_attn_bo"])
    T["w2_fe"] = c(np.concatenate([a["L2_ffn_W" + n] for n in "qkv"], 2).transpose(1, 0, 2))
    T["w2_fb"] = c(np.stack([a["L2_ffn_b" + n].T for n in "qk"], 1))
    T["w2_fbv"] = a["L2_ffn_bv"]
    T["w2_g1"] = a["L2_ffn_Wg1"]
    T["w2_b1"] = a["L2_ffn_bg1"][:, None]
    T["w2_g2"] = a["L2_ffn_Wg2"]
    T["w2_b2"] = c(np.broadcast_to(a["L2_ffn_bg2"], (128, 4)))
    T["w2_fo"] = padded_out(a["L2_ffn_Wo"], a["L2_ffn_bo"])

    T["w3_lin"] = c(np.stack([a["L3_attn_" + n].T for n in ("Wq", "Wk", "Wv")], 1))
    T["w3_o"] = padded_out(a["L3_attn_Wo"].T, a["L3_attn_b_o"])
    T["w3_rt"] = c(a["L3_ffn_router"].T)
    for n in ("up", "gate"):
        both = np.concatenate([a["L3_ffn_" + n], a[f"L3_ffn_w_{n}_s"][None]])
        T["w3_" + n] = c(both.transpose(2, 0, 1))
    down = np.concatenate([a["L3_ffn_down"], a["L3_ffn_w_down_s"][None]])
    T["w3_down"] = c(down.reshape(9, 128, 2, 128).transpose(3, 0, 2, 1).reshape(128, 9, 256))
    rk, rv = a["L3_attn_rel_k_emb"], a["L3_attn_rel_v_emb"]
    T["w3_relk"] = c(np.stack([np.tile(rk[0], HEADS), np.tile(rk[2 * MAX_REL], HEADS)], 1))
    clipped = np.clip(np.arange(BAND) - BAND // 2, -MAX_REL, MAX_REL) + MAX_REL
    off = np.zeros((HEADS, DH, HEADS, BAND), f)
    for h in range(HEADS):
        off[h, :, h, :] = rk[clipped].T
    T["w3_rk"] = off.reshape(128, HEADS * BAND)
    band = np.zeros((BAND, GROW), f)
    band[:, 0:DH] = rv[clipped]
    T["w3_rvb"] = band
    blocks = S // 32
    for n, row in ((0, 0), (1, 2 * MAX_REL)):
        m = np.zeros((4, GROW, 4, GROW), f)
        for g in range(4):
            m[g, DH:DH + blocks, g, 0:DH] = rv[row]
        T[f"w3_rv{n}"] = m.reshape(128, 128)
    u, blk = np.arange(blocks)[:, None], np.arange(S)[None] // 32
    for n, far in ((0, u < blk - 1), (1, u > blk + 1)):
        m = np.zeros((4, GROW, S), f)
        m[:, DH:DH + blocks] = far
        T[f"w3_m{n}"] = m.reshape(128, S)
    r, p = np.arange(BAND)[:, None] - BAND // 2, np.arange(128)[None] % 32
    T["w3_ma"] = ((r + p >= -32) & (r + p < 64)).astype(f)
    sel = np.zeros((4, GROW, 4, GROW), f)
    for g in range(4):
        sel[g, range(DH), g, range(DH)] = 1
        sel[g, DH:DH + blocks, g, DH] = 1
    T["w3_sel"] = sel.reshape(128, 128)
    return T


def kernel(**inputs):
    import concourse.bacc as bacc
    from concourse.bass_utils import run_bass_kernel_spmd

    arrays = laid_out(inputs)
    nc = bacc.Bacc("TRN2", target_bir_lowering=False, num_devices=1)
    T = {n: nc.dram_tensor(f"in_{n}", v.shape, mybir.dt.from_np(v.dtype), kind="ExternalInput").ap()
         for n, v in arrays.items()}
    out = nc.dram_tensor("out_x", (B, S, D), mybir.dt.float32, kind="ExternalOutput").ap()
    build(nc, T, out)
    r = run_bass_kernel_spmd(nc, [{f"in_{n}": v for n, v in arrays.items()}], core_ids=[0])
    return r.results[0]["out_x"]
```

```python
import concourse.bass as bass
from concourse import mybir
from contextlib import ExitStack
import numpy as np

B, S, D = 4, 512, 128
NTT = S // 128
EPS = 1e-5
L1_HEADS, L1_DH = 16, 64
HEADS, DH = 16, 8
L1_EXPERTS = 16
L0_EXPERTS = 8
L3_EXPERTS, L3_HID = 9, 256
MAX_REL = 32
BAND = 127
WIN = 96
A_ROW = 224
GROW = 32
NPARTS = 3
STACK = NPARTS * NPARTS * DH
NEG = -1e30


class Steps:

    def __init__(self, eng, sem):
        self.eng, self.sem, self.n = eng, sem, 0

    def add(self, ins):
        ins.then_inc(self.sem, 1)
        self.n += 1

    def settle(self):
        self.eng.wait_ge(self.sem, self.n)


class Jobs:

    def __init__(self, banks, filled, emptied, jobs):
        self.banks, self.filled, self.emptied = banks, filled, emptied
        self.names = [n for n, _ in jobs]
        self.engines = [e for _, e in jobs]

    def bank(self, name):
        return self.banks[self.names.index(name) % len(self.banks)]

    def n_filled(self, name):
        return self.names.index(name) + 1

    def n_emptied(self, j):
        return self.emptied[self.engines[j]], self.engines[:j + 1].count(self.engines[j])

    def wait_free(self, pe, name):
        j = self.names.index(name) - len(self.banks)
        if j >= 0:
            pe.wait_ge(*self.n_emptied(j))

    def wait_filled(self, eng, name):
        eng.wait_ge(self.filled, self.n_filled(name))

    def wait_emptied(self, eng, name):
        eng.wait_ge(*self.n_emptied(self.names.index(name)))

    def wait_all_free(self, pe):
        for e in sorted(set(self.engines)):
            pe.wait_ge(self.emptied[e], self.engines.count(e))


def build(nc, T, out):
    f32, bf16 = mybir.dt.float32, mybir.dt.bfloat16
    ALU, ACT, AX = mybir.AluOpType, mybir.ActivationFunctionType, mybir.AxisListType

    ctx = ExitStack()
    with ctx:
        def sb(name, shape, dt=f32):
            return ctx.enter_context(nc.sbuf_tensor(name, shape, dt))

        wa = sb("wa", [128, 5632])
        wb = sb("wb", [128, 10624])
        x_all = sb("x_all", [128, B, NTT, D])
        ident = sb("ident", [128, 128])
        ident_b = sb("ident_b", [128, 128], bf16)
        ones_row = sb("ones_row", [1, 128])
        causal_f = sb("causal_f", [128, 128])
        causal_b = sb("causal_b", [128, 128], bf16)
        tri = sb("tri", [128, 15, 15])
        arena = sb("arena", [128, 32768], bf16)
        arena_f = arena[:, :].bitcast(f32)
        pt = sb("pt", [128, 4, NTT, S])
        pt_f = pt[:, :, :, :].rearrange("p a b c -> p (a b c)")
        prob = sb("prob", [128, 3, S])
        prob_f = prob[:, :, :].rearrange("p a b -> p (a b)")
        xn = sb("xn", [128, NTT, D])
        xnT = sb("xnT", [128, S])
        acc = sb("acc", [128, NTT, D])
        acc_f = acc[:, :, :].rearrange("p t d -> p (t d)")
        tmp = sb("tmp", [128, 2, NTT, D])
        ctx_raw = sb("ctx_raw", [128, S])
        ctx_n = sb("ctx_n", [128, 2, S])
        v_pad = sb("v_pad", [128, NTT, HEADS, GROW])
        negmax = sb("negmax", [128, 64])
        rowsum = sb("rowsum", [128, 64])
        ln_st = sb("ln_st", [128, NTT, 6])
        ln_mv = sb("ln_mv", [128, NTT, 2])
        ln_rs = sb("ln_rs", [128, NTT])
        minus_half = sb("minus_half", [128, 1])
        lg = sb("lg", [128, NTT, 16])
        ex = sb("ex", [128, NTT, 16])
        gate = sb("gate", [128, NTT, 16])
        rank = sb("rank", [128, NTT, 16])
        red = sb("red", [128, NTT])
        small = sb("small", [128, 64])

        def ps(name):
            return ctx.enter_context(nc.psum_tensor(name, [128, 512], f32))

        bank_s = [ps(f"bank_s{i}") for i in range(3)]
        bank_t = [ps(f"bank_t{i}") for i in range(2)]
        bank_v = ps("bank_v")
        bank_m = [ps(f"bank_m{i}") for i in range(2)]
        bank_o = bank_m[1]
        score_banks = bank_s + bank_m[0:1]

        kept = {}
        for n in ("loaded", "w0", "w1", "w2", "w3", "consts", "stored", "go0", "go1", "go2", "go3",
                  "causal_set", "q1_zeroed", "stack_zeroed", "keys_zeroed", "centred", "v_set", "zeroed", "half_set", "first_stats", "first_var", "first_step", "first_rstd", "first_xn", "v3_set"):
            kept[n] = ctx.enter_context(nc.semaphore(n))
        s_esent = [ctx.enter_context(nc.semaphore(f"s_esent{i}")) for i in range(2)]
        s_askew = [ctx.enter_context(nc.semaphore(f"s_askew{i}")) for i in range(2)]
        SENT, SKEWED = 16 * 4 * NTT // 2, 16 * HEADS // 2
        cleared = {}

        def sem(name):
            cleared[name] = ctx.enter_context(nc.semaphore(name))
            return cleared[name]

        fin, s_resumed = sem("fin"), sem("s_resumed")
        s_dve, s_act, s_pool = sem("s_dve"), sem("s_act"), sem("s_pool")
        s_var, s_rstd, s_xn = sem("s_var"), sem("s_rstd"), sem("s_xn")
        a_fill, a_act, a_dve = sem("a_fill"), sem("a_act"), sem("a_dve")
        f_fill, f_act, f_dve = sem("f_fill"), sem("f_act"), sem("f_dve")
        r_fill, r_dve = sem("r_fill"), sem("r_dve")
        r2_fill, r2_dve = sem("r2_fill"), sem("r2_dve")
        s_gate, s_lgsub, s_exp, s_acc, s_silu, s_e1 = (sem(n) for n in
                                                      ("s_gate", "s_lgsub", "s_exp", "s_acc", "s_silu", "s_e1"))
        att = {}
        for i in range(2):
            att[i] = {n: sem(f"{n}_{i}") for n in ("scored", "maxed", "exped", "turned", "ev_dve", "ev_act",
                                                   "pv", "craw", "inverted", "projected")}
        s_final = sem("s_final")
        s_round, s_rest, s_sent, s_pooled, s_mixed, s_squared, s_normed, s_hvar, s_hrstd, s_again, s_taken = (sem(n) for n in (
            "s_round", "s_rest", "s_sent", "s_pooled", "s_mixed", "s_squared", "s_normed", "s_hvar", "s_hrstd", "s_again", "s_taken"))
        (s_qkept, s_offsets, s_tanh, s_aturned, s_amasked, s_band, s_bmasked, s_numer, s_normal, r_act) = (
            sem(n) for n in ("s_qkept", "s_offsets", "s_tanh", "s_aturned", "s_amasked", "s_band", "s_bmasked",
                             "s_numer", "s_normal", "r_act"))
        s_near = [sem(f"s_near{i}") for i in range(2)]
        s_written = [sem(f"s_written{i}") for i in range(3)]
        s_stacked = [sem(f"s_stacked{i}") for i in range(2)]
        nums = [s.num for s in cleared.values()]
        assert nums == list(range(nums[0], nums[0] + len(nums)))
        clear_range = range(nums[0], nums[-1] + 1)

        block = ctx.enter_context(nc.Block())

        def iterations(eng, go):
            return eng.Fori(0, B)

        def meet(eng, go, b):
            eng.drain().then_inc(fin, 1)
            eng.wait_ge(go, b + 1)

        def meet_sync(sp, go, b):
            meet(sp, go, b)
            sp.sem_inc(s_resumed, 1)
            sp.wait_ge(s_resumed, 1)

        def meet_and_clear(pool, go, b, others=4):
            pool.drain()
            pool.wait_ge(fin, others)
            pool.sem_clear(clear_range)
            pool.drain().then_inc(go, 1)
            pool.wait_ge(go, b + 1)

        def x_of(b):
            return x_all[:, bass.ds(b, 1), :, :].rearrange("p b t d -> p (b t) d")

        def flat(t3):
            return t3.rearrange("p t d -> p (t d)")

        def bank3(bank):
            return bank[:, :].rearrange("p (t d) -> p t d", t=NTT)

        def norm_stats(dve, b, settle, var):
            x = x_of(b)
            for t in range(NTT):
                ins = dve.bn_stats(ln_st[:, t, :], x[:, t, :])
                settle.add(ins)
            settle.settle()
            for t in range(NTT):
                dve.bn_aggr(ln_mv[:, t, :], ln_st[:, t, :]).then_inc(var, 1)
            dve.wait_ge(var, NTT)

        def norm_apply(dve, b, rstd, done):
            x = x_of(b)
            dve.wait_ge(rstd, 1)
            for t in range(NTT):
                dve.tensor_scalar(xn[:, t, :], x[:, t, :], ln_mv[:, t, 0:1], ln_rs[:, t:t + 1],
                                  ALU.subtract, ALU.mult).then_inc(done, 1)

        def inverse_deviation(pool, var, step, rstd):
            pool.wait_ge(var, NTT)
            pool.tensor_scalar(ln_rs[:, :], ln_mv[:, :, 1], EPS, None, ALU.add).then_inc(step, 1)
            pool.wait_ge(step, 1)
            pool.tensor_tensor(ln_rs[:, :], ln_rs[:, :], minus_half[:, 0:1].to_broadcast([128, NTT]), ALU.pow
                               ).then_inc(rstd, 1)

        def after(b):
            return (b + 1) % B

        class NextNorm:

            def __init__(self, dve, b, d):
                self.dve, self.b, self.d = dve, b, d

            def stats(self):
                norm_stats(self.dve, after(self.b), self.d, s_var)

            def apply(self):
                norm_apply(self.dve, after(self.b), s_rstd, s_xn)

        def turn_xn(pe, A):
            for t in range(NTT):
                last = pe.transpose(A.bank("X")[:, t * 128:(t + 1) * 128], xn[:, t, :], ident[:, :])
            last.then_inc(A.filled, 1)

        def evac(eng, A, name, dst, src=None, scale=None):
            A.wait_filled(eng, name)
            src = A.bank(name)[:, :] if src is None else src
            if eng is nc.scalar or A.engines[A.names.index(name)] == "act":
                ins = nc.scalar.activation(dst, src, ACT.Copy, scale=1.0 if scale is None else scale)
            elif scale is None:
                ins = nc.vector.tensor_copy(dst, src)
            else:
                ins = nc.vector.tensor_scalar(dst, src, scale, None, ALU.mult)
            ins.then_inc(A.emptied[A.engines[A.names.index(name)]], 1)

        def project(pe, A, name, w, rhs, n=S):
            A.wait_free(pe, name)
            pe.matmul(A.bank(name)[:, 0:n], w, rhs, start=True, stop=True).then_inc(A.filled, 1)

        def token_products(pe, A, name, rhs, width, lhs=None, bias=None):
            A.wait_free(pe, name)
            lhs = xnT if lhs is None else lhs
            for t in range(NTT):
                o = A.bank(name)[:, t * width:(t + 1) * width]
                last = pe.matmul(o, lhs[:, t * 128:(t + 1) * 128], rhs, start=True, stop=bias is None)
                if bias is not None:
                    last = pe.matmul(o, ones_row[0:1, :], bias, start=False, stop=True)
            last.then_inc(A.filled, 1)

        def top_k(dve, d, logits, T_, E, k, mask, cmp_a, cmp_b):
            mine = logits.unsqueeze(3).to_broadcast([128, T_, E, E])
            other = logits.unsqueeze(2).to_broadcast([128, T_, E, E])
            ca = cmp_a.rearrange("p (t e f) -> p t e f", t=T_, e=E)
            cb = cmp_b.rearrange("p (t e f) -> p t e f", t=T_, e=E)
            d.add(dve.tensor_tensor(ca, other, mine, ALU.is_gt))
            d.add(dve.tensor_tensor(cb, other, mine, ALU.is_ge))
            d.settle()
            for t in range(T_):
                d.add(dve.tensor_tensor(cb[:, t], cb[:, t], tri[:, 0:E, 0:E], ALU.mult))
            d.settle()
            d.add(dve.tensor_tensor(ca, ca, cb, ALU.max))
            d.settle()
            d.add(dve.tensor_reduce(rank[:, 0:T_, 0:E], ca, AX.X, ALU.add))
            d.settle()
            d.add(dve.tensor_scalar(mask, rank[:, 0:T_, 0:E], float(k) - 0.5, None, ALU.is_lt))

        def shifted(dve, d, logits, T_, E):
            d.add(dve.tensor_reduce(red[:, 0:T_], logits, AX.X, ALU.max))
            d.settle()
            dve.tensor_tensor(ex[:, 0:T_, 0:E], logits, red[:, 0:T_].unsqueeze(2).to_broadcast([128, T_, E]),
                              ALU.subtract).then_inc(s_lgsub, 1)

        def exp_logits(act, T_, E):
            act.wait_ge(s_lgsub, 1)
            act.activation(ex[:, 0:T_, 0:E], ex[:, 0:T_, 0:E], ACT.Exp).then_inc(s_exp, 1)

        def gates(dve, d, T_, E, of_all):
            d.settle()
            dve.wait_ge(s_exp, 1)
            d.add(dve.tensor_tensor(gate[:, 0:T_, 0:E], ex[:, 0:T_, 0:E], gate[:, 0:T_, 0:E], ALU.mult))
            d.settle()
            d.add(dve.tensor_reduce(red[:, 0:T_], (ex if of_all else gate)[:, 0:T_, 0:E], AX.X, ALU.add))
            d.settle()
            d.add(dve.reciprocal(red[:, 0:T_], red[:, 0:T_]))
            d.settle()
            dve.tensor_tensor(gate[:, 0:T_, 0:E], gate[:, 0:T_, 0:E],
                              red[:, 0:T_].unsqueeze(2).to_broadcast([128, T_, E]), ALU.mult).then_inc(s_gate, 1)

        def gated(dve, F, e, first=0):
            F.wait_filled(dve, f"Y{e}")
            if e - 1 - first > 0:
                dve.wait_ge(s_acc, e - 1 - first)
            dst = acc[:, :, :] if e < first else tmp[:, e % 2]
            dve.tensor_tensor(dst, bank3(F.bank(f"Y{e}")), gate[:, :, e:e + 1].to_broadcast([128, NTT, D]),
                              ALU.mult).then_inc(F.emptied["dve"], 1)

        def add_up(pool, F, es, base):
            for e in es:
                i = e - (1 if base == "Y0" else 0)
                F.wait_emptied(pool, f"Y{e}")
                if i:
                    pool.wait_ge(s_acc, i)
                elif base is not None:
                    F.wait_emptied(pool, base)
                pool.tensor_tensor(acc[:, :, :], acc[:, :, :], tmp[:, e % 2], ALU.add).then_inc(s_acc, 1)

        def silu_tanh(act, n):
            act.wait_ge(s_acc, n)
            act.activation(flat(tmp[:, 0]), acc_f, ACT.Tanh, scale=0.5).then_inc(s_e1, 1)

        def silu(dve, d):
            dve.wait_ge(s_e1, 1)
            dve.scalar_tensor_tensor(acc_f, flat(tmp[:, 0]), 1.0, acc_f, ALU.add, ALU.mult).then_inc(s_silu, 1)
            dve.wait_ge(s_silu, 1)

        def residual(dve, d, b, src):
            d.add(dve.scalar_tensor_tensor(tmp[:, 1], src, 0.5, acc[:, :, :], ALU.mult, ALU.mult))
            d.settle()
            x = x_of(b)
            dve.tensor_tensor(x, x, tmp[:, 1], ALU.add).then_inc(s_final, 1)

        class Attention:

            LAG = 3

            def __init__(self, which, per_group, R, scores, pv, wo, blocks=lambda k: NTT, heads=HEADS,
                         unit=None, n_scores=4, by_rows=False, pt_free=None):
                self.s = att[which]
                self.pt_free = pt_free
                self.banks = score_banks[0:n_scores]
                self.unit = unit or per_group * NTT
                self.by_rows = by_rows
                self.heads, self.per_group, self.R = heads, per_group, R
                self.scores, self.pv_products, self.wo, self.blocks = scores, pv, wo, blocks
                self.nt = heads * NTT
                self.groups = heads // per_group
                self.per = per_group * NTT
                self.units = self.per // self.unit
                self.steps = self.nt + 12

            def wait_copied(self, eng, k):
                eng.wait_ge(self.s["ev_dve" if k % 2 == 0 else "ev_act"], k // 2 + 1)

            def at(self, tau, after):
                g, r = divmod(tau - after - self.LAG - (self.per - 1), self.per)
                return g if r == 0 and 0 <= g < self.groups else None

            def unit_at(self, tau, after):
                u, r = divmod(tau - after - self.LAG - (self.unit - 1), self.unit)
                return u if r == 0 and 0 <= u < self.nt // self.unit else None

            def number(self, g, m, i):
                return g * self.per + (i * self.per_group + m if self.by_rows else m * NTT + i)

            def copy_tile(self, eng, k):
                h, i = divmod(k, NTT)
                n = self.blocks(k)
                if k < 2 and self.pt_free is not None:
                    eng.wait_ge(*self.pt_free)
                eng.wait_ge(self.s["turned"], k + 1)
                if h >= 4:
                    eng.wait_ge(self.s["pv"], (k - 4 * NTT) // self.unit + 1)
                dst = pt[:, h % 4, 0:n, i * 128:(i + 1) * 128]
                src = bank_t[k % 2][:, 0:n * 128].rearrange("p (j i) -> p j i", j=n)
                if k % 2 == 0:
                    nc.vector.tensor_copy(dst, src).then_inc(self.s["ev_dve"], 1)
                else:
                    nc.scalar.activation(dst, src, ACT.Copy).then_inc(self.s["ev_act"], 1)

            def spread_sums(self, pe, g, bank):
                rows = 128 // self.per_group
                for i in range(NTT):
                    for m in range(self.per_group):
                        k = self.number(g, m, i)
                        last = pe.matmul(bank[rows * m:rows * m + rows, i * 128:(i + 1) * 128],
                                         rowsum[:, k:k + 1].to_broadcast([128, rows]), ident[:, :],
                                         start=True, stop=True, skip_group_check=True)
                return last

            def pe(self, pe):
                s = self.s
                for tau in range(self.steps):
                    if tau < self.nt:
                        n = len(self.banks)
                        if tau >= n:
                            pe.wait_ge(s["exped"], tau - n + 1)
                        self.scores(pe, tau, self.banks[tau % len(self.banks)]).then_inc(s["scored"], 1)
                    k = tau - self.LAG
                    if 0 <= k < self.nt:
                        pe.wait_ge(s["exped"], k + 1)
                        if k >= 2:
                            self.wait_copied(pe, k - 2)
                        for j in range(self.blocks(k)):
                            last = pe.transpose(bank_t[k % 2][:, j * 128:(j + 1) * 128],
                                                prob[:, k % 3, j * 128:(j + 1) * 128], ident[:, :])
                        last.then_inc(s["turned"], 1)
                    u = self.unit_at(tau, 2)
                    if u is not None:
                        self.wait_copied(pe, self.unit * (u + 1) - 1)
                        self.wait_copied(pe, self.unit * (u + 1) - 2)
                        g = u // self.units
                        if g >= len(self.R.banks):
                            self.R.wait_emptied(pe, f"R{g - len(self.R.banks)}")
                        self.pv_products(pe, u).then_inc(s["pv"], 1)
                    g = self.at(tau, 5)
                    if g is not None:
                        pe.wait_ge(s["inverted"], g + 1)
                        pe.wait_ge(s["craw"], g + 1)
                        self.spread_sums(pe, g, self.R.bank(f"R{g}")).then_inc(self.R.filled, 1)
                    g = self.at(tau, 8)
                    if g is not None:
                        self.R.wait_emptied(pe, f"R{g}")
                        for t in range(NTT):
                            last = pe.matmul(bank_o[:, t * 128:(t + 1) * 128], ctx_n[:, g % 2, t * 128:(t + 1) * 128],
                                             self.wo[:, g, :], start=(g == 0 and t == 0), stop=(g == self.groups - 1),
                                             skip_group_check=True)
                        last.then_inc(s["projected"], 1)

            def act(self, act):
                s = self.s
                for tau in range(self.steps):
                    k = tau - self.LAG
                    if 0 <= k < self.nt and k % 2 == 1:
                        self.copy_tile(act, k)
                    if tau < self.nt:
                        act.wait_ge(s["maxed"], tau + 1)
                        if tau >= 3:
                            act.wait_ge(s["turned"], tau - 2)
                        n = self.blocks(tau) * 128
                        act.activation(prob[:, tau % 3, 0:n], self.banks[tau % len(self.banks)][:, 0:n], ACT.Exp,
                                       bias=negmax[:, tau:tau + 1], accum_out=rowsum[:, tau:tau + 1]
                                       ).then_inc(s["exped"], 1)
                    g = self.at(tau, 3)
                    if g is not None:
                        act.wait_ge(s["pv"], (g + 1) * self.units)
                        if g >= 1:
                            self.R.wait_emptied(act, f"R{g - 1}")
                        act.activation(ctx_raw[:, :], self.R.bank(f"R{g}")[:, :], ACT.Copy).then_inc(s["craw"], 1)

            def dve(self, dve, norm=None):
                s = self.s
                for tau in range(self.steps):
                    if norm and tau == self.nt + 1:
                        norm.stats()
                    if norm and tau == self.nt + 5:
                        norm.apply()
                    if tau < self.nt:
                        dve.wait_ge(s["scored"], tau + 1)
                        n = self.blocks(tau) * 128
                        dve.tensor_reduce(negmax[:, tau:tau + 1], self.banks[tau % len(self.banks)][:, 0:n], AX.X, ALU.max,
                                          negate=True).then_inc(s["maxed"], 1)
                    k = tau - self.LAG
                    if 0 <= k < self.nt and k % 2 == 0:
                        self.copy_tile(dve, k)
                    g = self.at(tau, 3)
                    if g is not None:
                        cols = rowsum[:, g * self.per:(g + 1) * self.per]
                        dve.wait_ge(s["exped"], (g + 1) * self.per)
                        dve.reciprocal(cols, cols).then_inc(s["inverted"], 1)
                    g = self.at(tau, 6)
                    if g is not None:
                        dve.wait_ge(s["craw"], g + 1)
                        self.R.wait_filled(dve, f"R{g}")
                        if g >= 2:
                            dve.wait_ge(s["projected"], g - 1)
                        dve.tensor_tensor(ctx_n[:, g % 2, :], ctx_raw[:, :], self.R.bank(f"R{g}")[:, :],
                                          ALU.mult).then_inc(self.R.emptied["dve"], 1)

        def carve(base, spec):
            at, views = 0, {}
            for name, shape in spec:
                n = int(np.prod(shape[1:]))
                v = base[0:shape[0], at:at + n]
                if len(shape) == 3:
                    v = v.rearrange("p (a b) -> p a b", a=shape[1])
                elif len(shape) == 4:
                    v = v.rearrange("p (a b c) -> p a b c", a=shape[1], b=shape[2])
                views[name] = v
                at += n
            assert at <= base.shape[1], (at, base.shape)
            return views

        spec0 = [(n, T[n].shape) for n in ("w0_lin", "w0_g", "w0_e", "w0_be")]
        spec2 = [(n, T[n].shape) for n in ("w2_qk", "w2_v", "w2_ln", "w2_o", "w2_fe", "w2_fb", "w2_fbv", "w2_g1",
                                           "w2_b1", "w2_g2", "w2_b2", "w2_fo")]
        spec1 = [(n, T[n].shape) for n in ("w1_qkv", "w1_o", "w1_bo", "w1_r", "w1_rb", "w1_e1", "w1_eb1", "w1_e2",
                                           "w1_eb2")]
        w_a = carve(wa, spec0 + spec2)
        w_b = carve(wb, spec1)
        w = {**w_a, **w_b}
        W3B = ("w3_lin", "w3_o", "w3_up", "w3_gate", "w3_down", "w3_rt", "w3_relk", "w3_rv0", "w3_rv1", "w3_rvb",
               "w3_m0", "w3_m1", "w3_ma", "w3_sel")
        late_views = carve(wb, [(n, T[n].shape) for n in W3B])

        def loads_sync(sp):
            sp.dma_start(x_all[:, :, :, :].rearrange("p b t d -> p (b t) d"),
                         T["x"].rearrange("b (t p) d -> p (b t) d", p=128)).then_inc(kept["loaded"], 16)
            for n in ("ident", "causal", "tri", "ones_row"):
                dst = {"ident": ident, "causal": causal_f, "tri": tri, "ones_row": ones_row}[n]
                sp.dma_start(dst[tuple(slice(None) for _ in dst.shape)], T[n]).then_inc(kept["consts"], 16)
            for key, spec in (("w0", spec0), ("w1", spec1), ("w2", spec2)):
                for n, _ in spec:
                    sp.dma_start(w[n], T[n]).then_inc(kept[key], 16)

        def wait_weights(eng, key, n):
            eng.wait_ge(kept[key], 16 * n)

        L0A = lambda: Jobs(bank_m, a_fill, {"act": a_act, "dve": a_dve},
                           [("X", "act"), ("LG", "dve"), ("Q", "act"), ("K", "act"), ("V", "dve"), ("GT", "dve"),
                            ("AK", "act"), ("B", "dve"), ("U", "dve")]
                           + [(f"Y{e}", "dve") for e in range(L0_EXPERTS)])
        q0, k0, ak0, v0 = (arena_f[:, i * S:(i + 1) * S] for i in range(4))
        u0 = arena_f[:, 4 * S:5 * S].rearrange("p (j d) -> p j d", j=NTT)
        gT = ctx_raw

        def l0_scores(pe, k, bank):
            return pe.matmul(bank[:, :], q0[:, k * 128:(k + 1) * 128], ak0, start=True, stop=True)

        def l0_attention():
            return Attention(0, 1, None, l0_scores, None, None, heads=1)

        def layer0_tensor(pe):
            wait_weights(pe, "consts", 4)
            wait_weights(pe, "w0", len(spec0))
            pe.wait_ge(kept["first_xn"], NTT)
            with iterations(pe, 0) as b:
                A, M = L0A(), l0_attention()
                turn_xn(pe, A)
                A.wait_emptied(pe, "X")
                token_products(pe, A, "LG", w["w0_g"], L0_EXPERTS)
                project(pe, A, "Q", w["w0_lin"][:, 0, :], xnT[:, :])
                project(pe, A, "K", w["w0_lin"][:, 1, :], xnT[:, :])
                project(pe, A, "V", w["w0_lin"][:, 2, :], xnT[:, :])
                pe.wait_ge(s_gate, 1)
                A.wait_free(pe, "GT")
                for t in range(NTT):
                    last = pe.transpose(A.bank("GT")[0:L0_EXPERTS, t * 128:(t + 1) * 128],
                                        gate[:, t, 0:L0_EXPERTS], ident[:, :])
                last.then_inc(A.filled, 1)
                A.wait_emptied(pe, "K")
                project(pe, A, "AK", w["w0_lin"][:, 3, :], k0)
                A.wait_emptied(pe, "GT")
                token_products(pe, A, "B", w["w0_be"], D, lhs=gT[0:L0_EXPERTS])
                A.wait_emptied(pe, "V")
                token_products(pe, A, "U", w["w0_lin"][:, 4, :], D, lhs=v0)
                s = M.s
                A.wait_emptied(pe, "AK")
                for k in range(3):
                    l0_scores(pe, k, bank_s[k]).then_inc(s["scored"], 1)
                for k in range(NTT):
                    if k == 1:
                        pe.wait_ge(s["exped"], 1)
                        l0_scores(pe, 3, bank_s[0]).then_inc(s["scored"], 1)
                    pe.wait_ge(s["exped"], k + 1)
                    if k >= 2:
                        M.wait_copied(pe, k - 2)
                    for j in range(NTT):
                        last = pe.transpose(bank_t[k % 2][:, j * 128:(j + 1) * 128],
                                            prob[:, k % 3, j * 128:(j + 1) * 128], ident[:, :])
                    last.then_inc(s["turned"], 1)
                    for e in (2 * k, 2 * k + 1):
                        token_products(pe, A, f"Y{e}", w["w0_e"][:, e, :], D)
                A.wait_emptied(pe, "U")
                for i in range(NTT):
                    M.wait_copied(pe, i)
                    for j in range(NTT):
                        last = pe.matmul(bank_v[:, i * 128:(i + 1) * 128], pt[:, 0, j, i * 128:(i + 1) * 128],
                                         u0[:, j, :], start=(j == 0), stop=(j == NTT - 1))
                last.then_inc(s["pv"], 1)
                meet(pe, kept["go0"], b)

        def layer0_scalar(act):
            wait_weights(act, "consts", 4)
            with iterations(act, 0) as b:
                A, M = L0A(), l0_attention()
                evac(act, A, "X", xnT[:, :])
                evac(act, A, "Q", q0)
                exp_logits(act, NTT, L0_EXPERTS)
                evac(act, A, "K", k0)
                evac(act, A, "AK", ak0)
                s = M.s
                for tau in range(NTT + 2):
                    if tau < NTT:
                        act.wait_ge(s["maxed"], tau + 1)
                        if tau >= 3:
                            act.wait_ge(s["turned"], tau - 2)
                        act.activation(prob[:, tau % 3, :], bank_s[tau % 3][:, :], ACT.Exp,
                                       bias=negmax[:, tau:tau + 1], accum_out=rowsum[:, tau:tau + 1]
                                       ).then_inc(s["exped"], 1)
                    if tau >= 2 and tau % 2 == 1:
                        M.copy_tile(act, tau - 2)
                silu_tanh(act, L0_EXPERTS)
                meet(act, kept["go0"], b)

        def layer0_vector(dve):
            wait_weights(dve, "loaded", 1)
            wait_weights(dve, "consts", 4)
            dve.tensor_copy(ident_b[:, :], ident[:, :])
            dve.tensor_copy(causal_b[:, :], causal_f[:, :]).then_inc(kept["causal_set"], 1)
            norm_stats(dve, 0, Steps(dve, kept["first_stats"]), kept["first_var"])
            norm_apply(dve, 0, kept["first_rstd"], kept["first_xn"])
            with iterations(dve, 0) as b:
                A, M = L0A(), l0_attention()
                d = Steps(dve, s_dve)
                norm = NextNorm(dve, b, d)
                E = L0_EXPERTS
                evac(dve, A, "LG", lg[:, :, 0:E], A.bank("LG")[:, 0:NTT * E].rearrange("p (t e) -> p t e", t=NTT))
                A.wait_emptied(dve, "LG")
                shifted(dve, d, lg[:, :, 0:E], NTT, E)
                n = NTT * E * E
                top_k(dve, d, lg[:, :, 0:E], NTT, E, 2, gate[:, :, 0:E], prob_f[:, 0:n], prob_f[:, n:2 * n])
                evac(dve, A, "V", v0)
                gates(dve, d, NTT, E, of_all=False)
                evac(dve, A, "GT", gT[0:E, :], A.bank("GT")[0:E, :])
                evac(dve, A, "B", acc[:, :, :], bank3(A.bank("B")))
                evac(dve, A, "U", u0, bank3(A.bank("U")))
                s = M.s

                def negated_max(k):
                    dve.wait_ge(s["scored"], k + 1)
                    dve.tensor_reduce(negmax[:, k:k + 1], bank_s[k % 3][:, :], AX.X, ALU.max, negate=True
                                      ).then_inc(s["maxed"], 1)

                for k in range(3):
                    negated_max(k)
                for k in range(NTT):
                    if k == 1:
                        negated_max(3)
                    if k % 2 == 0:
                        M.copy_tile(dve, k)
                    for e in (2 * k, 2 * k + 1):
                        gated(dve, A, e)
                norm.stats()
                silu(dve, d)
                norm.apply()
                dve.wait_ge(s["pv"], 1)
                dve.wait_ge(s["exped"], NTT)
                d.add(dve.reciprocal(rowsum[:, 0:NTT], rowsum[:, 0:NTT]))
                d.settle()
                d.add(dve.tensor_tensor(tmp[:, 0], bank3(bank_v),
                                        rowsum[:, 0:NTT].unsqueeze(2).to_broadcast([128, NTT, D]), ALU.mult))
                d.settle()
                residual(dve, d, b, tmp[:, 0])
                meet(dve, kept["go0"], b)

        def layer0_gpsimd(pool):
            pool.memset(minus_half[:, :], -0.5).then_inc(kept["half_set"], 1)
            pool.wait_ge(kept["half_set"], 1)
            inverse_deviation(pool, kept["first_var"], kept["first_step"], kept["first_rstd"])
            with iterations(pool, 0) as b:
                A = L0A()
                add_up(pool, A, range(L0_EXPERTS), "B")
                inverse_deviation(pool, s_var, s_pool, s_rstd)
                meet_and_clear(pool, kept["go0"], b, others=3)

        QK1 = [f"{m}{c}" for c in range(8) for m in "QK"]
        all_banks = bank_m + bank_s + bank_t + [bank_v]
        L1A = lambda: Jobs(all_banks, a_fill, {"act": a_act, "dve": a_dve},
                           [("X", "act"), ("LG", "dve")]
                           + [(n, "act" if n[0] == "Q" else "dve") for n in QK1]
                           + [(f"V{t}{i}", "dve" if i else "act") for t in range(NTT) for i in range(2)]
                           + [("H0", "act"), ("GT", "dve"), ("B", "dve")]
                           + [j for e in range(L1_EXPERTS)
                              for j in ([(f"H{e + 1}", "act")] if e + 1 < L1_EXPERTS else []) + [(f"Y{e}", "dve")]])
        L1R = lambda: Jobs([bank_v], r_fill, {"dve": r_dve}, [(f"R{g}", "dve") for g in range(8)])
        q1 = arena_f[:, 0:16 * S].rearrange("p (h s) -> p h s", h=L1_HEADS)
        k1 = arena_f[:, 16 * S:24 * S].rearrange("p (c s) -> p c s", c=8)
        v1 = arena_f[:, 24 * S:32 * S].rearrange("p (t n) -> p t n", t=NTT)
        hid = pt[:, 0]

        def l1_scores(pe, k, bank):
            h, i = divmod(k, NTT)
            return pe.matmul(bank[:, :], q1[:, h, i * 128:(i + 1) * 128], k1[:, h // 2, :], start=True, stop=True)

        def l1_pv(pe, g):
            for j in range(NTT):
                for m in range(2):
                    h = 2 * g + m
                    last = pe.matmul(bank_v[64 * m:64 * m + 64, :], v1[:, j, h * 64:(h + 1) * 64], pt[:, h % 4, j, :],
                                     start=(j == 0), stop=(j == NTT - 1), skip_group_check=True)
            return last

        def l1_attention():
            return Attention(0, 2, L1R(), l1_scores, l1_pv, w["w1_o"])

        def layer1_tensor(pe):
            wait_weights(pe, "w1", len(spec1))
            with iterations(pe, 1) as b:
                A, M = L1A(), l1_attention()
                turn_xn(pe, A)
                A.wait_emptied(pe, "X")
                token_products(pe, A, "LG", w["w1_r"], 15, bias=w["w1_rb"])
                for n in QK1:
                    c = int(n[1:])
                    project(pe, A, n, w["w1_qkv"][:, "QK".index(n[0]), c * 128:(c + 1) * 128], xnT[:, :])
                for t in range(NTT):
                    for i in range(2):
                        A.wait_free(pe, f"V{t}{i}")
                        pe.matmul(A.bank(f"V{t}{i}")[:, :], xnT[:, t * 128:(t + 1) * 128],
                                  w["w1_qkv"][:, 2, i * 512:(i + 1) * 512], start=True, stop=True
                                  ).then_inc(A.filled, 1)
                project(pe, A, "H0", w["w1_e1"][:, 0, :], xnT[:, :])
                pe.wait_ge(s_gate, 1)
                A.wait_free(pe, "GT")
                for t in range(NTT):
                    last = pe.transpose(A.bank("GT")[0:16, t * 128:(t + 1) * 128], gate[:, t, :], ident[:, :])
                last.then_inc(A.filled, 1)
                A.wait_emptied(pe, "GT")
                token_products(pe, A, "B", w["w1_eb2"], D, lhs=gT[0:16])
                for e in range(L1_EXPERTS):
                    if e + 1 < L1_EXPERTS:
                        project(pe, A, f"H{e + 1}", w["w1_e1"][:, e + 1, :], xnT[:, :])
                    A.wait_emptied(pe, f"H{e}")
                    token_products(pe, A, f"Y{e}", w["w1_e2"][:, e, :], D, lhs=hid[:, e % 4, :])
                A.wait_all_free(pe)
                M.pe(pe)
                for t in range(NTT):
                    last = pe.matmul(bank_o[:, t * 128:(t + 1) * 128], ones_row[0:1, :], w["w1_bo"],
                                     start=False, stop=True, skip_group_check=True)
                last.then_inc(M.s["projected"], 1)
                meet(pe, kept["go1"], b)

        def layer1_scalar(act):
            wait_weights(act, "w1", len(spec1))
            with iterations(act, 1) as b:
                A, M = L1A(), l1_attention()
                evac(act, A, "X", xnT[:, :])
                act.wait_ge(kept["q1_zeroed"], 1)
                for n in QK1:
                    if n[0] == "Q":
                        A.wait_filled(act, n)
                        for m in range(2):
                            rows = slice(64 * m, 64 * m + 64)
                            last = act.activation(q1[rows, 2 * int(n[1:]) + m, :], A.bank(n)[rows, :], ACT.Copy,
                                                  scale=L1_DH ** -0.5)
                        last.then_inc(a_act, 1)
                    if n == "Q1":
                        exp_logits(act, NTT, 15)
                for t in range(NTT):
                    evac(act, A, f"V{t}0", v1[:, t, 0:512])
                for e in range(L1_EXPERTS):
                    if e >= 4:
                        A.wait_filled(act, f"Y{e - 4}")
                    A.wait_filled(act, f"H{e}")
                    act.activation(hid[:, e % 4, :], A.bank(f"H{e}")[:, :], ACT.Relu, bias=w["w1_eb1"][:, e:e + 1]
                                   ).then_inc(A.emptied["act"], 1)
                silu_tanh(act, L1_EXPERTS)
                M.act(act)
                meet(act, kept["go1"], b)

        def layer1_vector(dve):
            with iterations(dve, 1) as b:
                A, M = L1A(), l1_attention()
                d = Steps(dve, s_dve)
                norm = NextNorm(dve, b, d)
                E = 15
                evac(dve, A, "LG", lg[:, :, 0:E], A.bank("LG")[:, 0:NTT * E].rearrange("p (t e) -> p t e", t=NTT))
                A.wait_emptied(dve, "LG")
                shifted(dve, d, lg[:, :, 0:E], NTT, E)
                n = NTT * E * E
                vp = v_pad[:, :, :, :].rearrange("p a b c -> p (a b c)")
                top_k(dve, d, lg[:, :, 0:E], NTT, E, 3, gate[:, :, 0:E], vp[:, 0:n], vp[:, n:2 * n])
                d.add(dve.memset(gate[:, :, 15:16], 1.0))
                for c in range(8):
                    evac(dve, A, f"K{c}", k1[:, c, :])
                for t in range(NTT):
                    evac(dve, A, f"V{t}1", v1[:, t, 512:1024])
                gates(dve, d, NTT, E, of_all=True)
                evac(dve, A, "GT", gT[0:16, :], A.bank("GT")[0:16, :])
                evac(dve, A, "B", acc[:, :, :], bank3(A.bank("B")))
                for e in range(L1_EXPERTS):
                    gated(dve, A, e)
                silu(dve, d)
                M.dve(dve, norm)
                dve.wait_ge(M.s["projected"], M.groups + 1)
                residual(dve, d, b, bank3(bank_o))
                meet(dve, kept["go1"], b)

        def layer1_gpsimd(pool):
            pool.memset(arena_f[:, 0:16 * S], 0.0).then_inc(kept["q1_zeroed"], 1)
            with iterations(pool, 1) as b:
                add_up(pool, L1A(), range(L1_EXPERTS), "B")
                inverse_deviation(pool, s_var, s_pool, s_rstd)
                meet_and_clear(pool, kept["go1"], b, others=3)

        scratch_t = nc.dram_tensor("qk_parts", (4, NPARTS, 2, 128, S), bf16)
        scratch = scratch_t.ap()

        def stack(slot):
            return arena[:, slot * HEADS * S:(slot + 1) * HEADS * S].rearrange("p (h s) -> p h s", h=HEADS)

        def send_parts(sp, version, parts, ready, n, stored):
            sp.wait_ge(ready, n)
            sp.dma_start(scratch[version].rearrange("a q p s -> p (a q) s"), parts).then_inc(stored, 16)

        def fetch_stack(sp, version, which, slot, is_query, done):
            for j in range(NPARTS):
                part, step = (j, 0) if is_query else (0, 2 * 128 * S)
                src = bass.AP(scratch_t, ((version * NPARTS + part) * 2 + which) * 128 * S,
                              [[step, NPARTS], [HEADS * S, DH], [1, HEADS * S]])
                dst = stack(slot)[j * NPARTS * DH:(j + 1) * NPARTS * DH].rearrange("p h s -> p (h s)")
                sp.dma_start(dst, src).then_inc(done, 16)

        N_FETCH = 16 * NPARTS

        class Split:

            def __init__(self, number, whole, parts):
                self.n, self.whole, self.parts = number, whole, parts

            def act(self, act):
                for i in range(2):
                    if i:
                        act.wait_ge(s_rest, 2 * self.n + 1)
                    act.activation(self.parts[:, i], self.whole, ACT.Copy).then_inc(s_round, 1)

            def dve_step(self, dve, i):
                dve.wait_ge(s_round, 2 * self.n + i + 1)
                if i:
                    dve.wait_ge(s_rest, 2 * self.n + 1)
                dst = self.parts[:, 2] if i else self.whole
                dve.tensor_tensor(dst, self.whole, self.parts[:, i], ALU.subtract).then_inc(s_rest, 1)

            def dve(self, dve):
                for i in range(2):
                    self.dve_step(dve, i)

        def part_view(words):
            return words.bitcast(bf16).rearrange("p (a n) -> p a n", a=NPARTS)

        L2A = lambda: Jobs(all_banks, a_fill, {"act": a_act, "dve": a_dve, "norm": s_normed},
                           [("X", "act"), ("P1", "dve"), ("QK0", "norm"), ("QK1", "norm"), ("P2", "dve"), ("VA", "act"),
                            ("WT", "dve"), ("FQ", "dve"), ("FK", "dve"), ("FV", "act"), ("QT", "act"), ("KT", "dve")])
        v_banks = [bank_v, bank_m[0]]
        L2R = lambda i: Jobs(v_banks, (r_fill, r2_fill)[i], {"dve": (r_dve, r2_dve)[i]},
                             [(f"R{g}", "dve") for g in range(4)])
        heads_qk = pt_f[:, 0:1024]
        heads_sq = pt_f[:, 1024:2048]
        whole2 = [pt_f[:, 2048:3072], pt_f[:, 3072:4096]]
        parts2 = [part_view(pt_f[:, 4096:5632]), part_view(pt_f[:, 5632:7168])]
        mixed_w = pt_f[:, 7168:7552]
        h_sum, h_var = pt_f[:, 7552:7680], pt_f[:, 7680:7808]
        pooled, hidden1, mixed_b, prod_b = small[:, 0:1], small[:, 1:2], small[:, 2:4], small[:, 4:12]
        head_means = small[:, 16:48]
        ln_scaled = small[:, 48:52]
        va = xn

        def stacked_scores(first_slot, causal):
            def scores(pe, k, bank):
                g, r = divmod(k, 4 * NTT)
                i, m = divmod(r, 4)
                h = 4 * g + m
                n = (i + 1) * 128 if causal else S
                last = pe.matmul(bank[:, 0:n], stack(first_slot)[:, h, i * 128:(i + 1) * 128],
                                 stack(first_slot + 1)[:, h, 0:n], start=True, stop=not causal)
                if causal:
                    last = pe.matmul(bank[:, i * 128:n], ident_b[:, :], causal_b[:, :], start=False, stop=True)
                return last
            return scores

        def group_pv(causal):
            def pv(pe, u):
                g, i = divmod(u, NTT)
                n = i + 1 if causal else NTT
                for j in range(n):
                    for m in range(4):
                        last = pe.matmul(v_banks[g % 2][GROW * m:GROW * (m + 1), i * 128:(i + 1) * 128],
                                         v_pad[:, j, 4 * g + m, :], pt[:, u % 4, j, m * 128:(m + 1) * 128],
                                         start=(j == 0), stop=(j == n - 1), skip_group_check=True)
                return last
            return pv

        def l2_attention(i):
            return Attention(i, 4, L2R(i), stacked_scores(2 * i, i == 1), group_pv(i == 1),
                             w["w2_fo"] if i == 0 else w["w2_o"],
                             blocks=(lambda k: k % (4 * NTT) // 4 + 1) if i == 1 else (lambda k: NTT),
                             unit=4, n_scores=3, by_rows=True, pt_free=(s_sent, 32) if i == 0 else None)

        def layer2_tensor(pe):
            wait_weights(pe, "w2", len(spec2))
            pe.wait_ge(kept["v_set"], 2)
            pe.wait_ge(kept["centred"], 4)
            pe.wait_ge(kept["causal_set"], 1)
            with iterations(pe, 2) as b:
                A = L2A()
                turn_xn(pe, A)
                pe.wait_ge(s_pooled, 1)
                project(pe, A, "P1", w["w2_g1"], pooled, n=1)
                for i in range(2):
                    A.wait_free(pe, f"QK{i}")
                    for t in range(2):
                        last = pe.matmul(A.bank(f"QK{i}")[:, t * 256:(t + 1) * 256],
                                         xnT[:, (2 * i + t) * 128:(2 * i + t + 1) * 128], w["w2_qk"],
                                         start=True, stop=True)
                    last.then_inc(A.filled, 1)
                A.wait_emptied(pe, "P1")
                project(pe, A, "P2", hidden1.to_broadcast([128, 128]), w["w2_g2"], n=4)
                token_products(pe, A, "VA", w["w2_v"], D)
                pe.wait_ge(s_gate, 1)
                A.wait_free(pe, "WT")
                pe.transpose(A.bank("WT")[0:4, 0:128], gate[:, 0, 0:4], ident[:, :]).then_inc(A.filled, 1)
                pe.wait_ge(s_mixed, 1)
                project(pe, A, "FQ", mixed_w[:, 0:128], xnT[:, :])
                project(pe, A, "FK", mixed_w[:, 128:256], xnT[:, :])
                A.wait_free(pe, "FV")
                A.wait_emptied(pe, "WT")
                for t in range(NTT):
                    o = A.bank("FV")[:, t * 128:(t + 1) * 128]
                    pe.matmul(o, xnT[:, t * 128:(t + 1) * 128], mixed_w[:, 256:384], start=True, stop=False)
                    last = pe.matmul(o, gT[0:4, 0:128], w["w2_fbv"], start=False, stop=True)
                last.then_inc(A.filled, 1)
                A.wait_emptied(pe, "QK0")
                A.wait_emptied(pe, "QK1")
                for i, n in enumerate(("QT", "KT")):
                    A.wait_free(pe, n)
                    for t in range(NTT):
                        last = pe.transpose(A.bank(n)[:, t * 128:(t + 1) * 128],
                                            heads_qk[:, (2 * t + i) * 128:(2 * t + i + 1) * 128], ident[:, :])
                    last.then_inc(A.filled, 1)
                A.wait_all_free(pe)
                for i in range(2):
                    pe.wait_ge(s_stacked[i], 2 * N_FETCH)
                    if i:
                        pe.wait_ge(s_again, 1)
                        pe.wait_ge(s_taken, 1)
                    l2_attention(i).pe(pe)
                meet(pe, kept["go2"], b)

        def layer2_scalar(act):
            wait_weights(act, "w2", len(spec2))
            act.wait_ge(kept["centred"], 4)
            with iterations(act, 2) as b:
                A = L2A()
                evac(act, A, "X", xnT[:, :])
                for i in range(2):
                    A.wait_filled(act, f"QK{i}")
                    act.activation(heads_sq[:, i * 512:(i + 1) * 512], A.bank(f"QK{i}")[:, :], ACT.Square
                                   ).then_inc(s_squared, 1)
                exp_logits(act, 1, 4)
                evac(act, A, "VA", flat(va[:, :, :]))
                act.wait_ge(s_hvar, 1)
                act.activation(h_var, h_var, ACT.Sqrt).then_inc(s_hrstd, 1)
                A.wait_emptied(act, "FQ")
                A.wait_emptied(act, "FK")
                Split(0, whole2[0], parts2[0]).act(act)
                act.wait_ge(kept["v_set"], 2)
                act_copy = A.bank("FV")[:, :].rearrange("p (t h d) -> p t h d", t=NTT, h=HEADS)
                A.wait_filled(act, "FV")
                act.activation(v_pad[:, :, :, 0:DH], act_copy, ACT.Copy).then_inc(A.emptied["act"], 1)
                A.wait_filled(act, "QT")
                act.activation(whole2[1][:, 0:S], A.bank("QT")[:, :], ACT.Identity, bias=ln_scaled[:, 2:3],
                               scale=ln_scaled[:, 0:1]).then_inc(a_act, 1)
                A.wait_emptied(act, "QT")
                A.wait_emptied(act, "KT")
                Split(1, whole2[1], parts2[1]).act(act)
                for i in range(2):
                    l2_attention(i).act(act)
                    if i == 0:
                        act.wait_ge(s_taken, 1)
                        act.activation(flat(tmp[:, 0]), acc_f, ACT.Tanh, scale=0.5).then_inc(s_e1, 1)
                meet(act, kept["go2"], b)

        def layer2_vector(dve):
            wait_weights(dve, "w2", len(spec2))
            scale2 = float(D) ** -0.25
            dve.memset(arena_f[64:128, 16 * S:32 * S], 0.0).then_inc(kept["keys_zeroed"], 1)
            heads_w = w["w2_qk"].rearrange("p (n d) -> p n d", d=DH)
            once = Steps(dve, kept["centred"])
            once.add(dve.tensor_scalar(ln_scaled, w["w2_ln"], scale2, None, ALU.mult))
            once.add(dve.tensor_reduce(head_means, heads_w, AX.X, ALU.add))
            once.settle()
            once.add(dve.tensor_scalar(head_means, head_means, 1.0 / DH, None, ALU.mult))
            once.settle()
            once.add(dve.tensor_tensor(heads_w, heads_w, head_means.unsqueeze(2).to_broadcast([128, 2 * HEADS, DH]),
                                       ALU.subtract))
            once.settle()
            with iterations(dve, 2) as b:
                A = L2A()
                d = Steps(dve, s_dve)
                norm = NextNorm(dve, b, d)
                A.wait_emptied(dve, "X")
                d.add(dve.tensor_reduce(pooled, xnT[:, :], AX.X, ALU.add))
                d.settle()
                dve.tensor_scalar(pooled, pooled, 1.0 / S, None, ALU.mult).then_inc(s_pooled, 1)
                A.wait_filled(dve, "P1")
                dve.tensor_scalar(hidden1, A.bank("P1")[:, 0:1], w["w2_b1"], 0.0, ALU.add, ALU.max
                                  ).then_inc(A.emptied["dve"], 1)
                A.wait_filled(dve, "P2")
                dve.tensor_tensor(lg[:, 0, 0:4], A.bank("P2")[:, 0:4], w["w2_b2"], ALU.add
                                  ).then_inc(A.emptied["dve"], 1)
                A.wait_emptied(dve, "P2")
                shifted(dve, d, lg[:, 0:1, 0:4], 1, 4)
                top_k(dve, d, lg[:, 0:1, 0:4], 1, 4, 2, gate[:, 0:1, 0:4], prob_f[:, 0:16], prob_f[:, 16:32])
                gates(dve, d, 1, 4, of_all=False)
                dve.wait_ge(s_gate, 1)
                for e in range(4):
                    if e == 0:
                        d.add(dve.tensor_scalar(mixed_w, w["w2_fe"][:, 0, :], gate[:, 0, 0:1], None, ALU.mult))
                    else:
                        d.settle()
                        d.add(dve.scalar_tensor_tensor(mixed_w, w["w2_fe"][:, e, :], gate[:, 0, e:e + 1], mixed_w,
                                                       ALU.mult, ALU.add))
                d.settle()
                pb = prod_b.rearrange("p (a e) -> p a e", a=2)
                dve.tensor_tensor(pb, w["w2_fb"], gate[:, 0:1, 0:4].to_broadcast([128, 2, 4]), ALU.mult
                                  ).then_inc(s_mixed, 1)
                dve.wait_ge(s_mixed, 1)
                d.add(dve.tensor_reduce(mixed_b, pb, AX.X, ALU.add))
                d.settle()
                evac(dve, A, "WT", gT[0:4, 0:128], A.bank("WT")[0:4, 0:128])
                dve.wait_ge(s_squared, 2)
                d.add(dve.tensor_reduce(h_var, heads_sq.rearrange("p (n d) -> p n d", d=DH), AX.X, ALU.add))
                d.settle()
                dve.tensor_scalar(h_var, h_var, 1.0 / DH, EPS, ALU.mult, ALU.add).then_inc(s_hvar, 1)
                A.wait_filled(dve, "FQ")
                dve.tensor_scalar(whole2[0][:, 0:S], A.bank("FQ")[:, :], mixed_b[:, 0:1], DH ** -0.5, ALU.add, ALU.mult
                                  ).then_inc(A.emptied["dve"], 1)
                A.wait_filled(dve, "FK")
                dve.tensor_scalar(whole2[0][:, S:2 * S], A.bank("FK")[:, :], mixed_b[:, 1:2], None, ALU.add
                                  ).then_inc(A.emptied["dve"], 1)
                dve.wait_ge(s_hrstd, 1)
                d.add(dve.reciprocal(h_var, h_var))
                A.wait_emptied(dve, "FK")
                first, second = Split(0, whole2[0], parts2[0]), Split(1, whole2[1], parts2[1])
                first.dve_step(dve, 0)
                d.settle()
                for i in range(2):
                    A.wait_filled(dve, f"QK{i}")
                    dve.tensor_tensor(heads_qk[:, i * 512:(i + 1) * 512].rearrange("p (n d h) -> p n h d", d=DH, h=HEADS),
                                      A.bank(f"QK{i}")[:, :].rearrange("p (n h d) -> p n h d", d=DH, h=HEADS),
                                      h_var[:, i * 64:(i + 1) * 64].rearrange("p (n h) -> p n h", h=HEADS)
                                      .unsqueeze(3).to_broadcast([128, 4, HEADS, DH]), ALU.mult
                                      ).then_inc(s_normed, 1)
                first.dve_step(dve, 1)
                A.wait_filled(dve, "KT")
                dve.tensor_scalar(whole2[1][:, S:2 * S], A.bank("KT")[:, :], ln_scaled[:, 1:2], ln_scaled[:, 3:4],
                                  ALU.mult, ALU.add).then_inc(a_dve, 1)
                A.wait_emptied(dve, "KT")
                A.wait_emptied(dve, "QT")
                second.dve(dve)
                l2_attention(0).dve(dve)
                dve.wait_ge(att[0]["projected"], 4)
                dve.tensor_copy(acc[:, :, :], bank3(bank_o)).then_inc(s_taken, 1)
                silu(dve, d)
                l2_attention(1).dve(dve, norm)
                dve.wait_ge(att[1]["projected"], 4)
                residual(dve, d, b, bank3(bank_o))
                meet(dve, kept["go2"], b)

        def layer2_gpsimd(pool):
            pool.memset(arena_f[64:128, 0:16 * S], 0.0).then_inc(kept["stack_zeroed"], 1)
            pool.wait_ge(kept["stack_zeroed"], 1)
            pool.memset(v_pad[:, :, :, :].rearrange("p a b c -> p (a b c)"), 0.0).then_inc(kept["v_set"], 1)
            pool.wait_ge(kept["v_set"], 1)
            pool.memset(v_pad[:, :, :, DH:DH + 1].rearrange("p a b c -> p (a b) c"), 1.0).then_inc(kept["v_set"], 1)
            with iterations(pool, 2) as b:
                pool.wait_ge(att[0]["pv"], 4 * NTT)
                L2A().wait_emptied(pool, "VA")
                pool.tensor_copy(v_pad[:, :, :, 0:DH], va[:, :, :].rearrange("p t (h d) -> p t h d", h=HEADS)
                                 ).then_inc(s_again, 1)
                inverse_deviation(pool, s_var, s_pool, s_rstd)
                meet_and_clear(pool, kept["go2"], b)

        def load_weights(sp, spec, views, sem_):
            for n, _ in spec:
                sp.dma_start(views[n], T[n]).then_inc(sem_, 16)

        def layer2_sync(sp):
            sp.wait_ge(kept["go1"], B)
            load_weights(sp, [(n, None) for n in W3B], {n: late_views[n] for n in W3B}, kept["w3"])
            sp.wait_ge(kept["stack_zeroed"], 1)
            sp.wait_ge(kept["keys_zeroed"], 1)
            with iterations(sp, 2) as b:
                for i in range(2):
                    send_parts(sp, i, parts2[i].rearrange("p a (q s) -> p (a q) s", q=2), s_rest, 2 * i + 2, s_sent)
                    sp.wait_ge(s_sent, 16 * (i + 1))
                    fetch_stack(sp, i, 0, 2 * i, True, s_stacked[i])
                    fetch_stack(sp, i, 1, 2 * i + 1, False, s_stacked[i])
                meet_sync(sp, kept["go2"], b)

        E_ROW = HEADS * BAND
        A_SLOT = 32 + 128 * A_ROW
        offset_scores = nc.dram_tensor("offset_scores", (S, HEADS, BAND), f32)
        skewed = nc.dram_tensor("skewed_probs", (NTT, 4, A_SLOT), f32)
        spec3b = [(n, T[n].shape) for n in W3B]
        spec3a = [("w3_rk", T["w3_rk"].shape)]
        w3b = carve(wb, spec3b + [("masked0", (128, S)), ("masked1", (128, S))])
        w3a = carve(wa, spec3a + [("banded", (128, 2, NTT, 128)), ("bandedT", (BAND, 4, S))])
        N_W3 = len(spec3a) + len(spec3b)

        L3E = 4 * NTT
        L3A = lambda: Jobs(bank_m, a_fill, {"act": a_act, "dve": a_dve},
                           [("X", "act"), ("LG", "dve"), ("Q", "act"), ("K", "dve"), ("V", "act")]
                           + [(f"E{j}", "act") for j in range(L3E)])
        L3F = lambda: Jobs(bank_s + bank_t, f_fill, {"act": f_act, "dve": f_dve},
                           [(f"{m}{e}{i}", "dve") for e in range(1) for i in range(2) for m in "GU"]
                           + [(n, "dve") for e in range(1, L3_EXPERTS)
                              for n in [f"{m}{e}{i}" for i in range(2) for m in "GU"] + [f"Y{e - 1}"]]
                           + [(f"Y{L3_EXPERTS - 1}", "dve")])
        L3R = lambda: Jobs(v_banks, r_fill, {"act": r_act}, [(f"R{g}", "act") for g in range(4)])
        hid3 = pt_f[:, 0:2048].rearrange("p (a i s) -> p a i s", a=2, i=2)
        tanh3 = pt_f[:, 2048:3072].rearrange("p (a s) -> p a s", a=2)
        gate3 = pt_f[:, 3072:4096].rearrange("p (a s) -> p a s", a=2)
        whole3 = [pt_f[:, 4096:5120], pt_f[:, 5120:6144]]
        parts3 = [part_view(pt_f[:, 6144:7680]), part_view(prob_f)]
        q_kept = pt_f[:, 7680:8192]
        near = tmp[:, :, :, :].rearrange("p a t d -> p (a t d)")[:, 0:2 * NTT * WIN].rearrange(
            "p (a m w) -> p a m w", a=2, m=4)
        sums_sb = flat(xn[:, :, :])
        bank_a = bank_s[2]
        NU = HEADS // 4 * NTT

        def window(i, c):
            w0 = i * 128 + 32 * c - 32
            return max(0, w0), min(S, w0 + WIN), max(0, w0) - w0

        class OffsetAttention(Attention):

            def __init__(self, b):
                self.b = b
                super().__init__(0, 4, L3R(), None, None, w3b["w3_o"], unit=4, n_scores=2, by_rows=True,
                                 pt_free=(s_sent, 32))
                self.steps = self.nt + 18

            def pe(self, pe):
                s = self.s
                for tau in range(self.steps):
                    if tau < self.nt:
                        u, m = divmod(tau, 4)
                        h, i = 4 * (u // NTT) + m, u % NTT
                        if tau >= 2:
                            pe.wait_ge(s["exped"], tau - 1)
                        if m == 0:
                            pe.wait_ge(s_near[u % 2], 64 * (u // 2 + 1))
                        bank = self.banks[tau % 2]
                        for slot in (2, 3, 1):
                            for c in range(4):
                                lo, hi, at = window(i, c)
                                a, z = {2: (0, lo), 3: (hi, S), 1: (lo, hi)}[slot]
                                if z > a:
                                    pe.matmul(bank[32 * c:32 * c + 32, a:z],
                                              stack(0)[:, h, i * 128 + 32 * c:i * 128 + 32 * c + 32],
                                              stack(slot)[:, h, a:z], start=True, stop=(slot != 1),
                                              skip_group_check=True)
                        for c in range(4):
                            lo, hi, at = window(i, c)
                            rows = slice(32 * c, 32 * c + 32)
                            last = pe.matmul(bank[rows, lo:hi], ident[:, rows], near[:, u % 2, m, at:at + hi - lo],
                                             start=False, stop=True, skip_group_check=True)
                        last.then_inc(s["scored"], 1)
                    k = tau - self.LAG
                    if 0 <= k < self.nt:
                        pe.wait_ge(s["exped"], k + 1)
                        if k >= 2:
                            self.wait_copied(pe, k - 2)
                        for j in range(NTT):
                            last = pe.transpose(bank_t[k % 2][:, j * 128:(j + 1) * 128],
                                                prob[:, k % 3, j * 128:(j + 1) * 128], ident[:, :])
                        last.then_inc(s["turned"], 1)
                    u = self.unit_at(tau, 2)
                    if u is not None:
                        self.wait_copied(pe, 4 * u + 3)
                        self.wait_copied(pe, 4 * u + 2)
                        g, i = divmod(u, NTT)
                        if g >= 2 and i == 0:
                            pe.wait_ge(s_normal, g - 1)
                        for j in range(NTT):
                            for m in range(4):
                                last = pe.matmul(v_banks[g % 2][GROW * m:GROW * (m + 1), i * 128:(i + 1) * 128],
                                                 v_pad[:, j, 4 * g + m, :], pt[:, u % 4, j, m * 128:(m + 1) * 128],
                                                 start=(i == 0 and j == 0), stop=False, skip_group_check=True)
                        last.then_inc(s["pv"], 1)
                    u, r = divmod(tau - 11, 4)
                    if r == 0 and 0 <= u < NU:
                        pe.wait_ge(s_askew[u % 2], self.b * SKEWED + 16 * (u // 2 + 1))
                        if u >= 1:
                            pe.wait_ge(s_amasked, u)
                        for m in range(4):
                            last = pe.transpose(bank_a[0:BAND, m * 128:(m + 1) * 128],
                                                w3a["banded"][:, u % 2, m, 0:BAND], ident[:, :])
                        last.then_inc(s_aturned, 1)
                    u, r = divmod(tau - 13, 4)
                    if r == 0 and 0 <= u < NU:
                        pe.wait_ge(s_amasked, u + 1)
                        g, i = divmod(u, NTT)
                        for m in range(4):
                            last = pe.matmul(v_banks[g % 2][GROW * m:GROW * (m + 1), i * 128:(i + 1) * 128],
                                             w3b["w3_rvb"], w3a["bandedT"][:, u % 4, m * 128:(m + 1) * 128],
                                             start=False, stop=True, skip_group_check=True)
                        last.then_inc(s_band, 1)
                    g = self.at(tau, 9)
                    if g is not None:
                        pe.wait_ge(s["inverted"], g + 1)
                        pe.wait_ge(s["craw"], g + 1)
                        self.spread_sums(pe, g, self.R.bank(f"R{g}")).then_inc(self.R.filled, 1)
                    g = self.at(tau, 12)
                    if g is not None:
                        self.R.wait_emptied(pe, f"R{g}")
                        pe.matmul(v_banks[g % 2][:, :], w3b["w3_sel"], ctx_raw[:, :], start=True, stop=False)
                        for n in range(2):
                            pe.wait_ge(s_bmasked, 2 * g + n + 1)
                            last = pe.matmul(v_banks[g % 2][:, :], w3b[f"w3_rv{n}"], w3b[f"masked{n}"],
                                             start=False, stop=(n == 1))
                        last.then_inc(s_numer, 1)
                    g = self.at(tau, 14)
                    if g is not None:
                        pe.wait_ge(s_normal, g + 1)
                        for t in range(NTT):
                            last = pe.matmul(bank_o[:, t * 128:(t + 1) * 128], ctx_n[:, g % 2, t * 128:(t + 1) * 128],
                                             self.wo[:, g, :], start=(g == 0 and t == 0), stop=(g == self.groups - 1),
                                             skip_group_check=True)
                        last.then_inc(s["projected"], 1)

            def act(self, act):
                s = self.s
                for tau in range(self.steps):
                    k = tau - self.LAG
                    if 0 <= k < self.nt and k % 2 == 1:
                        self.copy_tile(act, k)
                    if tau < self.nt:
                        act.wait_ge(s["maxed"], tau + 1)
                        if tau >= 3:
                            act.wait_ge(s["turned"], tau - 2)
                            act.wait_ge(s_written[tau % 3], 16 * (tau // 3))
                        act.activation(prob[:, tau % 3, :], self.banks[tau % 2][:, :], ACT.Exp,
                                       bias=negmax[:, tau:tau + 1], accum_out=rowsum[:, tau:tau + 1]
                                       ).then_inc(s["exped"], 1)
                    g = self.at(tau, 8)
                    if g is not None:
                        act.wait_ge(s_band, 4 * (g + 1))
                        if g >= 1:
                            act.wait_ge(s_numer, g)
                        act.activation(ctx_raw[:, :], v_banks[g % 2][:, :], ACT.Copy).then_inc(s["craw"], 1)
                    g = self.at(tau, 10)
                    if g is not None:
                        if g >= 1:
                            act.wait_ge(s_normal, g)
                        self.R.wait_filled(act, f"R{g}")
                        act.activation(sums_sb, self.R.bank(f"R{g}")[:, :], ACT.Copy).then_inc(r_act, 1)

            def dve(self, dve, norm):
                s = self.s
                for tau in range(self.steps):
                    if tau == self.nt + 1:
                        norm.stats()
                    if tau < self.nt:
                        dve.wait_ge(s["scored"], tau + 1)
                        dve.tensor_reduce(negmax[:, tau:tau + 1], self.banks[tau % 2][:, :], AX.X, ALU.max,
                                          negate=True).then_inc(s["maxed"], 1)
                    k = tau - self.LAG
                    if 0 <= k < self.nt and k % 2 == 0:
                        self.copy_tile(dve, k)
                    g = self.at(tau, 1)
                    if g is not None:
                        cols = rowsum[:, g * self.per:(g + 1) * self.per]
                        dve.wait_ge(s["exped"], (g + 1) * self.per)
                        dve.reciprocal(cols, cols).then_inc(s["inverted"], 1)
                    u, r = divmod(tau - 12, 4)
                    if r == 0 and 0 <= u < NU:
                        dve.wait_ge(s_aturned, u + 1)
                        if u >= 4:
                            dve.wait_ge(s_band, u - 3)
                        dve.tensor_tensor(w3a["bandedT"][:, u % 4, :].rearrange("p (i n) -> p i n", i=NTT),
                                          bank_a[0:BAND, :].rearrange("p (i n) -> p i n", i=NTT),
                                          w3b["w3_ma"].unsqueeze(1).to_broadcast([BAND, NTT, 128]), ALU.mult
                                          ).then_inc(s_amasked, 1)
                    g = self.at(tau, 13)
                    if g is not None:
                        dve.wait_ge(s_numer, g + 1)
                        self.R.wait_emptied(dve, f"R{g}")
                        if g >= 2:
                            dve.wait_ge(s["projected"], g - 1)
                        dve.tensor_tensor(ctx_n[:, g % 2, :], v_banks[g % 2][:, :], sums_sb, ALU.mult).then_inc(s_normal, 1)

            def pool(self, pool):
                s = self.s
                for tau in range(self.steps):
                    if tau == self.nt + 1:
                        inverse_deviation(pool, s_var, s_pool, s_rstd)
                    u, r = divmod(tau - 4, 4)
                    if r == 0 and 0 <= u < NU:
                        for k in range(4 * u, 4 * u + 4):
                            pool.wait_ge(s_written[k % 3], 16 * (k // 3 + 1))
                        if u >= 2:
                            pool.wait_ge(s_aturned, u - 1)
                        src = bass.AP(skewed, (u % NTT) * 4 * A_SLOT + 1,
                                      [[A_ROW + 1, 128], [A_SLOT, 4], [1, BAND]])
                        pool.dma_start(w3a["banded"][:, u % 2, :, 0:BAND], src).then_inc(s_askew[u % 2], 16)
                    g = self.at(tau, 9)
                    if g is not None:
                        pool.wait_ge(s["craw"], g + 1)
                        if g >= 1:
                            pool.wait_ge(s_numer, g)
                        for n in range(2):
                            pool.tensor_tensor(w3b[f"masked{n}"], ctx_raw[:, :], w3b[f"w3_m{n}"], ALU.mult
                                               ).then_inc(s_bmasked, 1)

            def sync(self, sp):
                s = self.s

                def load_near(u):
                    g, i = divmod(u, NTT)
                    for c in range(4):
                        src = bass.AP(offset_scores, (i * 128 + 32 * c) * E_ROW + 4 * g * BAND + 31,
                                      [[E_ROW - 1, 32], [BAND, 4], [1, WIN]])
                        sp.dma_start(near[32 * c:32 * c + 32, u % 2], src).then_inc(s_near[u % 2], 16)

                load_near(0)
                load_near(1)
                for k in range(self.nt):
                    u, m = divmod(k, 4)
                    i = u % NTT
                    if u >= NTT and m == 0:
                        sp.wait_ge(s_aturned, u - NTT + 1)
                    sp.wait_ge(s["exped"], k + 1)
                    lo, hi = max(0, i * 128 - 32), min(S, i * 128 + 160)
                    dst = bass.AP(skewed, (i * 4 + m) * A_SLOT + 32 + lo - (i * 128 - 32), [[A_ROW, 128], [1, hi - lo]])
                    sp.dma_start(dst, prob[:, k % 3, lo:hi]).then_inc(s_written[k % 3], 16)
                    if m == 3 and u + 2 < NU:
                        sp.wait_ge(s["scored"], k + 1)
                        load_near(u + 2)

        def layer3_tensor(pe):
            wait_weights(pe, "w3", N_W3)
            pe.wait_ge(kept["v3_set"], 17)
            with iterations(pe, 3) as b:
                A, F = L3A(), L3F()
                turn_xn(pe, A)
                A.wait_emptied(pe, "X")
                token_products(pe, A, "LG", w3b["w3_rt"], 8)
                project(pe, A, "Q", w3b["w3_lin"][:, 0, :], xnT[:, :])
                project(pe, A, "K", w3b["w3_lin"][:, 1, :], xnT[:, :])
                token_products(pe, A, "V", w3b["w3_lin"][:, 2, :], D)
                pe.wait_ge(s_qkept, 1)

                def offsets(j):
                    t, q = divmod(j, 4)
                    project(pe, A, f"E{j}", q_kept[:, t * 128:(t + 1) * 128],
                            w3a["w3_rk"][:, q * 4 * BAND:(q + 1) * 4 * BAND], n=4 * BAND)

                def down(e):
                    F.wait_free(pe, f"Y{e}")
                    F.wait_emptied(pe, f"U{e}1")
                    for t in range(NTT):
                        for i in range(2):
                            last = pe.matmul(F.bank(f"Y{e}")[:, t * 128:(t + 1) * 128],
                                             hid3[:, e % 2, i, t * 128:(t + 1) * 128], w3b["w3_down"][:, e, i * D:(i + 1) * D],
                                             start=(i == 0), stop=(i == 1))
                    last.then_inc(F.filled, 1)

                for e in range(L3_EXPERTS):
                    for i in range(2):
                        project(pe, F, f"G{e}{i}", w3b["w3_gate"][:, e, i * 128:(i + 1) * 128], xnT[:, :])
                        project(pe, F, f"U{e}{i}", w3b["w3_up"][:, e, i * 128:(i + 1) * 128], xnT[:, :])
                        if 2 * e + i < L3E:
                            offsets(2 * e + i)
                    if e:
                        down(e - 1)
                down(L3_EXPERTS - 1)
                F.wait_all_free(pe)
                A.wait_all_free(pe)
                for i in range(2):
                    pe.wait_ge(s_stacked[i], 2 * N_FETCH)
                OffsetAttention(b).pe(pe)
                meet(pe, kept["go3"], b)

        def layer3_scalar(act):
            wait_weights(act, "w3", N_W3)
            act.wait_ge(kept["v3_set"], 17)
            with iterations(act, 3) as b:
                A, F = L3A(), L3F()
                evac(act, A, "X", xnT[:, :])
                A.wait_filled(act, "Q")
                act.activation(q_kept, A.bank("Q")[:, :], ACT.Copy, scale=DH ** -0.5).then_inc(s_qkept, 1)
                evac(act, A, "Q", whole3[0][:, 0:S], scale=DH ** -0.5)
                A.wait_filled(act, "V")
                act.activation(v_pad[:, :, :, 0:DH], A.bank("V")[:, :].rearrange("p (t h d) -> p t h d", t=NTT, h=HEADS),
                               ACT.Copy).then_inc(a_act, 1)
                A.wait_emptied(act, "Q")
                A.wait_emptied(act, "K")
                Split(0, whole3[0], parts3[0]).act(act)
                act.wait_ge(s_rest, 2)
                Split(1, whole3[1], parts3[1]).act(act)
                for n in range(2 * L3_EXPERTS):
                    name = f"G{n // 2}{n % 2}"
                    F.wait_filled(act, name)
                    if n >= 2:
                        F.wait_emptied(act, f"G{(n - 2) // 2}{n % 2}")
                    act.activation(tanh3[:, n % 2], F.bank(name)[:, :], ACT.Tanh, scale=0.5).then_inc(s_tanh, 1)
                    if n < L3E:
                        if n >= 2:
                            act.wait_ge(s_esent[n % 2], b * SENT + 16 * (n // 2))
                        evac(act, A, f"E{n}", ctx_n[:, n % 2, 0:4 * BAND], A.bank(f"E{n}")[:, 0:4 * BAND])
                silu_tanh(act, L3_EXPERTS - 1)
                act.wait_ge(s_sent, 32)
                OffsetAttention(b).act(act)
                meet(act, kept["go3"], b)

        def layer3_vector(dve):
            wait_weights(dve, "w3", N_W3)
            with iterations(dve, 3) as b:
                A, F, M = L3A(), L3F(), OffsetAttention(b)
                d = Steps(dve, s_dve)
                norm = NextNorm(dve, b, d)
                evac(dve, A, "LG", lg[:, :, 0:8], A.bank("LG")[:, 0:NTT * 8].rearrange("p (t e) -> p t e", t=NTT))
                A.wait_emptied(dve, "LG")
                d.add(dve.memset(gate[:, :, 8:9], 1.0))
                top_k(dve, d, lg[:, :, 0:8], NTT, 8, 1, gate[:, :, 0:8], prob_f[:, 0:256], prob_f[:, 256:512])
                A.wait_filled(dve, "K")
                dve.tensor_copy(whole3[0][:, S:2 * S], A.bank("K")[:, :])
                dve.tensor_scalar(whole3[1][:, 0:S], A.bank("K")[:, :], w3b["w3_relk"][:, 0:1], None, ALU.add)
                dve.tensor_scalar(whole3[1][:, S:2 * S], A.bank("K")[:, :], w3b["w3_relk"][:, 1:2], None, ALU.add
                                  ).then_inc(a_dve, 1)
                A.wait_emptied(dve, "K")
                A.wait_emptied(dve, "Q")
                Split(0, whole3[0], parts3[0]).dve(dve)
                Split(1, whole3[1], parts3[1]).dve(dve)
                for e in range(L3_EXPERTS):
                    for i in range(2):
                        n = 2 * e + i
                        dve.wait_ge(s_tanh, n + 1)
                        if n >= 2:
                            F.wait_emptied(dve, f"U{(n - 2) // 2}{n % 2}")
                        dve.scalar_tensor_tensor(gate3[:, n % 2], tanh3[:, n % 2], 1.0, F.bank(f"G{e}{i}")[:, :],
                                                 ALU.add, ALU.mult).then_inc(f_dve, 1)
                        F.wait_filled(dve, f"U{e}{i}")
                        F.wait_emptied(dve, f"G{e}{i}")
                        if e >= 2:
                            F.wait_filled(dve, f"Y{e - 2}")
                        dve.scalar_tensor_tensor(hid3[:, e % 2, i], gate3[:, n % 2], 0.5, F.bank(f"U{e}{i}")[:, :],
                                                 ALU.mult, ALU.mult).then_inc(f_dve, 1)
                    if e:
                        gated(dve, F, e - 1, first=1)
                gated(dve, F, L3_EXPERTS - 1, first=1)
                silu(dve, d)
                M.dve(dve, norm)
                dve.wait_ge(s_normal, 4)
                norm.apply()
                dve.wait_ge(M.s["projected"], 4)
                residual(dve, d, b, bank3(bank_o))
                meet(dve, kept["go3"], b)

        def layer3_gpsimd(pool):
            flat_v = v_pad[:, :, :, :].rearrange("p a b c -> p (a b c)")
            pool.memset(flat_v, 0.0).then_inc(kept["v3_set"], 1)
            pool.wait_ge(kept["v3_set"], 1)
            zeros = 2 * NTT * A_SLOT // 128
            for half in range(2):
                pool.dma_start(bass.AP(skewed, half * 128 * zeros, [[zeros, 128], [1, zeros]]), flat_v[:, 0:zeros]
                               ).then_inc(kept["zeroed"], 16)
            pool.wait_ge(kept["zeroed"], 32)
            for j in range(NTT):
                for a in range(4):
                    u = DH + 4 * j + a
                    pool.memset(v_pad[32 * a:32 * a + 32, j, :, u:u + 1], 1.0).then_inc(kept["v3_set"], 1)
            pool.wait_ge(kept["v3_set"], 17)
            with iterations(pool, 3) as b:
                A, F = L3A(), L3F()
                for j in range(L3E):
                    t, q = divmod(j, 4)
                    A.wait_emptied(pool, f"E{j}")
                    dst = bass.AP(offset_scores, t * 128 * E_ROW + q * 4 * BAND, [[E_ROW, 128], [1, 4 * BAND]])
                    pool.dma_start(dst, ctx_n[:, j % 2, 0:4 * BAND]).then_inc(s_esent[j % 2], 16)
                    if j % 2 and j > 3:
                        add_up(pool, F, [(j - 3) // 2], "Y0")
                add_up(pool, F, range(L3E // 2 - 1, L3_EXPERTS), "Y0")
                for i in range(2):
                    pool.wait_ge(s_esent[i], b * SENT + SENT)
                pool.sem_inc(s_offsets, 1)
                OffsetAttention(b).pool(pool)
                meet_and_clear(pool, kept["go3"], b)

        def layer3_sync(sp):
            load_weights(sp, spec3a, w3a, kept["w3"])
            sp.wait_ge(kept["zeroed"], 32)
            with iterations(sp, 3) as b:
                for i in range(2):
                    send_parts(sp, 2 + i, parts3[i].rearrange("p a (q s) -> p (a q) s", q=2), s_rest, 2 * i + 2, s_sent)
                    sp.wait_ge(s_sent, 16 * (i + 1))
                    fetch_stack(sp, 2 + i, 0, 2 * i, i == 0, s_stacked[i])
                    fetch_stack(sp, 2 + i, 1, 2 * i + 1, False, s_stacked[i])
                sp.wait_ge(s_offsets, 1)
                sp.wait_ge(s_silu, 1)
                OffsetAttention(b).sync(sp)
                meet_sync(sp, kept["go3"], b)

        def output_sync(sp):
            sp.dma_start(out.rearrange("b (t p) d -> p (b t) d", p=128),
                         x_all[:, :, :, :].rearrange("p b t d -> p (b t) d")).then_inc(kept["stored"], 16)
            sp.wait_ge(kept["stored"], 16)

        @block.sync
        def _(sp):
            loads_sync(sp)
            layer2_sync(sp)
            layer3_sync(sp)
            output_sync(sp)

        @block.tensor
        def _(pe):
            layer0_tensor(pe)
            layer1_tensor(pe)
            layer2_tensor(pe)
            layer3_tensor(pe)

        @block.vector
        def _(dve):
            layer0_vector(dve)
            layer1_vector(dve)
            layer2_vector(dve)
            layer3_vector(dve)

        @block.scalar
        def _(act):
            layer0_scalar(act)
            layer1_scalar(act)
            layer2_scalar(act)
            layer3_scalar(act)

        @block.gpsimd
        def _(pool):
            layer0_gpsimd(pool)
            layer1_gpsimd(pool)
            layer2_gpsimd(pool)
            layer3_gpsimd(pool)


def laid_out(i):
    a = {k: np.asarray(v) for k, v in i.items()}
    f = np.float32
    c = np.ascontiguousarray
    T = {"x": a["L0_attn_x"]}
    T["ident"] = np.eye(128, dtype=f)
    T["ones_row"] = np.ones((1, 128), f)
    T["causal"] = np.triu(np.full((128, 128), NEG, f), 1)
    T["tri"] = c(np.broadcast_to(np.tril(np.ones((15, 15), f), -1), (128, 15, 15)))
    T["w0_lin"] = c(np.stack([a["L0_attn_" + n].T for n in ("Wq", "Wk", "Wv", "Wa", "Wb")], 1))
    T["w0_g"] = a["L0_ffn_Wg"]
    T["w0_e"] = c(a["L0_ffn_We"].transpose(1, 0, 2))
    T["w0_be"] = a["L0_ffn_be"]
    T["w1_qkv"] = c(np.stack([a["L1_attn_" + n] for n in ("Wq", "Wk", "Wv")], 1))
    T["w1_o"] = c(a["L1_attn_Wo"].reshape(8, 128, 128).transpose(1, 0, 2))
    T["w1_bo"] = a["L1_attn_bo"][None]
    T["w1_r"] = a["L1_ffn_router_W"]
    T["w1_rb"] = a["L1_ffn_router_b"][None]
    T["w1_e1"] = c(np.concatenate([a["L1_ffn_eW1"], a["L1_ffn_sW1"][None]]).transpose(1, 0, 2))
    T["w1_eb1"] = c(np.concatenate([a["L1_ffn_eb1"], a["L1_ffn_sb1"][None]]).T)
    T["w1_e2"] = c(np.concatenate([a["L1_ffn_eW2"], a["L1_ffn_sW2"][None]]).transpose(1, 0, 2))
    T["w1_eb2"] = c(np.concatenate([a["L1_ffn_eb2"], a["L1_ffn_sb2"][None]]))

    def padded_out(wo, bo):
        p = np.zeros((4, GROW, 4, 128), f)
        p[:, 0:DH] = wo.reshape(4, 4, DH, 128).transpose(1, 2, 0, 3)
        p[0, DH, 0] = bo
        return p.reshape(128, 4, 128)

    T["w2_qk"] = c(np.concatenate([a["L2_attn_Wq"].T, a["L2_attn_Wk"].T], 1))
    T["w2_v"] = c(a["L2_attn_Wv"].T)
    T["w2_ln"] = c(np.stack([np.repeat(a["L2_attn_" + n], HEADS) for n in ("qln_g", "kln_g", "qln_b", "kln_b")], 1))
    T["w2_o"] = padded_out(a["L2_attn_Wo"].T, a["L2_attn_bo"])
    across = np.arange(128).reshape(HEADS, DH).T.ravel()
    T["w2_fe"] = c(np.concatenate([a["L2_ffn_Wq"][..., across], a["L2_ffn_Wk"][..., across], a["L2_ffn_Wv"]], 2
                                  ).transpose(1, 0, 2))
    T["w2_fb"] = c(np.stack([a["L2_ffn_b" + n][:, across].T for n in "qk"], 1))
    T["w2_fbv"] = a["L2_ffn_bv"]
    T["w2_g1"] = a["L2_ffn_Wg1"]
    T["w2_b1"] = a["L2_ffn_bg1"][:, None]
    T["w2_g2"] = a["L2_ffn_Wg2"]
    T["w2_b2"] = c(np.broadcast_to(a["L2_ffn_bg2"], (128, 4)))
    T["w2_fo"] = padded_out(a["L2_ffn_Wo"], a["L2_ffn_bo"])

    T["w3_lin"] = c(np.stack([a["L3_attn_Wq"].T[:, across], a["L3_attn_Wk"].T[:, across], a["L3_attn_Wv"].T], 1))
    T["w3_o"] = padded_out(a["L3_attn_Wo"].T, a["L3_attn_b_o"])
    T["w3_rt"] = c(a["L3_ffn_router"].T)
    for n in ("up", "gate"):
        both = np.concatenate([a["L3_ffn_" + n], a[f"L3_ffn_w_{n}_s"][None]])
        T["w3_" + n] = c(both.transpose(2, 0, 1))
    down = np.concatenate([a["L3_ffn_down"], a["L3_ffn_w_down_s"][None]])
    T["w3_down"] = c(down.reshape(9, 128, 2, 128).transpose(3, 0, 2, 1).reshape(128, 9, 256))
    rk, rv = a["L3_attn_rel_k_emb"], a["L3_attn_rel_v_emb"]
    T["w3_relk"] = c(np.stack([np.repeat(rk[0], HEADS), np.repeat(rk[2 * MAX_REL], HEADS)], 1))
    clipped = np.clip(np.arange(BAND) - BAND // 2, -MAX_REL, MAX_REL) + MAX_REL
    off = np.zeros((HEADS, DH, HEADS, BAND), f)
    for h in range(HEADS):
        off[h, :, h, :] = rk[clipped].T
    T["w3_rk"] = c(off.reshape(128, HEADS * BAND)[across])
    band = np.zeros((BAND, GROW), f)
    band[:, 0:DH] = rv[clipped]
    T["w3_rvb"] = band
    blocks = S // 32
    for n, row in ((0, 0), (1, 2 * MAX_REL)):
        m = np.zeros((4, GROW, 4, GROW), f)
        for g in range(4):
            m[g, DH:DH + blocks, g, 0:DH] = rv[row]
        T[f"w3_rv{n}"] = m.reshape(128, 128)
    u, blk = np.arange(blocks)[:, None], np.arange(S)[None] // 32
    for n, far in ((0, u < blk - 1), (1, u > blk + 1)):
        m = np.zeros((4, GROW, S), f)
        m[:, DH:DH + blocks] = far
        T[f"w3_m{n}"] = m.reshape(128, S)
    r, p = np.arange(BAND)[:, None] - BAND // 2, np.arange(128)[None] % 32
    T["w3_ma"] = ((r + p >= -32) & (r + p < 64)).astype(f)
    sel = np.zeros((4, GROW, 4, GROW), f)
    for g in range(4):
        sel[g, range(DH), g, range(DH)] = 1
        sel[g, DH:DH + blocks, g, DH] = 1
    T["w3_sel"] = sel.reshape(128, 128)
    return T


def kernel(**inputs):
    import concourse.bacc as bacc
    from concourse.bass_utils import run_bass_kernel_spmd

    arrays = laid_out(inputs)
    nc = bacc.Bacc("TRN2", target_bir_lowering=False, num_devices=1)
    T = {n: nc.dram_tensor(f"in_{n}", v.shape, mybir.dt.from_np(v.dtype), kind="ExternalInput").ap()
         for n, v in arrays.items()}
    out = nc.dram_tensor("out_x", (B, S, D), mybir.dt.float32, kind="ExternalOutput").ap()
    build(nc, T, out)
    r = run_bass_kernel_spmd(nc, [{f"in_{n}": v for n, v in arrays.items()}], core_ids=[0])
    return r.results[0]["out_x"]
```

```python
import concourse.bass as bass
from concourse import mybir
from contextlib import ExitStack
import numpy as np

B, S, D = 4, 512, 128
NTT = S // 128
EPS = 1e-5
L1_HEADS, L1_DH = 16, 64
HEADS, DH = 16, 8
L1_EXPERTS = 16
L0_EXPERTS = 8
L3_EXPERTS, L3_HID = 9, 256
MAX_REL = 32
BAND = 127
WIN = 96
A_ROW = 224
GROW = 32
NPARTS = 3
STACK = NPARTS * NPARTS * DH
NEG = -1e30


class Steps:

    def __init__(self, eng, sem):
        self.eng, self.sem, self.n = eng, sem, 0

    def add(self, ins):
        ins.then_inc(self.sem, 1)
        self.n += 1

    def settle(self):
        self.eng.wait_ge(self.sem, self.n)


class Jobs:

    def __init__(self, banks, filled, emptied, jobs):
        self.banks, self.filled, self.emptied = banks, filled, emptied
        self.names = [n for n, _ in jobs]
        self.engines = [e for _, e in jobs]

    def bank(self, name):
        return self.banks[self.names.index(name) % len(self.banks)]

    def n_filled(self, name):
        return self.names.index(name) + 1

    def n_emptied(self, j):
        return self.emptied[self.engines[j]], self.engines[:j + 1].count(self.engines[j])

    def wait_free(self, pe, name):
        j = self.names.index(name) - len(self.banks)
        if j >= 0:
            pe.wait_ge(*self.n_emptied(j))

    def wait_filled(self, eng, name):
        eng.wait_ge(self.filled, self.n_filled(name))

    def wait_emptied(self, eng, name):
        eng.wait_ge(*self.n_emptied(self.names.index(name)))

    def wait_all_free(self, pe):
        for e in sorted(set(self.engines)):
            pe.wait_ge(self.emptied[e], self.engines.count(e))


def build(nc, T, out):
    f32, bf16 = mybir.dt.float32, mybir.dt.bfloat16
    ALU, ACT, AX = mybir.AluOpType, mybir.ActivationFunctionType, mybir.AxisListType

    ctx = ExitStack()
    with ctx:
        def sb(name, shape, dt=f32):
            return ctx.enter_context(nc.sbuf_tensor(name, shape, dt))

        wa = sb("wa", [128, 5632])
        wb = sb("wb", [128, 10624])
        x_all = sb("x_all", [128, B, NTT, D])
        ident = sb("ident", [128, 128])
        ident_b = sb("ident_b", [128, 128], bf16)
        ones_row = sb("ones_row", [1, 128])
        causal_f = sb("causal_f", [128, 128])
        causal_b = sb("causal_b", [128, 128], bf16)
        tri = sb("tri", [128, 15, 15])
        arena = sb("arena", [128, 32768], bf16)
        arena_f = arena[:, :].bitcast(f32)
        pt = sb("pt", [128, 4, NTT, S])
        pt_f = pt[:, :, :, :].rearrange("p a b c -> p (a b c)")
        prob = sb("prob", [128, 3, S])
        prob_f = prob[:, :, :].rearrange("p a b -> p (a b)")
        xn = sb("xn", [128, NTT, D])
        xnT = sb("xnT", [128, S])
        acc = sb("acc", [128, NTT, D])
        acc_f = acc[:, :, :].rearrange("p t d -> p (t d)")
        tmp = sb("tmp", [128, 2, NTT, D])
        ctx_raw = sb("ctx_raw", [128, S])
        ctx_n = sb("ctx_n", [128, 2, S])
        v_pad = sb("v_pad", [128, NTT, HEADS, GROW])
        negmax = sb("negmax", [128, 64])
        rowsum = sb("rowsum", [128, 64])
        ln_st = sb("ln_st", [128, NTT, 6])
        ln_mv = sb("ln_mv", [128, NTT, 2])
        ln_rs = sb("ln_rs", [128, NTT])
        minus_half = sb("minus_half", [128, 1])
        lg = sb("lg", [128, NTT, 16])
        ex = sb("ex", [128, NTT, 16])
        gate = sb("gate", [128, NTT, 16])
        rank = sb("rank", [128, NTT, 16])
        red = sb("red", [128, NTT])
        small = sb("small", [128, 64])

        def ps(name):
            return ctx.enter_context(nc.psum_tensor(name, [128, 512], f32))

        bank_s = [ps(f"bank_s{i}") for i in range(3)]
        bank_t = [ps(f"bank_t{i}") for i in range(2)]
        bank_v = ps("bank_v")
        bank_m = [ps(f"bank_m{i}") for i in range(2)]
        bank_o = bank_m[1]
        score_banks = bank_s + bank_m[0:1]

        kept = {}
        for n in ("loaded", "w0", "w1", "w2", "w3", "consts", "stored", "go0", "go1", "go2", "go3",
                  "causal_set", "q1_zeroed", "stack_zeroed", "keys_zeroed", "centred", "rk_ready", "v_set",
                  "zeroed", "half_set", "first_stats", "first_var", "first_step", "first_rstd", "first_xn",
                  "v3_set"):
            kept[n] = ctx.enter_context(nc.semaphore(n))
        s_esent = [ctx.enter_context(nc.semaphore(f"s_esent{i}")) for i in range(2)]
        s_askew = [ctx.enter_context(nc.semaphore(f"s_askew{i}")) for i in range(2)]
        SENT, SKEWED = 16 * 4 * NTT // 2, 16 * HEADS // 2
        cleared = {}

        def sem(name):
            cleared[name] = ctx.enter_context(nc.semaphore(name))
            return cleared[name]

        fin, s_resumed = sem("fin"), sem("s_resumed")
        s_dve, s_pool = sem("s_dve"), sem("s_pool")
        s_var, s_rstd, s_xn = sem("s_var"), sem("s_rstd"), sem("s_xn")
        a_fill, a_act, a_dve = sem("a_fill"), sem("a_act"), sem("a_dve")
        f_fill, f_act, f_dve = sem("f_fill"), sem("f_act"), sem("f_dve")
        r_fill, r_dve = sem("r_fill"), sem("r_dve")
        s_gate, s_lgsub, s_exp, s_acc, s_silu, s_e1 = (sem(n) for n in
                                                      ("s_gate", "s_lgsub", "s_exp", "s_acc", "s_silu", "s_e1"))
        att = {n: sem(n) for n in ("scored", "maxed", "exped", "turned", "ev_dve", "ev_act", "pv", "craw",
                                   "inverted", "projected")}
        s_round, s_rest, s_sent = sem("s_round"), sem("s_rest"), sem("s_sent")
        s_pooled, s_mixed, s_squared, s_normed = sem("s_pooled"), sem("s_mixed"), sem("s_squared"), sem("s_normed")
        s_hvar, s_hrstd, s_taken = sem("s_hvar"), sem("s_hrstd"), sem("s_taken")
        s_offsets, s_tanh, s_aturned, s_amasked = (sem(n) for n in ("s_offsets", "s_tanh", "s_aturned", "s_amasked"))
        s_band, s_bmasked, s_numer, s_normal = (sem(n) for n in ("s_band", "s_bmasked", "s_numer", "s_normal"))
        r_act = sem("r_act")
        s_near = [sem(f"s_near{i}") for i in range(2)]
        s_written = [sem(f"s_written{i}") for i in range(3)]
        s_first_heads = sem("s_first_heads")
        s_stacked = [sem(f"s_stacked{i}") for i in range(2)]
        nums = [s.num for s in cleared.values()]
        assert nums == list(range(nums[0], nums[0] + len(nums)))
        clear_range = range(nums[0], nums[-1] + 1)

        block = ctx.enter_context(nc.Block())

        def iterations(eng, layer):
            return eng.Fori(0, B)

        def meet(eng, go, b):
            eng.drain().then_inc(fin, 1)
            eng.wait_ge(go, b + 1)

        def meet_sync(sp, go, b):
            meet(sp, go, b)
            sp.sem_inc(s_resumed, 1)
            sp.wait_ge(s_resumed, 1)

        def meet_and_clear(pool, go, b, others=4):
            pool.drain()
            pool.wait_ge(fin, others)
            pool.sem_clear(clear_range)
            pool.drain().then_inc(go, 1)
            pool.wait_ge(go, b + 1)

        def x_of(b):
            return x_all[:, bass.ds(b, 1), :, :].rearrange("p b t d -> p (b t) d")

        def flat(t3):
            return t3.rearrange("p t d -> p (t d)")

        def bank3(bank):
            return bank[:, :].rearrange("p (t d) -> p t d", t=NTT)

        def norm_stats(dve, b, settle, var):
            x = x_of(b)
            for t in range(NTT):
                ins = dve.bn_stats(ln_st[:, t, :], x[:, t, :])
                settle.add(ins)
            settle.settle()
            for t in range(NTT):
                dve.bn_aggr(ln_mv[:, t, :], ln_st[:, t, :]).then_inc(var, 1)
            dve.wait_ge(var, NTT)

        def norm_apply(dve, b, rstd, done):
            x = x_of(b)
            dve.wait_ge(rstd, 1)
            for t in range(NTT):
                dve.tensor_scalar(xn[:, t, :], x[:, t, :], ln_mv[:, t, 0:1], ln_rs[:, t:t + 1],
                                  ALU.subtract, ALU.mult).then_inc(done, 1)

        def inverse_deviation(pool, var, step, rstd):
            pool.wait_ge(var, NTT)
            pool.tensor_scalar(ln_rs[:, :], ln_mv[:, :, 1], EPS, None, ALU.add).then_inc(step, 1)
            pool.wait_ge(step, 1)
            pool.tensor_tensor(ln_rs[:, :], ln_rs[:, :], minus_half[:, 0:1].to_broadcast([128, NTT]), ALU.pow
                               ).then_inc(rstd, 1)

        def after(b):
            return (b + 1) % B

        class NextNorm:

            def __init__(self, dve, b, d):
                self.dve, self.b, self.d = dve, b, d

            def stats(self):
                norm_stats(self.dve, after(self.b), self.d, s_var)

            def apply(self):
                norm_apply(self.dve, after(self.b), s_rstd, s_xn)

        def turn_xn(pe, A):
            for t in range(NTT):
                last = pe.transpose(A.bank("X")[:, t * 128:(t + 1) * 128], xn[:, t, :], ident[:, :])
            last.then_inc(A.filled, 1)

        def evac(eng, A, name, dst, src=None, scale=None):
            A.wait_filled(eng, name)
            src = A.bank(name)[:, :] if src is None else src
            if eng is nc.scalar or A.engines[A.names.index(name)] == "act":
                ins = nc.scalar.activation(dst, src, ACT.Copy, scale=1.0 if scale is None else scale)
            elif scale is None:
                ins = nc.vector.tensor_copy(dst, src)
            else:
                ins = nc.vector.tensor_scalar(dst, src, scale, None, ALU.mult)
            ins.then_inc(A.emptied[A.engines[A.names.index(name)]], 1)

        def project(pe, A, name, w, rhs, n=S):
            A.wait_free(pe, name)
            pe.matmul(A.bank(name)[:, 0:n], w, rhs, start=True, stop=True).then_inc(A.filled, 1)

        def token_products(pe, A, name, rhs, width, lhs=None, bias=None):
            A.wait_free(pe, name)
            lhs = xnT if lhs is None else lhs
            for t in range(NTT):
                o = A.bank(name)[:, t * width:(t + 1) * width]
                last = pe.matmul(o, lhs[:, t * 128:(t + 1) * 128], rhs, start=True, stop=bias is None)
                if bias is not None:
                    last = pe.matmul(o, ones_row[0:1, :], bias, start=False, stop=True)
            last.then_inc(A.filled, 1)

        def top_k(dve, d, logits, T_, E, k, mask, cmp_a, cmp_b):
            mine = logits.unsqueeze(3).to_broadcast([128, T_, E, E])
            other = logits.unsqueeze(2).to_broadcast([128, T_, E, E])
            ca = cmp_a.rearrange("p (t e f) -> p t e f", t=T_, e=E)
            cb = cmp_b.rearrange("p (t e f) -> p t e f", t=T_, e=E)
            d.add(dve.tensor_tensor(ca, other, mine, ALU.is_gt))
            d.add(dve.tensor_tensor(cb, other, mine, ALU.is_ge))
            d.settle()
            for t in range(T_):
                d.add(dve.tensor_tensor(cb[:, t], cb[:, t], tri[:, 0:E, 0:E], ALU.mult))
            d.settle()
            d.add(dve.tensor_tensor(ca, ca, cb, ALU.max))
            d.settle()
            d.add(dve.tensor_reduce(rank[:, 0:T_, 0:E], ca, AX.X, ALU.add))
            d.settle()
            d.add(dve.tensor_scalar(mask, rank[:, 0:T_, 0:E], float(k) - 0.5, None, ALU.is_lt))

        def shifted(dve, d, logits, T_, E):
            d.add(dve.tensor_reduce(red[:, 0:T_], logits, AX.X, ALU.max))
            d.settle()
            dve.tensor_tensor(ex[:, 0:T_, 0:E], logits, red[:, 0:T_].unsqueeze(2).to_broadcast([128, T_, E]),
                              ALU.subtract).then_inc(s_lgsub, 1)

        def exp_logits(act, T_, E):
            act.wait_ge(s_lgsub, 1)
            act.activation(ex[:, 0:T_, 0:E], ex[:, 0:T_, 0:E], ACT.Exp).then_inc(s_exp, 1)

        def gates(dve, d, T_, E, of_all):
            d.settle()
            dve.wait_ge(s_exp, 1)
            d.add(dve.tensor_tensor(gate[:, 0:T_, 0:E], ex[:, 0:T_, 0:E], gate[:, 0:T_, 0:E], ALU.mult))
            d.settle()
            d.add(dve.tensor_reduce(red[:, 0:T_], (ex if of_all else gate)[:, 0:T_, 0:E], AX.X, ALU.add))
            d.settle()
            d.add(dve.reciprocal(red[:, 0:T_], red[:, 0:T_]))
            d.settle()
            dve.tensor_tensor(gate[:, 0:T_, 0:E], gate[:, 0:T_, 0:E],
                              red[:, 0:T_].unsqueeze(2).to_broadcast([128, T_, E]), ALU.mult).then_inc(s_gate, 1)

        def gated(dve, F, e, first=0):
            F.wait_filled(dve, f"Y{e}")
            if e - 1 - first > 0:
                dve.wait_ge(s_acc, e - 1 - first)
            dst = acc[:, :, :] if e < first else tmp[:, e % 2]
            dve.tensor_tensor(dst, bank3(F.bank(f"Y{e}")), gate[:, :, e:e + 1].to_broadcast([128, NTT, D]),
                              ALU.mult).then_inc(F.emptied["dve"], 1)

        def add_up(pool, F, es, base):
            for e in es:
                i = e - (1 if base == "Y0" else 0)
                F.wait_emptied(pool, f"Y{e}")
                if i:
                    pool.wait_ge(s_acc, i)
                elif base is not None:
                    F.wait_emptied(pool, base)
                pool.tensor_tensor(acc[:, :, :], acc[:, :, :], tmp[:, e % 2], ALU.add).then_inc(s_acc, 1)

        def silu_tanh(act, n):
            act.wait_ge(s_acc, n)
            act.activation(flat(tmp[:, 0]), acc_f, ACT.Tanh, scale=0.5).then_inc(s_e1, 1)

        def silu(dve):
            dve.wait_ge(s_e1, 1)
            dve.scalar_tensor_tensor(acc_f, flat(tmp[:, 0]), 1.0, acc_f, ALU.add, ALU.mult).then_inc(s_silu, 1)
            dve.wait_ge(s_silu, 1)

        def residual(dve, d, b, src):
            d.add(dve.scalar_tensor_tensor(tmp[:, 1], src, 0.5, acc[:, :, :], ALU.mult, ALU.mult))
            d.settle()
            x = x_of(b)
            dve.tensor_tensor(x, x, tmp[:, 1], ALU.add)

        class Attention:

            LAG = 3

            def __init__(self, per_group, R, scores, pv, wo, blocks=lambda k: NTT, heads=HEADS,
                         unit=None, n_scores=4, by_rows=False, pt_held=False, outputs=1):
                self.s = att
                self.pt_held = pt_held
                self.banks = score_banks[0:n_scores]
                self.unit = unit or per_group * NTT
                self.by_rows = by_rows
                self.heads, self.per_group, self.R = heads, per_group, R
                self.scores, self.pv_products, self.wo, self.blocks = scores, pv, wo, blocks
                self.nt = heads * NTT
                self.groups = heads // per_group
                self.per_out = self.groups // outputs
                self.per = per_group * NTT
                self.units = self.per // self.unit
                self.steps = self.nt + 12

            def beside_pe(self, pe, tau):
                pass

            def beside_act(self, act, tau):
                pass

            def beside_dve(self, dve, tau):
                pass

            def wait_copied(self, eng, k):
                eng.wait_ge(self.s["ev_dve" if k % 2 == 0 else "ev_act"], k // 2 + 1)

            def at(self, tau, after):
                g, r = divmod(tau - after - self.LAG - (self.per - 1), self.per)
                return g if r == 0 and 0 <= g < self.groups else None

            def unit_at(self, tau, after):
                u, r = divmod(tau - after - self.LAG - (self.unit - 1), self.unit)
                return u if r == 0 and 0 <= u < self.nt // self.unit else None

            def number(self, g, m, i):
                return g * self.per + (i * self.per_group + m if self.by_rows else m * NTT + i)

            def copy_tile(self, eng, k):
                h, i = divmod(k, NTT)
                n = self.blocks(k)
                if self.pt_held and k < 2:
                    eng.wait_ge(s_rest, 4)
                if self.pt_held and k in (8, 9):
                    eng.wait_ge(s_sent, 32)
                eng.wait_ge(self.s["turned"], k + 1)
                if h >= 4:
                    eng.wait_ge(self.s["pv"], (k - 4 * NTT) // self.unit + 1)
                dst = pt[:, h % 4, 0:n, i * 128:(i + 1) * 128]
                src = bank_t[k % 2][:, 0:n * 128].rearrange("p (j i) -> p j i", j=n)
                if k % 2 == 0:
                    nc.vector.tensor_copy(dst, src).then_inc(self.s["ev_dve"], 1)
                else:
                    nc.scalar.activation(dst, src, ACT.Copy).then_inc(self.s["ev_act"], 1)

            def spread_sums(self, pe, g, bank):
                rows = 128 // self.per_group
                for i in range(NTT):
                    for m in range(self.per_group):
                        k = self.number(g, m, i)
                        last = pe.matmul(bank[rows * m:rows * m + rows, i * 128:(i + 1) * 128],
                                         rowsum[:, k % 64:k % 64 + 1].to_broadcast([128, rows]), ident[:, :],
                                         start=True, stop=True, skip_group_check=True)
                return last

            def pe(self, pe):
                s = self.s
                for tau in range(self.steps):
                    self.beside_pe(pe, tau)
                    if tau < self.nt:
                        n = len(self.banks)
                        if tau >= n:
                            pe.wait_ge(s["exped"], tau - n + 1)
                        self.scores(pe, tau, self.banks[tau % len(self.banks)]).then_inc(s["scored"], 1)
                    k = tau - self.LAG
                    if 0 <= k < self.nt:
                        pe.wait_ge(s["exped"], k + 1)
                        if k >= 2:
                            self.wait_copied(pe, k - 2)
                        for j in range(self.blocks(k)):
                            last = pe.transpose(bank_t[k % 2][:, j * 128:(j + 1) * 128],
                                                prob[:, k % 3, j * 128:(j + 1) * 128], ident[:, :])
                        last.then_inc(s["turned"], 1)
                    u = self.unit_at(tau, 2)
                    if u is not None:
                        self.wait_copied(pe, self.unit * (u + 1) - 1)
                        self.wait_copied(pe, self.unit * (u + 1) - 2)
                        g = u // self.units
                        if g >= len(self.R.banks):
                            self.R.wait_emptied(pe, f"R{g - len(self.R.banks)}")
                        self.pv_products(pe, u).then_inc(s["pv"], 1)
                    g = self.at(tau, 5)
                    if g is not None:
                        pe.wait_ge(s["inverted"], g + 1)
                        pe.wait_ge(s["craw"], g + 1)
                        self.spread_sums(pe, g, self.R.bank(f"R{g}")).then_inc(self.R.filled, 1)
                    g = self.at(tau, 8)
                    if g is not None:
                        self.R.wait_emptied(pe, f"R{g}")
                        if g == self.per_out:
                            pe.wait_ge(s_taken, 1)
                        for t in range(NTT):
                            last = pe.matmul(bank_o[:, t * 128:(t + 1) * 128], ctx_n[:, g % 2, t * 128:(t + 1) * 128],
                                             self.wo(g), start=(g % self.per_out == 0 and t == 0),
                                             stop=(g % self.per_out == self.per_out - 1),
                                             skip_group_check=True)
                        last.then_inc(s["projected"], 1)

            def act(self, act):
                s = self.s
                for tau in range(self.steps):
                    self.beside_act(act, tau)
                    k = tau - self.LAG
                    if 0 <= k < self.nt and k % 2 == 1:
                        self.copy_tile(act, k)
                    if tau < self.nt:
                        act.wait_ge(s["maxed"], tau + 1)
                        if tau >= 3:
                            act.wait_ge(s["turned"], tau - 2)
                        n = self.blocks(tau) * 128
                        act.activation(prob[:, tau % 3, 0:n], self.banks[tau % len(self.banks)][:, 0:n], ACT.Exp,
                                       bias=negmax[:, tau % 64:tau % 64 + 1], accum_out=rowsum[:, tau % 64:tau % 64 + 1]
                                       ).then_inc(s["exped"], 1)
                    g = self.at(tau, 3)
                    if g is not None:
                        act.wait_ge(s["pv"], (g + 1) * self.units)
                        if g >= 1:
                            self.R.wait_emptied(act, f"R{g - 1}")
                        act.activation(ctx_raw[:, :], self.R.bank(f"R{g}")[:, :], ACT.Copy).then_inc(s["craw"], 1)

            def dve(self, dve, norm=None):
                s = self.s
                for tau in range(self.steps):
                    self.beside_dve(dve, tau)
                    if norm and tau == self.nt + 1:
                        norm.stats()
                    if norm and tau == self.nt + 7:
                        norm.apply()
                    if tau < self.nt:
                        dve.wait_ge(s["scored"], tau + 1)
                        n = self.blocks(tau) * 128
                        dve.tensor_reduce(negmax[:, tau % 64:tau % 64 + 1], self.banks[tau % len(self.banks)][:, 0:n], AX.X, ALU.max,
                                          negate=True).then_inc(s["maxed"], 1)
                    k = tau - self.LAG
                    if 0 <= k < self.nt and k % 2 == 0:
                        self.copy_tile(dve, k)
                    g = self.at(tau, 3)
                    if g is not None:
                        at = g * self.per % 64
                        cols = rowsum[:, at:at + self.per]
                        dve.wait_ge(s["exped"], (g + 1) * self.per)
                        dve.reciprocal(cols, cols).then_inc(s["inverted"], 1)
                    g = self.at(tau, 6)
                    if g is not None:
                        dve.wait_ge(s["craw"], g + 1)
                        self.R.wait_filled(dve, f"R{g}")
                        if g >= 2:
                            dve.wait_ge(s["projected"], g - 1)
                        dve.tensor_tensor(ctx_n[:, g % 2, :], ctx_raw[:, :], self.R.bank(f"R{g}")[:, :],
                                          ALU.mult).then_inc(self.R.emptied["dve"], 1)

        def carve(base, spec, at=0):
            views = {}
            for name, shape in spec:
                n = int(np.prod(shape[1:]))
                v = base[0:shape[0], at:at + n]
                if len(shape) == 3:
                    v = v.rearrange("p (a b) -> p a b", a=shape[1])
                elif len(shape) == 4:
                    v = v.rearrange("p (a b c) -> p a b c", a=shape[1], b=shape[2])
                views[name] = v
                at += n
            assert at <= base.shape[1], (at, base.shape)
            return views

        spec0 = [(n, T[n].shape) for n in ("w0_lin", "w0_g", "w0_e", "w0_be")]
        spec2 = [(n, T[n].shape) for n in ("w2_qk", "w2_v", "w2_ln", "w2_o", "w2_fe", "w2_fb", "w2_fbv", "w2_g1",
                                           "w2_b1", "w2_g2", "w2_b2", "w2_fo")]
        spec1 = [(n, T[n].shape) for n in ("w1_qkv", "w1_o", "w1_bo", "w1_r", "w1_rb", "w1_e1", "w1_eb1", "w1_e2",
                                           "w1_eb2")]
        v2_pad = carve(wa, [("v2_pad", (128, NTT, HEADS, GROW))])["v2_pad"]
        w_a = {**carve(wa, spec0), **carve(wa, spec2, at=NTT * HEADS * GROW)}
        assert sum(int(np.prod(shape[1:])) for _, shape in spec0) <= NTT * HEADS * GROW
        w_b = carve(wb, spec1)
        w = {**w_a, **w_b}
        W3B = ("w3_lin", "w3_o", "w3_up", "w3_gate", "w3_down", "w3_rt", "w3_relk", "w3_rv0", "w3_rv1", "w3_rvb",
               "w3_m0", "w3_m1", "w3_ma", "w3_sel")
        late_views = carve(wb, [(n, T[n].shape) for n in W3B])

        def loads_sync(sp):
            sp.dma_start(x_all[:, :, :, :].rearrange("p b t d -> p (b t) d"),
                         T["x"].rearrange("b (t p) d -> p (b t) d", p=128)).then_inc(kept["loaded"], 16)
            for n in ("ident", "causal", "tri", "ones_row"):
                dst = {"ident": ident, "causal": causal_f, "tri": tri, "ones_row": ones_row}[n]
                sp.dma_start(dst[tuple(slice(None) for _ in dst.shape)], T[n]).then_inc(kept["consts"], 16)
            for key, spec in (("w0", spec0), ("w1", spec1), ("w2", spec2)):
                for n, _ in spec:
                    sp.dma_start(w[n], T[n]).then_inc(kept[key], 16)

        def wait_weights(eng, key, n):
            eng.wait_ge(kept[key], 16 * n)

        L0A = lambda: Jobs(bank_m, a_fill, {"act": a_act, "dve": a_dve},
                           [("X", "act"), ("LG", "dve"), ("Q", "act"), ("K", "act"), ("V", "dve"), ("GT", "dve"),
                            ("AK", "act"), ("B", "dve"), ("U", "dve")]
                           + [(f"Y{e}", "dve") for e in range(L0_EXPERTS)])
        q0, k0, ak0, v0 = (arena_f[:, i * S:(i + 1) * S] for i in range(4))
        u0 = arena_f[:, 4 * S:5 * S].rearrange("p (j d) -> p j d", j=NTT)
        gT = ctx_raw

        def l0_scores(pe, k, bank):
            return pe.matmul(bank[:, :], q0[:, k * 128:(k + 1) * 128], ak0, start=True, stop=True)

        def l0_attention():
            return Attention(1, None, l0_scores, None, None, heads=1)

        def layer0_tensor(pe):
            wait_weights(pe, "consts", 4)
            wait_weights(pe, "w0", len(spec0))
            pe.wait_ge(kept["first_xn"], NTT)
            with iterations(pe, 0) as b:
                A, M = L0A(), l0_attention()
                turn_xn(pe, A)
                A.wait_emptied(pe, "X")
                token_products(pe, A, "LG", w["w0_g"], L0_EXPERTS)
                project(pe, A, "Q", w["w0_lin"][:, 0, :], xnT[:, :])
                project(pe, A, "K", w["w0_lin"][:, 1, :], xnT[:, :])
                project(pe, A, "V", w["w0_lin"][:, 2, :], xnT[:, :])
                pe.wait_ge(s_gate, 1)
                A.wait_free(pe, "GT")
                for t in range(NTT):
                    last = pe.transpose(A.bank("GT")[0:L0_EXPERTS, t * 128:(t + 1) * 128],
                                        gate[:, t, 0:L0_EXPERTS], ident[:, :])
                last.then_inc(A.filled, 1)
                A.wait_emptied(pe, "K")
                project(pe, A, "AK", w["w0_lin"][:, 3, :], k0)
                A.wait_emptied(pe, "GT")
                token_products(pe, A, "B", w["w0_be"], D, lhs=gT[0:L0_EXPERTS])
                A.wait_emptied(pe, "V")
                token_products(pe, A, "U", w["w0_lin"][:, 4, :], D, lhs=v0)
                s = M.s
                A.wait_emptied(pe, "AK")
                for k in range(3):
                    l0_scores(pe, k, bank_s[k]).then_inc(s["scored"], 1)
                for k in range(NTT):
                    if k == 1:
                        pe.wait_ge(s["exped"], 1)
                        l0_scores(pe, 3, bank_s[0]).then_inc(s["scored"], 1)
                    pe.wait_ge(s["exped"], k + 1)
                    if k >= 2:
                        M.wait_copied(pe, k - 2)
                    for j in range(NTT):
                        last = pe.transpose(bank_t[k % 2][:, j * 128:(j + 1) * 128],
                                            prob[:, k % 3, j * 128:(j + 1) * 128], ident[:, :])
                    last.then_inc(s["turned"], 1)
                    for e in (2 * k, 2 * k + 1):
                        token_products(pe, A, f"Y{e}", w["w0_e"][:, e, :], D)
                A.wait_emptied(pe, "U")
                for i in range(NTT):
                    M.wait_copied(pe, i)
                    for j in range(NTT):
                        last = pe.matmul(bank_v[:, i * 128:(i + 1) * 128], pt[:, 0, j, i * 128:(i + 1) * 128],
                                         u0[:, j, :], start=(j == 0), stop=(j == NTT - 1))
                last.then_inc(s["pv"], 1)
                meet(pe, kept["go0"], b)

        def layer0_scalar(act):
            wait_weights(act, "consts", 4)
            with iterations(act, 0) as b:
                A, M = L0A(), l0_attention()
                evac(act, A, "X", xnT[:, :])
                evac(act, A, "Q", q0)
                exp_logits(act, NTT, L0_EXPERTS)
                evac(act, A, "K", k0)
                evac(act, A, "AK", ak0)
                s = M.s
                for tau in range(NTT + 2):
                    if tau < NTT:
                        act.wait_ge(s["maxed"], tau + 1)
                        if tau >= 3:
                            act.wait_ge(s["turned"], tau - 2)
                        act.activation(prob[:, tau % 3, :], bank_s[tau % 3][:, :], ACT.Exp,
                                       bias=negmax[:, tau % 64:tau % 64 + 1], accum_out=rowsum[:, tau % 64:tau % 64 + 1]
                                       ).then_inc(s["exped"], 1)
                    if tau >= 2 and tau % 2 == 1:
                        M.copy_tile(act, tau - 2)
                silu_tanh(act, L0_EXPERTS)
                meet(act, kept["go0"], b)

        def layer0_vector(dve):
            wait_weights(dve, "loaded", 1)
            wait_weights(dve, "consts", 4)
            dve.tensor_copy(ident_b[:, :], ident[:, :])
            dve.tensor_copy(causal_b[:, :], causal_f[:, :]).then_inc(kept["causal_set"], 1)
            norm_stats(dve, 0, Steps(dve, kept["first_stats"]), kept["first_var"])
            norm_apply(dve, 0, kept["first_rstd"], kept["first_xn"])
            with iterations(dve, 0) as b:
                A, M = L0A(), l0_attention()
                d = Steps(dve, s_dve)
                norm = NextNorm(dve, b, d)
                E = L0_EXPERTS
                evac(dve, A, "LG", lg[:, :, 0:E], A.bank("LG")[:, 0:NTT * E].rearrange("p (t e) -> p t e", t=NTT))
                A.wait_emptied(dve, "LG")
                shifted(dve, d, lg[:, :, 0:E], NTT, E)
                n = NTT * E * E
                top_k(dve, d, lg[:, :, 0:E], NTT, E, 2, gate[:, :, 0:E], prob_f[:, 0:n], prob_f[:, n:2 * n])
                evac(dve, A, "V", v0)
                gates(dve, d, NTT, E, of_all=False)
                evac(dve, A, "GT", gT[0:E, :], A.bank("GT")[0:E, :])
                evac(dve, A, "B", acc[:, :, :], bank3(A.bank("B")))
                evac(dve, A, "U", u0, bank3(A.bank("U")))
                s = M.s

                def negated_max(k):
                    dve.wait_ge(s["scored"], k + 1)
                    dve.tensor_reduce(negmax[:, k:k + 1], bank_s[k % 3][:, :], AX.X, ALU.max, negate=True
                                      ).then_inc(s["maxed"], 1)

                for k in range(3):
                    negated_max(k)
                for k in range(NTT):
                    if k == 1:
                        negated_max(3)
                    if k % 2 == 0:
                        M.copy_tile(dve, k)
                    for e in (2 * k, 2 * k + 1):
                        gated(dve, A, e)
                norm.stats()
                silu(dve)
                norm.apply()
                dve.wait_ge(s["pv"], 1)
                dve.wait_ge(s["exped"], NTT)
                d.add(dve.reciprocal(rowsum[:, 0:NTT], rowsum[:, 0:NTT]))
                d.settle()
                d.add(dve.tensor_tensor(tmp[:, 0], bank3(bank_v),
                                        rowsum[:, 0:NTT].unsqueeze(2).to_broadcast([128, NTT, D]), ALU.mult))
                d.settle()
                residual(dve, d, b, tmp[:, 0])
                meet(dve, kept["go0"], b)

        def layer0_gpsimd(pool):
            pool.memset(minus_half[:, :], -0.5).then_inc(kept["half_set"], 1)
            pool.wait_ge(kept["half_set"], 1)
            inverse_deviation(pool, kept["first_var"], kept["first_step"], kept["first_rstd"])
            with iterations(pool, 0) as b:
                A = L0A()
                add_up(pool, A, range(L0_EXPERTS), "B")
                inverse_deviation(pool, s_var, s_pool, s_rstd)
                meet_and_clear(pool, kept["go0"], b, others=3)

        QK1 = [f"{m}{c}" for c in range(8) for m in "QK"]
        all_banks = bank_m + bank_s + bank_t + [bank_v]
        L1A = lambda: Jobs(all_banks, a_fill, {"act": a_act, "dve": a_dve},
                           [("X", "act"), ("LG", "dve")]
                           + [(n, "act" if n[0] == "Q" else "dve") for n in QK1]
                           + [(f"V{t}{i}", "dve" if i else "act") for t in range(NTT) for i in range(2)]
                           + [("H0", "act"), ("GT", "dve"), ("B", "dve")]
                           + [j for e in range(L1_EXPERTS)
                              for j in ([(f"H{e + 1}", "act")] if e + 1 < L1_EXPERTS else []) + [(f"Y{e}", "dve")]])
        L1R = lambda: Jobs([bank_v], r_fill, {"dve": r_dve}, [(f"R{g}", "dve") for g in range(8)])
        q1 = arena_f[:, 0:16 * S].rearrange("p (h s) -> p h s", h=L1_HEADS)
        k1 = arena_f[:, 16 * S:24 * S].rearrange("p (c s) -> p c s", c=8)
        v1 = arena_f[:, 24 * S:32 * S].rearrange("p (t n) -> p t n", t=NTT)
        hid = pt[:, 0]

        def l1_scores(pe, k, bank):
            h, i = divmod(k, NTT)
            return pe.matmul(bank[:, :], q1[:, h, i * 128:(i + 1) * 128], k1[:, h // 2, :], start=True, stop=True)

        def l1_pv(pe, g):
            for j in range(NTT):
                for m in range(2):
                    h = 2 * g + m
                    last = pe.matmul(bank_v[64 * m:64 * m + 64, :], v1[:, j, h * 64:(h + 1) * 64], pt[:, h % 4, j, :],
                                     start=(j == 0), stop=(j == NTT - 1), skip_group_check=True)
            return last

        def l1_attention():
            return Attention(2, L1R(), l1_scores, l1_pv, lambda g: w["w1_o"][:, g, :])

        def layer1_tensor(pe):
            wait_weights(pe, "w1", len(spec1))
            with iterations(pe, 1) as b:
                A, M = L1A(), l1_attention()
                turn_xn(pe, A)
                A.wait_emptied(pe, "X")
                token_products(pe, A, "LG", w["w1_r"], 15, bias=w["w1_rb"])
                for n in QK1:
                    c = int(n[1:])
                    project(pe, A, n, w["w1_qkv"][:, "QK".index(n[0]), c * 128:(c + 1) * 128], xnT[:, :])
                for t in range(NTT):
                    for i in range(2):
                        A.wait_free(pe, f"V{t}{i}")
                        pe.matmul(A.bank(f"V{t}{i}")[:, :], xnT[:, t * 128:(t + 1) * 128],
                                  w["w1_qkv"][:, 2, i * 512:(i + 1) * 512], start=True, stop=True
                                  ).then_inc(A.filled, 1)
                project(pe, A, "H0", w["w1_e1"][:, 0, :], xnT[:, :])
                pe.wait_ge(s_gate, 1)
                A.wait_free(pe, "GT")
                for t in range(NTT):
                    last = pe.transpose(A.bank("GT")[0:16, t * 128:(t + 1) * 128], gate[:, t, :], ident[:, :])
                last.then_inc(A.filled, 1)
                A.wait_emptied(pe, "GT")
                token_products(pe, A, "B", w["w1_eb2"], D, lhs=gT[0:16])
                for e in range(L1_EXPERTS):
                    if e + 1 < L1_EXPERTS:
                        project(pe, A, f"H{e + 1}", w["w1_e1"][:, e + 1, :], xnT[:, :])
                    A.wait_emptied(pe, f"H{e}")
                    token_products(pe, A, f"Y{e}", w["w1_e2"][:, e, :], D, lhs=hid[:, e % 4, :])
                A.wait_all_free(pe)
                M.pe(pe)
                for t in range(NTT):
                    last = pe.matmul(bank_o[:, t * 128:(t + 1) * 128], ones_row[0:1, :], w["w1_bo"],
                                     start=False, stop=True, skip_group_check=True)
                last.then_inc(M.s["projected"], 1)
                meet(pe, kept["go1"], b)

        def layer1_scalar(act):
            wait_weights(act, "w1", len(spec1))
            with iterations(act, 1) as b:
                A, M = L1A(), l1_attention()
                evac(act, A, "X", xnT[:, :])
                act.wait_ge(kept["q1_zeroed"], 1)
                for n in QK1:
                    if n[0] == "Q":
                        A.wait_filled(act, n)
                        for m in range(2):
                            rows = slice(64 * m, 64 * m + 64)
                            last = act.activation(q1[rows, 2 * int(n[1:]) + m, :], A.bank(n)[rows, :], ACT.Copy,
                                                  scale=L1_DH ** -0.5)
                        last.then_inc(a_act, 1)
                    if n == "Q1":
                        exp_logits(act, NTT, 15)
                for t in range(NTT):
                    evac(act, A, f"V{t}0", v1[:, t, 0:512])
                for e in range(L1_EXPERTS):
                    if e >= 4:
                        A.wait_filled(act, f"Y{e - 4}")
                    A.wait_filled(act, f"H{e}")
                    act.activation(hid[:, e % 4, :], A.bank(f"H{e}")[:, :], ACT.Relu, bias=w["w1_eb1"][:, e:e + 1]
                                   ).then_inc(A.emptied["act"], 1)
                silu_tanh(act, L1_EXPERTS)
                M.act(act)
                meet(act, kept["go1"], b)

        def layer1_vector(dve):
            with iterations(dve, 1) as b:
                A, M = L1A(), l1_attention()
                d = Steps(dve, s_dve)
                norm = NextNorm(dve, b, d)
                E = 15
                evac(dve, A, "LG", lg[:, :, 0:E], A.bank("LG")[:, 0:NTT * E].rearrange("p (t e) -> p t e", t=NTT))
                A.wait_emptied(dve, "LG")
                shifted(dve, d, lg[:, :, 0:E], NTT, E)
                n = NTT * E * E
                vp = v_pad[:, :, :, :].rearrange("p a b c -> p (a b c)")
                top_k(dve, d, lg[:, :, 0:E], NTT, E, 3, gate[:, :, 0:E], vp[:, 0:n], vp[:, n:2 * n])
                d.add(dve.memset(gate[:, :, 15:16], 1.0))
                for c in range(8):
                    evac(dve, A, f"K{c}", k1[:, c, :])
                for t in range(NTT):
                    evac(dve, A, f"V{t}1", v1[:, t, 512:1024])
                gates(dve, d, NTT, E, of_all=True)
                evac(dve, A, "GT", gT[0:16, :], A.bank("GT")[0:16, :])
                evac(dve, A, "B", acc[:, :, :], bank3(A.bank("B")))
                for e in range(L1_EXPERTS):
                    gated(dve, A, e)
                silu(dve)
                M.dve(dve, norm)
                dve.wait_ge(M.s["projected"], M.groups + 1)
                residual(dve, d, b, bank3(bank_o))
                meet(dve, kept["go1"], b)

        def layer1_gpsimd(pool):
            pool.memset(arena_f[:, 0:16 * S], 0.0).then_inc(kept["q1_zeroed"], 1)
            with iterations(pool, 1) as b:
                add_up(pool, L1A(), range(L1_EXPERTS), "B")
                inverse_deviation(pool, s_var, s_pool, s_rstd)
                meet_and_clear(pool, kept["go1"], b, others=3)

        scratch_t = nc.dram_tensor("qk_parts", (4, NPARTS, 2, 128, S), bf16)
        scratch = scratch_t.ap()

        def stack(slot):
            return arena[:, slot * HEADS * S:(slot + 1) * HEADS * S].rearrange("p (h s) -> p h s", h=HEADS)

        def send_parts(sp, version, parts, ready, n, stored):
            sp.wait_ge(ready, n)
            sp.dma_start(scratch[version].rearrange("a q p s -> p (a q) s"), parts).then_inc(stored, 16)

        def fetch_stack(sp, version, which, slot, is_query, done, h0=0, h1=HEADS):
            for j in range(NPARTS):
                part, step = (j, 0) if is_query else (0, 2 * 128 * S)
                src = bass.AP(scratch_t, ((version * NPARTS + part) * 2 + which) * 128 * S + h0 * S,
                              [[step, NPARTS], [HEADS * S, DH], [1, (h1 - h0) * S]])
                dst = stack(slot)[j * NPARTS * DH:(j + 1) * NPARTS * DH, h0:h1].rearrange("p h s -> p (h s)")
                sp.dma_start(dst, src).then_inc(done, 16)

        N_FETCH = 16 * NPARTS

        class Split:

            def __init__(self, number, whole, parts):
                self.n, self.whole, self.parts = number, whole, parts

            def act_step(self, act, i):
                if i:
                    act.wait_ge(s_rest, 2 * self.n + 1)
                act.activation(self.parts[:, i], self.whole, ACT.Copy).then_inc(s_round, 1)

            def act(self, act):
                for i in range(2):
                    self.act_step(act, i)

            def dve_step(self, dve, i):
                dve.wait_ge(s_round, 2 * self.n + i + 1)
                if i:
                    dve.wait_ge(s_rest, 2 * self.n + 1)
                dst = self.parts[:, 2] if i else self.whole
                dve.tensor_tensor(dst, self.whole, self.parts[:, i], ALU.subtract).then_inc(s_rest, 1)

            def dve(self, dve):
                for i in range(2):
                    self.dve_step(dve, i)

        def part_view(words):
            return words.bitcast(bf16).rearrange("p (a n) -> p a n", a=NPARTS)

        L2A = lambda: Jobs(all_banks, a_fill, {"act": a_act, "dve": a_dve, "norm": s_normed},
                           [("X", "act"), ("P1", "dve"), ("P2", "dve"), ("QK0", "norm"), ("QK1", "norm"), ("VA", "act"),
                            ("WT", "dve"), ("FQ", "dve"), ("FK", "dve"), ("FV", "act"), ("QT", "act"), ("KT", "dve")])
        v_banks = [bank_v, bank_m[0]]
        L2R = lambda: Jobs(v_banks, r_fill, {"dve": r_dve}, [(f"R{g}", "dve") for g in range(8)])
        heads_qk = pt_f[:, 0:1024]
        heads_sq = pt_f[:, 1024:2048]
        whole2 = [pt_f[:, 2048:3072], pt_f[:, 3072:4096]]
        parts2 = [part_view(pt_f[:, 4096:5632]), part_view(pt_f[:, 5632:7168])]
        mixed_w = pt_f[:, 7168:7552]
        h_sum, h_var = pt_f[:, 7552:7680], pt_f[:, 7680:7808]
        pooled, hidden1, mixed_b, prod_b = small[:, 0:1], small[:, 1:2], small[:, 2:4], small[:, 4:12]
        head_means = small[:, 16:48]
        ln_scaled = small[:, 48:52]

        def l2_place(k):
            g, r = divmod(k, 4 * NTT)
            i, m = divmod(r, 4)
            return g // 4, 4 * (g % 4) + m, i

        def l2_scores(pe, k, bank):
            causal, h, i = l2_place(k)
            n = (i + 1) * 128 if causal else S
            last = pe.matmul(bank[:, 0:n], stack(2 * causal)[:, h, i * 128:(i + 1) * 128],
                             stack(2 * causal + 1)[:, h, 0:n], start=True, stop=not causal)
            if causal:
                last = pe.matmul(bank[:, i * 128:n], ident_b[:, :], causal_b[:, :], start=False, stop=True)
            return last

        def l2_pv(pe, u):
            g, i = divmod(u, NTT)
            causal = g // 4
            n = i + 1 if causal else NTT
            values = v2_pad if causal else v_pad
            for j in range(n):
                for m in range(4):
                    last = pe.matmul(v_banks[g % 2][GROW * m:GROW * (m + 1), i * 128:(i + 1) * 128],
                                     values[:, j, 4 * (g % 4) + m, :], pt[:, u % 4, j, m * 128:(m + 1) * 128],
                                     start=(j == 0), stop=(j == n - 1), skip_group_check=True)
            return last

        class TwoAttentions(Attention):

            FIRST_OUT = 64 + 8 + 3 + 2

            def beside_pe(self, pe, tau):
                if tau == 16:
                    pe.wait_ge(s_stacked[0], 2 * N_FETCH)
                elif tau == 64:
                    pe.wait_ge(s_stacked[1], 2 * N_FETCH)

            def beside_act(self, act, tau):
                if tau == self.FIRST_OUT + 2:
                    act.wait_ge(s_taken, 1)
                    act.activation(flat(tmp[:, 0]), acc_f, ACT.Tanh, scale=0.5).then_inc(s_e1, 1)

            def beside_dve(self, dve, tau):
                if tau == self.FIRST_OUT:
                    dve.wait_ge(self.s["projected"], 4)
                    dve.tensor_copy(acc[:, :, :], bank3(bank_o)).then_inc(s_taken, 1)
                elif tau == self.FIRST_OUT + 4:
                    silu(dve)

        def l2_attention():
            return TwoAttentions(4, L2R(), l2_scores, l2_pv, lambda g: w["w2_o" if g >= 4 else "w2_fo"][:, g % 4, :],
                             blocks=lambda k: l2_place(k)[2] + 1 if l2_place(k)[0] else NTT, heads=2 * HEADS,
                             unit=4, n_scores=3, by_rows=True, pt_held=True, outputs=2)

        def layer2_tensor(pe):
            wait_weights(pe, "w2", len(spec2))
            pe.wait_ge(kept["v_set"], 4)
            pe.wait_ge(kept["centred"], 4)
            pe.wait_ge(kept["causal_set"], 1)
            with iterations(pe, 2) as b:
                A = L2A()
                turn_xn(pe, A)
                pe.wait_ge(s_pooled, 1)
                project(pe, A, "P1", w["w2_g1"], pooled, n=1)
                A.wait_emptied(pe, "P1")
                project(pe, A, "P2", hidden1.to_broadcast([128, 128]), w["w2_g2"], n=4)
                for i in range(2):
                    A.wait_free(pe, f"QK{i}")
                    for t in range(2):
                        last = pe.matmul(A.bank(f"QK{i}")[:, t * 256:(t + 1) * 256],
                                         xnT[:, (2 * i + t) * 128:(2 * i + t + 1) * 128], w["w2_qk"],
                                         start=True, stop=True)
                    last.then_inc(A.filled, 1)
                token_products(pe, A, "VA", w["w2_v"], D)
                pe.wait_ge(s_gate, 1)
                A.wait_free(pe, "WT")
                pe.transpose(A.bank("WT")[0:4, 0:128], gate[:, 0, 0:4], ident[:, :]).then_inc(A.filled, 1)
                pe.wait_ge(s_mixed, 1)
                project(pe, A, "FQ", mixed_w[:, 0:128], xnT[:, :])
                project(pe, A, "FK", mixed_w[:, 128:256], xnT[:, :])
                A.wait_free(pe, "FV")
                A.wait_emptied(pe, "WT")
                pe.wait_ge(s_mixed, 2)
                for t in range(NTT):
                    o = A.bank("FV")[:, t * 128:(t + 1) * 128]
                    pe.matmul(o, xnT[:, t * 128:(t + 1) * 128], mixed_w[:, 256:384], start=True, stop=False)
                    last = pe.matmul(o, gT[0:4, 0:128], w["w2_fbv"], start=False, stop=True)
                last.then_inc(A.filled, 1)
                A.wait_emptied(pe, "QK0")
                A.wait_emptied(pe, "QK1")
                for i, n in enumerate(("QT", "KT")):
                    A.wait_free(pe, n)
                    for t in range(NTT):
                        last = pe.transpose(A.bank(n)[:, t * 128:(t + 1) * 128],
                                            heads_qk[:, (2 * t + i) * 128:(2 * t + i + 1) * 128], ident[:, :])
                    last.then_inc(A.filled, 1)
                A.wait_all_free(pe)
                pe.wait_ge(s_first_heads, 2 * N_FETCH)
                l2_attention().pe(pe)
                meet(pe, kept["go2"], b)

        def layer2_scalar(act):
            wait_weights(act, "w2", len(spec2))
            act.wait_ge(kept["centred"], 4)
            with iterations(act, 2) as b:
                A = L2A()
                evac(act, A, "X", xnT[:, :])
                exp_logits(act, 1, 4)
                for i in range(2):
                    A.wait_filled(act, f"QK{i}")
                    act.activation(heads_sq[:, i * 512:(i + 1) * 512], A.bank(f"QK{i}")[:, :], ACT.Square
                                   ).then_inc(s_squared, 1)
                act.wait_ge(kept["v_set"], 4)
                evac(act, A, "VA", v2_pad[:, :, :, 0:DH],
                     A.bank("VA")[:, :].rearrange("p (t h d) -> p t h d", t=NTT, h=HEADS))
                act.wait_ge(s_hvar, 1)
                act.activation(h_var, h_var, ACT.Sqrt).then_inc(s_hrstd, 1)
                A.wait_emptied(act, "FQ")
                A.wait_emptied(act, "FK")
                Split(0, whole2[0], parts2[0]).act(act)
                act_copy = A.bank("FV")[:, :].rearrange("p (t h d) -> p t h d", t=NTT, h=HEADS)
                A.wait_filled(act, "FV")
                act.activation(v_pad[:, :, :, 0:DH], act_copy, ACT.Copy).then_inc(A.emptied["act"], 1)
                A.wait_filled(act, "QT")
                act.activation(whole2[1][:, 0:S], A.bank("QT")[:, :], ACT.Identity, bias=ln_scaled[:, 2:3],
                               scale=ln_scaled[:, 0:1]).then_inc(a_act, 1)
                A.wait_emptied(act, "QT")
                A.wait_emptied(act, "KT")
                Split(1, whole2[1], parts2[1]).act(act)
                l2_attention().act(act)
                meet(act, kept["go2"], b)

        def layer2_vector(dve):
            wait_weights(dve, "w2", len(spec2))
            scale2 = float(D) ** -0.25
            dve.memset(arena_f[64:128, 16 * S:32 * S], 0.0).then_inc(kept["keys_zeroed"], 1)
            heads_w = w["w2_qk"].rearrange("p (n d) -> p n d", d=DH)
            once = Steps(dve, kept["centred"])
            once.add(dve.tensor_scalar(ln_scaled, w["w2_ln"], scale2, None, ALU.mult))
            once.add(dve.tensor_reduce(head_means, heads_w, AX.X, ALU.add))
            once.settle()
            once.add(dve.tensor_scalar(head_means, head_means, 1.0 / DH, None, ALU.mult))
            once.settle()
            once.add(dve.tensor_tensor(heads_w, heads_w, head_means.unsqueeze(2).to_broadcast([128, 2 * HEADS, DH]),
                                       ALU.subtract))
            once.settle()
            with iterations(dve, 2) as b:
                A = L2A()
                d = Steps(dve, s_dve)
                norm = NextNorm(dve, b, d)
                A.wait_emptied(dve, "X")
                d.add(dve.tensor_reduce(pooled, xnT[:, :], AX.X, ALU.add))
                d.settle()
                dve.tensor_scalar(pooled, pooled, 1.0 / S, None, ALU.mult).then_inc(s_pooled, 1)
                A.wait_filled(dve, "P1")
                dve.tensor_scalar(hidden1, A.bank("P1")[:, 0:1], w["w2_b1"], 0.0, ALU.add, ALU.max
                                  ).then_inc(A.emptied["dve"], 1)
                A.wait_filled(dve, "P2")
                dve.tensor_tensor(lg[:, 0, 0:4], A.bank("P2")[:, 0:4], w["w2_b2"], ALU.add
                                  ).then_inc(A.emptied["dve"], 1)
                A.wait_emptied(dve, "P2")
                shifted(dve, d, lg[:, 0:1, 0:4], 1, 4)
                top_k(dve, d, lg[:, 0:1, 0:4], 1, 4, 2, gate[:, 0:1, 0:4], prob_f[:, 0:16], prob_f[:, 16:32])
                gates(dve, d, 1, 4, of_all=False)
                dve.wait_ge(s_gate, 1)

                def mix(cols):
                    for e in range(4):
                        if e == 0:
                            d.add(dve.tensor_scalar(mixed_w[:, cols], w["w2_fe"][:, 0, cols], gate[:, 0, 0:1], None,
                                                    ALU.mult))
                        else:
                            d.settle()
                            d.add(dve.scalar_tensor_tensor(mixed_w[:, cols], w["w2_fe"][:, e, cols],
                                                           gate[:, 0, e:e + 1], mixed_w[:, cols], ALU.mult, ALU.add))
                    d.settle()

                mix(slice(0, 256))
                pb = prod_b.rearrange("p (a e) -> p a e", a=2)
                dve.tensor_tensor(pb, w["w2_fb"], gate[:, 0:1, 0:4].to_broadcast([128, 2, 4]), ALU.mult
                                  ).then_inc(s_mixed, 1)
                dve.wait_ge(s_mixed, 1)
                d.add(dve.tensor_reduce(mixed_b, pb, AX.X, ALU.add))
                d.settle()
                evac(dve, A, "WT", gT[0:4, 0:128], A.bank("WT")[0:4, 0:128])
                dve.wait_ge(s_squared, 2)
                d.add(dve.tensor_reduce(h_var, heads_sq.rearrange("p (n d) -> p n d", d=DH), AX.X, ALU.add))
                d.settle()
                dve.tensor_scalar(h_var, h_var, 1.0 / DH, EPS, ALU.mult, ALU.add).then_inc(s_hvar, 1)
                A.wait_filled(dve, "FQ")
                dve.tensor_scalar(whole2[0][:, 0:S], A.bank("FQ")[:, :], mixed_b[:, 0:1], DH ** -0.5, ALU.add, ALU.mult
                                  ).then_inc(A.emptied["dve"], 1)
                A.wait_filled(dve, "FK")
                dve.tensor_scalar(whole2[0][:, S:2 * S], A.bank("FK")[:, :], mixed_b[:, 1:2], None, ALU.add
                                  ).then_inc(A.emptied["dve"], 1)
                mix(slice(256, 384))
                dve.sem_inc(s_mixed, 1)
                dve.wait_ge(s_hrstd, 1)
                A.wait_emptied(dve, "FK")
                first, second = Split(0, whole2[0], parts2[0]), Split(1, whole2[1], parts2[1])
                first.dve_step(dve, 0)
                d.add(dve.reciprocal(h_var, h_var))
                first.dve_step(dve, 1)
                d.settle()
                for i in range(2):
                    A.wait_filled(dve, f"QK{i}")
                    dve.tensor_tensor(heads_qk[:, i * 512:(i + 1) * 512].rearrange("p (n d h) -> p n h d", d=DH, h=HEADS),
                                      A.bank(f"QK{i}")[:, :].rearrange("p (n h d) -> p n h d", d=DH, h=HEADS),
                                      h_var[:, i * 64:(i + 1) * 64].rearrange("p (n h) -> p n h", h=HEADS)
                                      .unsqueeze(3).to_broadcast([128, 4, HEADS, DH]), ALU.mult
                                      ).then_inc(s_normed, 1)
                A.wait_filled(dve, "KT")
                dve.tensor_scalar(whole2[1][:, S:2 * S], A.bank("KT")[:, :], ln_scaled[:, 1:2], ln_scaled[:, 3:4],
                                  ALU.mult, ALU.add).then_inc(a_dve, 1)
                A.wait_emptied(dve, "KT")
                A.wait_emptied(dve, "QT")
                second.dve(dve)
                M = l2_attention()
                M.dve(dve, norm)
                dve.wait_ge(M.s["projected"], 8)
                residual(dve, d, b, bank3(bank_o))
                meet(dve, kept["go2"], b)

        def layer2_gpsimd(pool):
            pool.memset(arena_f[64:128, 0:16 * S], 0.0).then_inc(kept["stack_zeroed"], 1)
            pool.wait_ge(kept["stack_zeroed"], 1)
            for n, values in enumerate((v_pad, v2_pad)):
                pool.memset(values[:, :, :, :].rearrange("p a b c -> p (a b c)"), 0.0).then_inc(kept["v_set"], 1)
                pool.wait_ge(kept["v_set"], 2 * n + 1)
                pool.memset(values[:, :, :, DH:DH + 1].rearrange("p a b c -> p (a b) c"), 1.0
                            ).then_inc(kept["v_set"], 1)
                pool.wait_ge(kept["v_set"], 2 * n + 2)
            with iterations(pool, 2) as b:
                inverse_deviation(pool, s_var, s_pool, s_rstd)
                meet_and_clear(pool, kept["go2"], b)

        def load_weights(sp, spec, views, sem_):
            for n, _ in spec:
                sp.dma_start(views[n], T[n]).then_inc(sem_, 16)

        def layer2_sync(sp):
            sp.wait_ge(kept["go1"], B)
            load_weights(sp, [(n, None) for n in W3B], {n: late_views[n] for n in W3B}, kept["w3"])
            sp.wait_ge(kept["stack_zeroed"], 1)
            sp.wait_ge(kept["keys_zeroed"], 1)
            with iterations(sp, 2) as b:
                for i in range(2):
                    send_parts(sp, i, parts2[i].rearrange("p a (q s) -> p (a q) s", q=2), s_rest, 2 * i + 2, s_sent)
                    sp.wait_ge(s_sent, 16 * (i + 1))
                    if i == 0:
                        fetch_stack(sp, 0, 0, 0, True, s_first_heads, 0, 4)
                        fetch_stack(sp, 0, 1, 1, False, s_first_heads, 0, 4)
                    h0 = 4 if i == 0 else 0
                    fetch_stack(sp, i, 0, 2 * i, True, s_stacked[i], h0)
                    fetch_stack(sp, i, 1, 2 * i + 1, False, s_stacked[i], h0)
                meet_sync(sp, kept["go2"], b)

        E_ROW = HEADS * BAND
        A_SLOT = 32 + 128 * A_ROW
        offset_scores = nc.dram_tensor("offset_scores", (S, HEADS, BAND), f32)
        skewed = nc.dram_tensor("skewed_probs", (NTT, 4, A_SLOT), f32)
        spec3b = [(n, T[n].shape) for n in W3B]
        spec3a = [(n, T[n].shape) for n in ("w3_rk", "w3_part")]
        w3b = carve(wb, spec3b + [("masked0", (128, S)), ("masked1", (128, S))])
        w3a = carve(wa, spec3a + [("banded", (128, 2, NTT, 128)), ("bandedT", (BAND, 4, S)),
                               ("rk_rounded", (STACK, 64)), ("rk_stack", (STACK, 64)), ("near", (128, 2, 4, WIN))])
        rk_rounded, rk_stack = (w3a[n].bitcast(bf16)[:, 0:BAND] for n in ("rk_rounded", "rk_stack"))
        N_W3 = len(spec3a) + len(spec3b)

        L3E = 4 * NTT

        def offset_jobs(n):
            at = [k for k in range(4, 10)] + [k for k in range(10, 15) for _ in range(2)]
            return [j for j in range(L3E) if at[j] == n]

        L3A = lambda: Jobs(bank_m, a_fill, {"act": a_act, "dve": a_dve},
                           [("X", "act"), ("LG", "dve"), ("Q", "act"), ("K", "dve"), ("V", "act")]
                           + [(f"E{j}", "act") for j in range(L3E)])
        L3F = lambda: Jobs(bank_s + bank_t, f_fill, {"act": f_act, "dve": f_dve},
                           [(f"{m}{e}{i}", "dve") for e in range(1) for i in range(2) for m in "GU"]
                           + [(n, "dve") for e in range(1, L3_EXPERTS)
                              for n in [f"{m}{e}{i}" for i in range(2) for m in "GU"] + [f"Y{e - 1}"]]
                           + [(f"Y{L3_EXPERTS - 1}", "dve")])
        L3R = lambda: Jobs(v_banks, r_fill, {"act": r_act}, [(f"R{g}", "act") for g in range(4)])
        hid3 = pt_f[:, 0:2048].rearrange("p (a i s) -> p a i s", a=2, i=2)
        tanh3 = pt_f[:, 2048:3072].rearrange("p (a s) -> p a s", a=2)
        gate3 = pt_f[:, 3072:4096].rearrange("p (a s) -> p a s", a=2)
        whole3 = [pt_f[:, 4096:5120], pt_f[:, 5120:6144]]
        parts3 = [part_view(pt_f[:, 6144:7680]), part_view(prob_f)]
        near = w3a["near"]
        sums_sb = flat(xn[:, :, :])
        bank_a = bank_s[2]
        NU = HEADS // 4 * NTT

        def window(i, c):
            w0 = i * 128 + 32 * c - 32
            return max(0, w0), min(S, w0 + WIN), max(0, w0) - w0

        class OffsetAttention(Attention):

            def __init__(self, b):
                self.b = b
                super().__init__(4, L3R(), None, None, lambda g: w3b["w3_o"][:, g, :], unit=4, n_scores=2, by_rows=True,
                                 pt_held=True)
                self.steps = self.nt + 18

            def pe(self, pe):
                s = self.s
                for tau in range(self.steps):
                    if tau < self.nt:
                        u, m = divmod(tau, 4)
                        h, i = 4 * (u // NTT) + m, u % NTT
                        if tau >= 2:
                            pe.wait_ge(s["exped"], tau - 1)
                        if m == 0:
                            pe.wait_ge(s_near[u % 2], 64 * (u // 2 + 1))
                        bank = self.banks[tau % 2]
                        for slot in (2, 3, 1):
                            for c in range(4):
                                lo, hi, at = window(i, c)
                                a, z = {2: (0, lo), 3: (hi, S), 1: (lo, hi)}[slot]
                                if z > a:
                                    pe.matmul(bank[32 * c:32 * c + 32, a:z],
                                              stack(0)[:, h, i * 128 + 32 * c:i * 128 + 32 * c + 32],
                                              stack(slot)[:, h, a:z], start=True, stop=(slot != 1),
                                              skip_group_check=True)
                        for c in range(4):
                            lo, hi, at = window(i, c)
                            rows = slice(32 * c, 32 * c + 32)
                            last = pe.matmul(bank[rows, lo:hi], ident[:, rows], near[:, u % 2, m, at:at + hi - lo],
                                             start=False, stop=True, skip_group_check=True)
                        last.then_inc(s["scored"], 1)
                    k = tau - self.LAG
                    if 0 <= k < self.nt:
                        pe.wait_ge(s["exped"], k + 1)
                        if k >= 2:
                            self.wait_copied(pe, k - 2)
                        for j in range(NTT):
                            last = pe.transpose(bank_t[k % 2][:, j * 128:(j + 1) * 128],
                                                prob[:, k % 3, j * 128:(j + 1) * 128], ident[:, :])
                        last.then_inc(s["turned"], 1)
                    u = self.unit_at(tau, 2)
                    if u is not None:
                        self.wait_copied(pe, 4 * u + 3)
                        self.wait_copied(pe, 4 * u + 2)
                        g, i = divmod(u, NTT)
                        if g >= 2 and i == 0:
                            pe.wait_ge(s_normal, g - 1)
                        for j in range(NTT):
                            for m in range(4):
                                last = pe.matmul(v_banks[g % 2][GROW * m:GROW * (m + 1), i * 128:(i + 1) * 128],
                                                 v_pad[:, j, 4 * g + m, :], pt[:, u % 4, j, m * 128:(m + 1) * 128],
                                                 start=(i == 0 and j == 0), stop=False, skip_group_check=True)
                        last.then_inc(s["pv"], 1)
                    u, r = divmod(tau - 11, 4)
                    if r == 0 and 0 <= u < NU:
                        pe.wait_ge(s_askew[u % 2], self.b * SKEWED + 16 * (u // 2 + 1))
                        if u >= 1:
                            pe.wait_ge(s_amasked, u)
                        for m in range(4):
                            last = pe.transpose(bank_a[0:BAND, m * 128:(m + 1) * 128],
                                                w3a["banded"][:, u % 2, m, 0:BAND], ident[:, :])
                        last.then_inc(s_aturned, 1)
                    u, r = divmod(tau - 13, 4)
                    if r == 0 and 0 <= u < NU:
                        pe.wait_ge(s_amasked, u + 1)
                        g, i = divmod(u, NTT)
                        for m in range(4):
                            last = pe.matmul(v_banks[g % 2][GROW * m:GROW * (m + 1), i * 128:(i + 1) * 128],
                                             w3b["w3_rvb"], w3a["bandedT"][:, u % 4, m * 128:(m + 1) * 128],
                                             start=False, stop=True, skip_group_check=True)
                        last.then_inc(s_band, 1)
                    g = self.at(tau, 9)
                    if g is not None:
                        pe.wait_ge(s["inverted"], g + 1)
                        pe.wait_ge(s["craw"], g + 1)
                        self.spread_sums(pe, g, self.R.bank(f"R{g}")).then_inc(self.R.filled, 1)
                    g = self.at(tau, 12)
                    if g is not None:
                        self.R.wait_emptied(pe, f"R{g}")
                        pe.matmul(v_banks[g % 2][:, :], w3b["w3_sel"], ctx_raw[:, :], start=True, stop=False)
                        for n in range(2):
                            pe.wait_ge(s_bmasked, 2 * g + n + 1)
                            last = pe.matmul(v_banks[g % 2][:, :], w3b[f"w3_rv{n}"], w3b[f"masked{n}"],
                                             start=False, stop=(n == 1))
                        last.then_inc(s_numer, 1)
                    g = self.at(tau, 14)
                    if g is not None:
                        pe.wait_ge(s_normal, g + 1)
                        for t in range(NTT):
                            last = pe.matmul(bank_o[:, t * 128:(t + 1) * 128], ctx_n[:, g % 2, t * 128:(t + 1) * 128],
                                             self.wo(g), start=(g % self.per_out == 0 and t == 0),
                                             stop=(g % self.per_out == self.per_out - 1),
                                             skip_group_check=True)
                        last.then_inc(s["projected"], 1)

            def act(self, act):
                s = self.s
                for tau in range(self.steps):
                    k = tau - self.LAG
                    if 0 <= k < self.nt and k % 2 == 1:
                        self.copy_tile(act, k)
                    if tau < self.nt:
                        act.wait_ge(s["maxed"], tau + 1)
                        if tau >= 3:
                            act.wait_ge(s["turned"], tau - 2)
                            act.wait_ge(s_written[tau % 3], 16 * (tau // 3))
                        act.activation(prob[:, tau % 3, :], self.banks[tau % 2][:, :], ACT.Exp,
                                       bias=negmax[:, tau % 64:tau % 64 + 1], accum_out=rowsum[:, tau % 64:tau % 64 + 1]
                                       ).then_inc(s["exped"], 1)
                    g = self.at(tau, 8)
                    if g is not None:
                        act.wait_ge(s_band, 4 * (g + 1))
                        if g >= 1:
                            act.wait_ge(s_numer, g)
                        act.activation(ctx_raw[:, :], v_banks[g % 2][:, :], ACT.Copy).then_inc(s["craw"], 1)
                    g = self.at(tau, 10)
                    if g is not None:
                        if g >= 1:
                            act.wait_ge(s_normal, g)
                        self.R.wait_filled(act, f"R{g}")
                        act.activation(sums_sb, self.R.bank(f"R{g}")[:, :], ACT.Copy).then_inc(r_act, 1)

            def dve(self, dve, norm):
                s = self.s
                for tau in range(self.steps):
                    if tau == self.nt + 1:
                        norm.stats()
                    if tau < self.nt:
                        dve.wait_ge(s["scored"], tau + 1)
                        dve.tensor_reduce(negmax[:, tau % 64:tau % 64 + 1], self.banks[tau % 2][:, :], AX.X, ALU.max,
                                          negate=True).then_inc(s["maxed"], 1)
                    k = tau - self.LAG
                    if 0 <= k < self.nt and k % 2 == 0:
                        self.copy_tile(dve, k)
                    g = self.at(tau, 1)
                    if g is not None:
                        at = g * self.per % 64
                        cols = rowsum[:, at:at + self.per]
                        dve.wait_ge(s["exped"], (g + 1) * self.per)
                        dve.reciprocal(cols, cols).then_inc(s["inverted"], 1)
                    u, r = divmod(tau - 12, 4)
                    if r == 0 and 0 <= u < NU:
                        dve.wait_ge(s_aturned, u + 1)
                        if u >= 4:
                            dve.wait_ge(s_band, u - 3)
                        dve.tensor_tensor(w3a["bandedT"][:, u % 4, :].rearrange("p (i n) -> p i n", i=NTT),
                                          bank_a[0:BAND, :].rearrange("p (i n) -> p i n", i=NTT),
                                          w3b["w3_ma"].unsqueeze(1).to_broadcast([BAND, NTT, 128]), ALU.mult
                                          ).then_inc(s_amasked, 1)
                    g = self.at(tau, 13)
                    if g is not None:
                        dve.wait_ge(s_numer, g + 1)
                        self.R.wait_emptied(dve, f"R{g}")
                        if g >= 2:
                            dve.wait_ge(s["projected"], g - 1)
                        dve.tensor_tensor(ctx_n[:, g % 2, :], v_banks[g % 2][:, :], sums_sb, ALU.mult).then_inc(s_normal, 1)

            def pool(self, pool):
                s = self.s
                for tau in range(self.steps):
                    if tau == self.nt + 1:
                        inverse_deviation(pool, s_var, s_pool, s_rstd)
                    u, r = divmod(tau - 4, 4)
                    if r == 0 and 0 <= u < NU:
                        for k in range(4 * u, 4 * u + 4):
                            pool.wait_ge(s_written[k % 3], 16 * (k // 3 + 1))
                        if u >= 2:
                            pool.wait_ge(s_aturned, u - 1)
                        src = bass.AP(skewed, (u % NTT) * 4 * A_SLOT + 1,
                                      [[A_ROW + 1, 128], [A_SLOT, 4], [1, BAND]])
                        pool.dma_start(w3a["banded"][:, u % 2, :, 0:BAND], src).then_inc(s_askew[u % 2], 16)
                    g = self.at(tau, 9)
                    if g is not None:
                        pool.wait_ge(s["craw"], g + 1)
                        if g >= 1:
                            pool.wait_ge(s_numer, g)
                        for n in range(2):
                            pool.tensor_tensor(w3b[f"masked{n}"], ctx_raw[:, :], w3b[f"w3_m{n}"], ALU.mult
                                               ).then_inc(s_bmasked, 1)

            def sync(self, sp):
                s = self.s

                def load_near(u):
                    g, i = divmod(u, NTT)
                    for c in range(4):
                        src = bass.AP(offset_scores, (i * 128 + 32 * c) * E_ROW + 4 * g * BAND + 31,
                                      [[E_ROW - 1, 32], [BAND, 4], [1, WIN]])
                        sp.dma_start(near[32 * c:32 * c + 32, u % 2], src).then_inc(s_near[u % 2], 16)

                load_near(0)
                load_near(1)
                for k in range(self.nt):
                    u, m = divmod(k, 4)
                    i = u % NTT
                    if u >= NTT and m == 0:
                        sp.wait_ge(s_aturned, u - NTT + 1)
                    sp.wait_ge(s["exped"], k + 1)
                    lo, hi = max(0, i * 128 - 32), min(S, i * 128 + 160)
                    dst = bass.AP(skewed, (i * 4 + m) * A_SLOT + 32 + lo - (i * 128 - 32), [[A_ROW, 128], [1, hi - lo]])
                    sp.dma_start(dst, prob[:, k % 3, lo:hi]).then_inc(s_written[k % 3], 16)
                    if m == 3 and u + 2 < NU:
                        sp.wait_ge(s["scored"], k + 1)
                        load_near(u + 2)

        def layer3_tensor(pe):
            wait_weights(pe, "w3", N_W3)
            pe.wait_ge(kept["v3_set"], 17)
            pe.wait_ge(kept["rk_ready"], 3 * NPARTS)
            with iterations(pe, 3) as b:
                A, F = L3A(), L3F()
                turn_xn(pe, A)
                A.wait_emptied(pe, "X")
                token_products(pe, A, "LG", w3b["w3_rt"], 8)
                project(pe, A, "Q", w3b["w3_lin"][:, 0, :], xnT[:, :])
                project(pe, A, "K", w3b["w3_lin"][:, 1, :], xnT[:, :])
                token_products(pe, A, "V", w3b["w3_lin"][:, 2, :], D)

                def offsets(j):
                    q, t = divmod(j, NTT)
                    if j == 0:
                        pe.wait_ge(s_first_heads, 2 * N_FETCH)
                    elif j == NTT:
                        pe.wait_ge(s_stacked[0], 2 * N_FETCH)
                    A.wait_free(pe, f"E{j}")
                    for m in range(4):
                        last = pe.matmul(A.bank(f"E{j}")[:, m * BAND:(m + 1) * BAND],
                                         stack(0)[0:STACK, 4 * q + m, t * 128:(t + 1) * 128], rk_stack,
                                         start=True, stop=True)
                    last.then_inc(A.filled, 1)

                def down(e):
                    F.wait_free(pe, f"Y{e}")
                    F.wait_emptied(pe, f"U{e}1")
                    for t in range(NTT):
                        for i in range(2):
                            last = pe.matmul(F.bank(f"Y{e}")[:, t * 128:(t + 1) * 128],
                                             hid3[:, e % 2, i, t * 128:(t + 1) * 128], w3b["w3_down"][:, e, i * D:(i + 1) * D],
                                             start=(i == 0), stop=(i == 1))
                    last.then_inc(F.filled, 1)

                for e in range(L3_EXPERTS):
                    for i in range(2):
                        project(pe, F, f"G{e}{i}", w3b["w3_gate"][:, e, i * 128:(i + 1) * 128], xnT[:, :])
                        project(pe, F, f"U{e}{i}", w3b["w3_up"][:, e, i * 128:(i + 1) * 128], xnT[:, :])
                        for j in offset_jobs(2 * e + i):
                            offsets(j)
                    if e:
                        down(e - 1)
                down(L3_EXPERTS - 1)
                F.wait_all_free(pe)
                A.wait_all_free(pe)
                for i in range(2):
                    pe.wait_ge(s_stacked[i], 2 * N_FETCH)
                OffsetAttention(b).pe(pe)
                meet(pe, kept["go3"], b)

        def layer3_scalar(act):
            wait_weights(act, "w3", N_W3)
            act.wait_ge(kept["v3_set"], 17)
            with iterations(act, 3) as b:
                A, F = L3A(), L3F()
                evac(act, A, "X", xnT[:, :])
                evac(act, A, "Q", whole3[0][:, 0:S], scale=DH ** -0.5)
                A.wait_filled(act, "V")
                act.activation(v_pad[:, :, :, 0:DH], A.bank("V")[:, :].rearrange("p (t h d) -> p t h d", t=NTT, h=HEADS),
                               ACT.Copy).then_inc(a_act, 1)
                A.wait_emptied(act, "Q")
                A.wait_emptied(act, "K")
                Split(0, whole3[0], parts3[0]).act(act)
                for n in range(2 * L3_EXPERTS):
                    name = f"G{n // 2}{n % 2}"
                    F.wait_filled(act, name)
                    if n >= 2:
                        F.wait_emptied(act, f"G{(n - 2) // 2}{n % 2}")
                    act.activation(tanh3[:, n % 2], F.bank(name)[:, :], ACT.Tanh, scale=0.5).then_inc(s_tanh, 1)
                    if n in (1, 3):
                        Split(1, whole3[1], parts3[1]).act_step(act, n // 2)
                    for j in offset_jobs(n):
                        if j >= 2:
                            act.wait_ge(s_esent[j % 2], b * SENT + 16 * (j // 2))
                        evac(act, A, f"E{j}", ctx_n[:, j % 2, 0:4 * BAND], A.bank(f"E{j}")[:, 0:4 * BAND])
                silu_tanh(act, L3_EXPERTS - 1)
                act.wait_ge(s_sent, 32)
                OffsetAttention(b).act(act)
                meet(act, kept["go3"], b)

        def layer3_vector(dve):
            wait_weights(dve, "w3", N_W3)
            once = Steps(dve, kept["rk_ready"])
            rest, part = w3a["w3_rk"], w3a["w3_part"]
            for p in range(NPARTS):
                once.add(dve.tensor_copy(rk_rounded, rest))
                once.settle()
                if p == 0:
                    once.add(dve.tensor_scalar(rk_stack, rk_rounded, part[:, p:p + 1], None, ALU.mult))
                else:
                    once.add(dve.scalar_tensor_tensor(rk_stack, rk_rounded, part[:, p:p + 1], rk_stack,
                                                      ALU.mult, ALU.add))
                once.add(dve.tensor_tensor(rest, rest, rk_rounded, ALU.subtract))
                once.settle()
            with iterations(dve, 3) as b:
                A, F, M = L3A(), L3F(), OffsetAttention(b)
                d = Steps(dve, s_dve)
                norm = NextNorm(dve, b, d)
                evac(dve, A, "LG", lg[:, :, 0:8], A.bank("LG")[:, 0:NTT * 8].rearrange("p (t e) -> p t e", t=NTT))
                A.wait_emptied(dve, "LG")
                d.add(dve.memset(gate[:, :, 8:9], 1.0))
                top_k(dve, d, lg[:, :, 0:8], NTT, 8, 1, gate[:, :, 0:8], prob_f[:, 0:256], prob_f[:, 256:512])
                A.wait_filled(dve, "K")
                dve.tensor_copy(whole3[0][:, S:2 * S], A.bank("K")[:, :])
                dve.tensor_scalar(whole3[1][:, 0:S], A.bank("K")[:, :], w3b["w3_relk"][:, 0:1], None, ALU.add)
                dve.tensor_scalar(whole3[1][:, S:2 * S], A.bank("K")[:, :], w3b["w3_relk"][:, 1:2], None, ALU.add
                                  ).then_inc(a_dve, 1)
                A.wait_emptied(dve, "K")
                A.wait_emptied(dve, "Q")
                Split(0, whole3[0], parts3[0]).dve(dve)
                for e in range(L3_EXPERTS):
                    for i in range(2):
                        n = 2 * e + i
                        dve.wait_ge(s_tanh, n + 1)
                        if n >= 2:
                            F.wait_emptied(dve, f"U{(n - 2) // 2}{n % 2}")
                        dve.scalar_tensor_tensor(gate3[:, n % 2], tanh3[:, n % 2], 1.0, F.bank(f"G{e}{i}")[:, :],
                                                 ALU.add, ALU.mult).then_inc(f_dve, 1)
                        F.wait_filled(dve, f"U{e}{i}")
                        F.wait_emptied(dve, f"G{e}{i}")
                        if e >= 2:
                            F.wait_filled(dve, f"Y{e - 2}")
                        dve.scalar_tensor_tensor(hid3[:, e % 2, i], gate3[:, n % 2], 0.5, F.bank(f"U{e}{i}")[:, :],
                                                 ALU.mult, ALU.mult).then_inc(f_dve, 1)
                    if e < 2:
                        Split(1, whole3[1], parts3[1]).dve_step(dve, e)
                    if e:
                        gated(dve, F, e - 1, first=1)
                gated(dve, F, L3_EXPERTS - 1, first=1)
                silu(dve)
                M.dve(dve, norm)
                dve.wait_ge(s_normal, 4)
                norm.apply()
                dve.wait_ge(M.s["projected"], 4)
                residual(dve, d, b, bank3(bank_o))
                meet(dve, kept["go3"], b)

        def layer3_gpsimd(pool):
            flat_v = v_pad[:, :, :, :].rearrange("p a b c -> p (a b c)")
            pool.memset(flat_v, 0.0).then_inc(kept["v3_set"], 1)
            pool.wait_ge(kept["v3_set"], 1)
            zeros = 2 * NTT * A_SLOT // 128
            for half in range(2):
                pool.dma_start(bass.AP(skewed, half * 128 * zeros, [[zeros, 128], [1, zeros]]), flat_v[:, 0:zeros]
                               ).then_inc(kept["zeroed"], 16)
            pool.wait_ge(kept["zeroed"], 32)
            for j in range(NTT):
                for a in range(4):
                    u = DH + 4 * j + a
                    pool.memset(v_pad[32 * a:32 * a + 32, j, :, u:u + 1], 1.0).then_inc(kept["v3_set"], 1)
            pool.wait_ge(kept["v3_set"], 17)
            with iterations(pool, 3) as b:
                A, F = L3A(), L3F()
                for n in range(2 * L3_EXPERTS):
                    for j in offset_jobs(n):
                        q, t = divmod(j, NTT)
                        A.wait_emptied(pool, f"E{j}")
                        dst = bass.AP(offset_scores, t * 128 * E_ROW + q * 4 * BAND, [[E_ROW, 128], [1, 4 * BAND]])
                        pool.dma_start(dst, ctx_n[:, j % 2, 0:4 * BAND]).then_inc(s_esent[j % 2], 16)
                    if n == 16:
                        for i in range(2):
                            pool.wait_ge(s_esent[i], b * SENT + SENT)
                        pool.sem_inc(s_offsets, 1)
                    if n % 2 and n > 3:
                        add_up(pool, F, [(n - 3) // 2], "Y0")
                add_up(pool, F, [L3_EXPERTS - 1], "Y0")
                OffsetAttention(b).pool(pool)
                meet_and_clear(pool, kept["go3"], b)

        def layer3_sync(sp):
            load_weights(sp, spec3a, w3a, kept["w3"])
            sp.wait_ge(kept["zeroed"], 32)
            with iterations(sp, 3) as b:
                for i in range(2):
                    send_parts(sp, 2 + i, parts3[i].rearrange("p a (q s) -> p (a q) s", q=2), s_rest, 2 * i + 2, s_sent)
                    sp.wait_ge(s_sent, 16 * (i + 1))
                    if i == 0:
                        fetch_stack(sp, 2, 0, 0, True, s_first_heads, 0, 4)
                        fetch_stack(sp, 2, 1, 1, False, s_first_heads, 0, 4)
                    h0 = 4 if i == 0 else 0
                    fetch_stack(sp, 2 + i, 0, 2 * i, i == 0, s_stacked[i], h0)
                    fetch_stack(sp, 2 + i, 1, 2 * i + 1, False, s_stacked[i], h0)
                sp.wait_ge(s_offsets, 1)
                OffsetAttention(b).sync(sp)
                meet_sync(sp, kept["go3"], b)

        def output_sync(sp):
            sp.dma_start(out.rearrange("b (t p) d -> p (b t) d", p=128),
                         x_all[:, :, :, :].rearrange("p b t d -> p (b t) d")).then_inc(kept["stored"], 16)
            sp.wait_ge(kept["stored"], 16)

        @block.sync
        def _(sp):
            loads_sync(sp)
            layer2_sync(sp)
            layer3_sync(sp)
            output_sync(sp)

        @block.tensor
        def _(pe):
            layer0_tensor(pe)
            layer1_tensor(pe)
            layer2_tensor(pe)
            layer3_tensor(pe)

        @block.vector
        def _(dve):
            layer0_vector(dve)
            layer1_vector(dve)
            layer2_vector(dve)
            layer3_vector(dve)

        @block.scalar
        def _(act):
            layer0_scalar(act)
            layer1_scalar(act)
            layer2_scalar(act)
            layer3_scalar(act)

        @block.gpsimd
        def _(pool):
            layer0_gpsimd(pool)
            layer1_gpsimd(pool)
            layer2_gpsimd(pool)
            layer3_gpsimd(pool)


def laid_out(i):
    a = {k: np.asarray(v) for k, v in i.items()}
    f = np.float32
    c = np.ascontiguousarray
    T = {"x": a["L0_attn_x"]}
    T["ident"] = np.eye(128, dtype=f)
    T["ones_row"] = np.ones((1, 128), f)
    T["causal"] = np.triu(np.full((128, 128), NEG, f), 1)
    T["tri"] = c(np.broadcast_to(np.tril(np.ones((15, 15), f), -1), (128, 15, 15)))
    T["w0_lin"] = c(np.stack([a["L0_attn_" + n].T for n in ("Wq", "Wk", "Wv", "Wa", "Wb")], 1))
    T["w0_g"] = a["L0_ffn_Wg"]
    T["w0_e"] = c(a["L0_ffn_We"].transpose(1, 0, 2))
    T["w0_be"] = a["L0_ffn_be"]
    T["w1_qkv"] = c(np.stack([a["L1_attn_" + n] for n in ("Wq", "Wk", "Wv")], 1))
    T["w1_o"] = c(a["L1_attn_Wo"].reshape(8, 128, 128).transpose(1, 0, 2))
    T["w1_bo"] = a["L1_attn_bo"][None]
    T["w1_r"] = a["L1_ffn_router_W"]
    T["w1_rb"] = a["L1_ffn_router_b"][None]
    T["w1_e1"] = c(np.concatenate([a["L1_ffn_eW1"], a["L1_ffn_sW1"][None]]).transpose(1, 0, 2))
    T["w1_eb1"] = c(np.concatenate([a["L1_ffn_eb1"], a["L1_ffn_sb1"][None]]).T)
    T["w1_e2"] = c(np.concatenate([a["L1_ffn_eW2"], a["L1_ffn_sW2"][None]]).transpose(1, 0, 2))
    T["w1_eb2"] = c(np.concatenate([a["L1_ffn_eb2"], a["L1_ffn_sb2"][None]]))

    def padded_out(wo, bo):
        p = np.zeros((4, GROW, 4, 128), f)
        p[:, 0:DH] = wo.reshape(4, 4, DH, 128).transpose(1, 2, 0, 3)
        p[0, DH, 0] = bo
        return p.reshape(128, 4, 128)

    T["w2_qk"] = c(np.concatenate([a["L2_attn_Wq"].T, a["L2_attn_Wk"].T], 1))
    T["w2_v"] = c(a["L2_attn_Wv"].T)
    T["w2_ln"] = c(np.stack([np.repeat(a["L2_attn_" + n], HEADS) for n in ("qln_g", "kln_g", "qln_b", "kln_b")], 1))
    T["w2_o"] = padded_out(a["L2_attn_Wo"].T, a["L2_attn_bo"])
    across = np.arange(128).reshape(HEADS, DH).T.ravel()
    T["w2_fe"] = c(np.concatenate([a["L2_ffn_Wq"][..., across], a["L2_ffn_Wk"][..., across], a["L2_ffn_Wv"]], 2
                                  ).transpose(1, 0, 2))
    T["w2_fb"] = c(np.stack([a["L2_ffn_b" + n][:, across].T for n in "qk"], 1))
    T["w2_fbv"] = a["L2_ffn_bv"]
    T["w2_g1"] = a["L2_ffn_Wg1"]
    T["w2_b1"] = a["L2_ffn_bg1"][:, None]
    T["w2_g2"] = a["L2_ffn_Wg2"]
    T["w2_b2"] = c(np.broadcast_to(a["L2_ffn_bg2"], (128, 4)))
    T["w2_fo"] = padded_out(a["L2_ffn_Wo"], a["L2_ffn_bo"])

    T["w3_lin"] = c(np.stack([a["L3_attn_Wq"].T[:, across], a["L3_attn_Wk"].T[:, across], a["L3_attn_Wv"].T], 1))
    T["w3_o"] = padded_out(a["L3_attn_Wo"].T, a["L3_attn_b_o"])
    T["w3_rt"] = c(a["L3_ffn_router"].T)
    for n in ("up", "gate"):
        both = np.concatenate([a["L3_ffn_" + n], a[f"L3_ffn_w_{n}_s"][None]])
        T["w3_" + n] = c(both.transpose(2, 0, 1))
    down = np.concatenate([a["L3_ffn_down"], a["L3_ffn_w_down_s"][None]])
    T["w3_down"] = c(down.reshape(9, 128, 2, 128).transpose(3, 0, 2, 1).reshape(128, 9, 256))
    rk, rv = a["L3_attn_rel_k_emb"], a["L3_attn_rel_v_emb"]
    T["w3_relk"] = c(np.stack([np.repeat(rk[0], HEADS), np.repeat(rk[2 * MAX_REL], HEADS)], 1))
    clipped = np.clip(np.arange(BAND) - BAND // 2, -MAX_REL, MAX_REL) + MAX_REL
    T["w3_rk"] = c(np.tile(rk[clipped].T, (NPARTS * NPARTS, 1)))
    T["w3_part"] = c(np.tile(np.repeat(np.eye(NPARTS, dtype=f), DH, 0), (NPARTS, 1)))
    band = np.zeros((BAND, GROW), f)
    band[:, 0:DH] = rv[clipped]
    T["w3_rvb"] = band
    blocks = S // 32
    for n, row in ((0, 0), (1, 2 * MAX_REL)):
        m = np.zeros((4, GROW, 4, GROW), f)
        for g in range(4):
            m[g, DH:DH + blocks, g, 0:DH] = rv[row]
        T[f"w3_rv{n}"] = m.reshape(128, 128)
    u, blk = np.arange(blocks)[:, None], np.arange(S)[None] // 32
    for n, far in ((0, u < blk - 1), (1, u > blk + 1)):
        m = np.zeros((4, GROW, S), f)
        m[:, DH:DH + blocks] = far
        T[f"w3_m{n}"] = m.reshape(128, S)
    r, p = np.arange(BAND)[:, None] - BAND // 2, np.arange(128)[None] % 32
    T["w3_ma"] = ((r + p >= -32) & (r + p < 64)).astype(f)
    sel = np.zeros((4, GROW, 4, GROW), f)
    for g in range(4):
        sel[g, range(DH), g, range(DH)] = 1
        sel[g, DH:DH + blocks, g, DH] = 1
    T["w3_sel"] = sel.reshape(128, 128)
    return T


def kernel(**inputs):
    import concourse.bacc as bacc
    from concourse.bass_utils import run_bass_kernel_spmd

    arrays = laid_out(inputs)
    nc = bacc.Bacc("TRN2", target_bir_lowering=False, num_devices=1)
    T = {n: nc.dram_tensor(f"in_{n}", v.shape, mybir.dt.from_np(v.dtype), kind="ExternalInput").ap()
         for n, v in arrays.items()}
    out = nc.dram_tensor("out_x", (B, S, D), mybir.dt.float32, kind="ExternalOutput").ap()
    build(nc, T, out)
    r = run_bass_kernel_spmd(nc, [{f"in_{n}": v for n, v in arrays.items()}], core_ids=[0])
    return r.results[0]["out_x"]
```
